# Optimizing a Trainium2 kernel written in Bass

```python
import numpy as np
import jax
import jax.numpy as jnp

def _softmax(x, axis=-1):
    return jax.nn.softmax(x, axis=axis)

def _gelu(x):
    return jax.nn.gelu(x, approximate=True)

def _silu(x):
    return jax.nn.silu(x)

def _sigmoid(x):
    return jax.nn.sigmoid(x)

def _layernorm(x, axis=-1, eps=1e-05):
    m = jnp.mean(x, axis=axis, keepdims=True)
    v = jnp.var(x, axis=axis, keepdims=True)
    return (x - m) / jnp.sqrt(v + eps)

def _scatter_add(tgt, idx, src, axis=0):
    return tgt.at[idx].add(src)

def _segment_sum(src, seg, n):
    return jax.ops.segment_sum(src, seg, n)
kernel_name = 'mk_xattn_ffn_d2_seqx_r8_dcbd4e'

def setup_inputs(seed: int=0):
    np.random.seed(seed)
    _w = jnp.asarray

    def _rec_inputs():
        import jax
        import jax.numpy as jnp
        _rk = jax.random.key(seed)
        x = -0.0002928 + 1 * jax.random.normal(jax.random.fold_in(_rk, 1), (16, 128, 128), jnp.float32)
        _lenS = 128 - jax.random.randint(jax.random.fold_in(_rk, 7), (16,), 0, max(1, 128 // 4) + 1, jnp.int32)
        _lenS2 = 128 - jax.random.randint(jax.random.fold_in(_rk, 8), (16,), 0, max(1, 128 // 4) + 1, jnp.int32)
        _ctx_1024P = jax.random.normal(jax.random.fold_in(_rk, 11), (16, 16, 128), jnp.float32)
        _ctx_1024c = jax.random.dirichlet(jax.random.fold_in(_rk, 511), 0.3 * jnp.ones((16,), jnp.float32), (16, 128))
        _ctx_1024t = jnp.einsum('bsk,bkd->bsd', _ctx_1024c, _ctx_1024P)
        _ctx_1024t = _ctx_1024t * jax.lax.rsqrt(jnp.mean(jnp.square(_ctx_1024t)) + 1e-12) * 0.953939
        ctx_1024 = -1.39393e-06 + 0.999914 * (_ctx_1024t + 0.3 * jax.random.normal(jax.random.fold_in(_rk, 611), (16, 128, 128), jnp.float32))
        return (x, ctx_1024)
    x, ctx_1024 = _rec_inputs()

    def _L0_xattn_setup():
        import jax, jax.numpy as jnp
        import numpy as np
        D_MODEL = 128
        N_HEAD = 16
        D_HEAD = D_MODEL // N_HEAD
        key = jax.random.key(seed)
        ks = jax.random.split(key, 11)
        B, S = (2, 256)
        scale = 1.0 / np.sqrt(D_MODEL)
        inp = {'q': jax.random.normal(ks[0], (B, S, D_MODEL), jnp.float32), 'k': jax.random.normal(ks[1], (B, S, D_MODEL), jnp.float32), 'v': jax.random.normal(ks[2], (B, S, D_MODEL), jnp.float32), 'w_q': jax.random.normal(ks[3], (D_MODEL, D_MODEL), jnp.float32) * scale, 'b_q': jnp.zeros((D_MODEL,), jnp.float32), 'w_k': jax.random.normal(ks[4], (D_MODEL, D_MODEL), jnp.float32) * scale, 'b_k': jnp.zeros((D_MODEL,), jnp.float32), 'w_v': jax.random.normal(ks[5], (D_MODEL, D_MODEL), jnp.float32) * scale, 'b_v': jnp.zeros((D_MODEL,), jnp.float32), 'w_out': jax.random.normal(ks[6], (D_MODEL, D_MODEL), jnp.float32) * scale, 'b_out': jnp.zeros((D_MODEL,), jnp.float32)}
        return inp
    _L0_xattn_all = _L0_xattn_setup()
    _L0_xattn_in = {k: v for k, v in _L0_xattn_all.items() if k in ('w_q', 'b_q', 'w_k', 'b_k', 'w_v', 'b_v', 'w_out', 'b_out')}
    del _L0_xattn_all

    def _L0_ffn_setup():
        import jax, jax.numpy as jnp
        import numpy as np
        HIDDEN = 128
        NUM_EXPERTS = 16
        TOP_K = 6
        EPS = 1e-10
        key = jax.random.key(seed)
        k1, k2, k3, k4 = jax.random.split(key, 4)
        tokens = jax.random.normal(k1, (4, 256, HIDDEN), dtype=jnp.float32)
        bound = 1.0 / np.sqrt(HIDDEN)
        router_w = jax.random.uniform(k2, (NUM_EXPERTS, HIDDEN), jnp.float32, -bound, bound)
        router_b = jax.random.uniform(k3, (NUM_EXPERTS,), jnp.float32, -bound, bound)
        expert_w = jax.random.normal(k4, (NUM_EXPERTS, HIDDEN, HIDDEN), dtype=jnp.float32) / np.sqrt(HIDDEN)
        return {'tokens': tokens, 'router_w': router_w, 'router_b': router_b, 'expert_w': expert_w}
    _L0_ffn_all = _L0_ffn_setup()
    _L0_ffn_in = {k: v for k, v in _L0_ffn_all.items() if k in ('router_w', 'router_b', 'expert_w')}
    del _L0_ffn_all

    def _L1_xattn_setup():
        import jax, jax.numpy as jnp
        import numpy as np
        DIM = 128
        HEAD_DIM = 64
        NUM_HEADS = 8
        INNER = HEAD_DIM * NUM_HEADS
        ROT_DIM = HEAD_DIM
        ROPE_BASE = 10000.0
        EPS = 1e-05

        def layer_norm(x, g, b):
            mu = jnp.mean(x, axis=-1, keepdims=True)
            var = jnp.var(x, axis=-1, keepdims=True)
            return (x - mu) * jax.lax.rsqrt(var + EPS) * g + b

        def rope_rotate_k(k):
            n = k.shape[1]
            half = ROT_DIM // 2
            inv_freq = 1.0 / ROPE_BASE ** (jnp.arange(0, ROT_DIM, 2, dtype=jnp.float32) / ROT_DIM)
            theta = jnp.arange(n, dtype=jnp.float32)[:, None] * inv_freq[None, :]
            angles = jnp.concatenate([theta, theta], axis=-1)
            cos = jnp.cos(angles)[None, :, None, :].astype(k.dtype)
            sin = jnp.sin(angles)[None, :, None, :].astype(k.dtype)
            k_rope, k_pass = (k[..., :ROT_DIM], k[..., ROT_DIM:])
            neg_half = jnp.concatenate([-k_rope[..., half:], k_rope[..., :half]], axis=-1)
            k_rope = k_rope * cos + neg_half * sin
            return jnp.concatenate([k_rope, k_pass], axis=-1)
        key = jax.random.key(seed)
        ks = jax.random.split(key, 5)
        b, n, m = (8, 1024, 64)
        s = 1.0 / np.sqrt(DIM)
        return {'x': jax.random.normal(ks[0], (b, n, DIM), jnp.float32), 'latents': jax.random.normal(ks[1], (b, m, DIM), jnp.float32), 'gamma_x': jnp.ones((DIM,), jnp.float32), 'beta_x': jnp.zeros((DIM,), jnp.float32), 'gamma_l': jnp.ones((DIM,), jnp.float32), 'beta_l': jnp.zeros((DIM,), jnp.float32), 'Wq': jax.random.normal(ks[2], (DIM, INNER), jnp.float32) * s, 'Wkv': jax.random.normal(ks[3], (DIM, 2 * INNER), jnp.float32) * s, 'Wo': jax.random.normal(ks[4], (INNER, DIM), jnp.float32) * (1.0 / np.sqrt(INNER))}
    _L1_xattn_all = _L1_xattn_setup()
    _L1_xattn_in = {k: v for k, v in _L1_xattn_all.items() if k in ('gamma_x', 'beta_x', 'gamma_l', 'beta_l', 'Wq', 'Wkv', 'Wo')}
    del _L1_xattn_all

    def _L1_ffn_setup():
        import jax, jax.numpy as jnp
        import numpy as np
        DIM = 128
        DEPTH = 6
        HEADS = 16
        DIM_HEAD = 64
        WINDOW = 32
        INNER = HEADS * DIM_HEAD
        DIM_INNER = int(DIM * 4 * 2 / 3)
        QK_SCALE = 8.0

        def shift_tokens(t):
            a, s = jnp.split(t, 2, -1)
            s = jnp.pad(s, ((0, 0), (1, 0), (0, 0)))[:, :-1]
            return jnp.concatenate([a, s], -1)

        def l2norm(t):
            return t / jnp.maximum(jnp.linalg.norm(t, axis=-1, keepdims=True), 1e-12)

        def rotate_half(x):
            x1, x2 = jnp.split(x, 2, -1)
            return jnp.concatenate([-x2, x1], -1)

        def rotary_tables(n):
            half = jnp.arange(0, DIM_HEAD, 2, dtype=jnp.float32)
            inv_freq = 1.0 / 10000.0 ** (half / DIM_HEAD)
            t = jnp.arange(n, dtype=jnp.float32)
            freqs = t[:, None] * inv_freq[None, :]
            freqs = jnp.concatenate([freqs, freqs], -1)
            base_scale = (half + 0.4 * DIM_HEAD) / (1.4 * DIM_HEAD)
            power = (t - n // 2) / (WINDOW // 2)
            scale = base_scale[None, :] ** power[:, None]
            scale = jnp.concatenate([scale, scale], -1)
            return (freqs, scale)

        def local_attention(q, k, v):
            b, h, n, d = q.shape
            w = WINDOW
            nw = n // w
            bq = q.reshape(b, h, nw, w, d)
            bk = k.reshape(b, h, nw, w, d)
            bv = v.reshape(b, h, nw, w, d)

            def look(t):
                p = jnp.pad(t, ((0, 0), (0, 0), (1, 0), (0, 0), (0, 0)))
                return jnp.concatenate([p[:, :, :nw], p[:, :, 1:]], axis=3)
            bk2, bv2 = (look(bk), look(bv))
            seq = jnp.arange(n).reshape(nw, w)
            seq_p = jnp.pad(seq, ((1, 0), (0, 0)), constant_values=-1)
            jt = jnp.concatenate([seq_p[:nw], seq_p[1:]], axis=1)
            it = seq[:, :, None]
            jb = jt[:, None, :]
            mask = (it < jb) | (it > jb + w) | (jb == -1)
            sim = jnp.einsum('bhwie,bhwje->bhwij', bq, bk2) * QK_SCALE
            sim = jnp.where(mask, -jnp.finfo(sim.dtype).max, sim)
            attn = jax.nn.softmax(sim, -1)
            out = jnp.einsum('bhwij,bhwje->bhwie', attn, bv2)
            return out.reshape(b, h, n, d)

        def attn_layer(x, Wqkv, qs, ksc, Wo):
            b, n, _ = x.shape
            qkv = x @ Wqkv
            q, k, v = jnp.split(qkv, 3, -1)
            sh = lambda t: t.reshape(b, n, HEADS, DIM_HEAD).transpose(0, 2, 1, 3)
            q, k, v = (sh(q), sh(k), sh(v))
            q = l2norm(q) * qs
            k = l2norm(k) * ksc
            freqs, scale = rotary_tables(n)
            cos, sin = (jnp.cos(freqs), jnp.sin(freqs))
            q = q * cos * scale + rotate_half(q) * sin * scale
            inv = 1.0 / scale
            k = k * cos * inv + rotate_half(k) * sin * inv
            out = local_attention(q, k, v)
            out = out.transpose(0, 2, 1, 3).reshape(b, n, INNER)
            return out @ Wo

        def ffn_layer(x, g, bln, W1, b1, W2, b2):
            mu = x.mean(-1, keepdims=True)
            var = ((x - mu) ** 2).mean(-1, keepdims=True)
            xn = (x - mu) / jnp.sqrt(var + 1e-05) * g + bln
            hg = xn @ W1 + b1
            a, gate = jnp.split(hg, 2, -1)
            return a * jax.nn.gelu(gate, approximate=False) @ W2 + b2
        key = jax.random.key(seed)
        ks = jax.random.split(key, 8)
        B, N = (2, 256)
        init = lambda k, shape: jax.random.normal(k, shape, jnp.float32) * 0.02
        return {'x': jax.random.normal(ks[0], (B, N, DIM), jnp.float32), 'Wqkv': init(ks[1], (DEPTH, DIM, 3 * INNER)), 'q_scale': jnp.ones((DEPTH, DIM_HEAD), jnp.float32), 'k_scale': jnp.ones((DEPTH, DIM_HEAD), jnp.float32), 'Wo': init(ks[2], (DEPTH, INNER, DIM)), 'ln_g': jnp.ones((DEPTH, DIM), jnp.float32), 'ln_b': jnp.zeros((DEPTH, DIM), jnp.float32), 'W1': init(ks[3], (DEPTH, DIM, 2 * DIM_INNER)), 'b1': jnp.zeros((DEPTH, 2 * DIM_INNER), jnp.float32), 'W2': init(ks[4], (DEPTH, DIM_INNER, DIM)), 'b2': jnp.zeros((DEPTH, DIM), jnp.float32)}
    _L1_ffn_all = _L1_ffn_setup()
    _L1_ffn_in = {k: v for k, v in _L1_ffn_all.items() if k in ('Wqkv', 'q_scale', 'k_scale', 'Wo', 'ln_g', 'ln_b', 'W1', 'b1', 'W2', 'b2')}
    del _L1_ffn_all
    return {'x': x, 'ctx_1024': ctx_1024, 'L0_xattn_w_q': _L0_xattn_in['w_q'], 'L0_xattn_b_q': _L0_xattn_in['b_q'], 'L0_xattn_w_k': _L0_xattn_in['w_k'], 'L0_xattn_b_k': _L0_xattn_in['b_k'], 'L0_xattn_w_v': _L0_xattn_in['w_v'], 'L0_xattn_b_v': _L0_xattn_in['b_v'], 'L0_xattn_w_out': _L0_xattn_in['w_out'], 'L0_xattn_b_out': _L0_xattn_in['b_out'], 'L0_ffn_router_w': _L0_ffn_in['router_w'], 'L0_ffn_router_b': _L0_ffn_in['router_b'], 'L0_ffn_expert_w': _L0_ffn_in['expert_w'], 'L1_xattn_gamma_x': _L1_xattn_in['gamma_x'], 'L1_xattn_beta_x': _L1_xattn_in['beta_x'], 'L1_xattn_gamma_l': _L1_xattn_in['gamma_l'], 'L1_xattn_beta_l': _L1_xattn_in['beta_l'], 'L1_xattn_Wq': _L1_xattn_in['Wq'], 'L1_xattn_Wkv': _L1_xattn_in['Wkv'], 'L1_xattn_Wo': _L1_xattn_in['Wo'], 'L1_ffn_Wqkv': _L1_ffn_in['Wqkv'], 'L1_ffn_q_scale': _L1_ffn_in['q_scale'], 'L1_ffn_k_scale': _L1_ffn_in['k_scale'], 'L1_ffn_Wo': _L1_ffn_in['Wo'], 'L1_ffn_ln_g': _L1_ffn_in['ln_g'], 'L1_ffn_ln_b': _L1_ffn_in['ln_b'], 'L1_ffn_W1': _L1_ffn_in['W1'], 'L1_ffn_b1': _L1_ffn_in['b1'], 'L1_ffn_W2': _L1_ffn_in['W2'], 'L1_ffn_b2': _L1_ffn_in['b2']}

def reference(x, ctx_1024, L0_xattn_w_q, L0_xattn_b_q, L0_xattn_w_k, L0_xattn_b_k, L0_xattn_w_v, L0_xattn_b_v, L0_xattn_w_out, L0_xattn_b_out, L0_ffn_router_w, L0_ffn_router_b, L0_ffn_expert_w, L1_xattn_gamma_x, L1_xattn_beta_x, L1_xattn_gamma_l, L1_xattn_beta_l, L1_xattn_Wq, L1_xattn_Wkv, L1_xattn_Wo, L1_ffn_Wqkv, L1_ffn_q_scale, L1_ffn_k_scale, L1_ffn_Wo, L1_ffn_ln_g, L1_ffn_ln_b, L1_ffn_W1, L1_ffn_b1, L1_ffn_W2, L1_ffn_b2):
    import jax
    import jax.numpy as jnp

    def _L0_xattn_ref(q, k, v, w_q, b_q, w_k, b_k, w_v, b_v, w_out, b_out):
        import jax, jax.numpy as jnp
        import numpy as np
        D_MODEL = 128
        N_HEAD = 16
        D_HEAD = D_MODEL // N_HEAD
        B, S, _ = q.shape
        qh = (q @ w_q.T + b_q).reshape(B, S, N_HEAD, D_HEAD)
        kh = (k @ w_k.T + b_k).reshape(B, S, N_HEAD, D_HEAD)
        vh = (v @ w_v.T + b_v).reshape(B, S, N_HEAD, D_HEAD)
        scores = jnp.einsum('bqhd,bkhd->bhqk', qh, kh) / jnp.sqrt(jnp.asarray(D_HEAD, qh.dtype))
        attn = jax.nn.softmax(scores, axis=-1)
        out = jnp.einsum('bhqk,bkhd->bqhd', attn, vh).reshape(B, S, D_MODEL)
        return out @ w_out.T + b_out

    def _L0_ffn_ref(tokens, router_w, router_b, expert_w):
        import jax, jax.numpy as jnp
        import numpy as np
        HIDDEN = 128
        NUM_EXPERTS = 16
        TOP_K = 6
        EPS = 1e-10
        B, S, H = tokens.shape
        E = expert_w.shape[0]
        T = B * S
        logits = jnp.einsum('bsh,eh->bse', tokens, router_w) + router_b
        probs = jax.nn.softmax(logits, axis=-1)
        top_p, top_i = jax.lax.top_k(probs, TOP_K)
        top_p = top_p / (jnp.sum(top_p, axis=-1, keepdims=True) + EPS)
        x = tokens.reshape(T, H)
        flat_i = top_i.reshape(T, TOP_K)
        flat_p = top_p.reshape(T, TOP_K)
        gate = jnp.zeros((T, E), dtype=flat_p.dtype)
        gate = gate.at[jnp.arange(T)[:, None], flat_i].add(flat_p)
        acc = jnp.maximum(jnp.sum(gate, axis=-1), EPS)
        out = jnp.zeros_like(x)
        for e in range(E):
            out = out + x @ expert_w[e] * gate[:, e:e + 1]
        out = (out / acc[:, None]).reshape(B, S, H)
        out = out + EPS * jnp.sum(top_p, axis=-1, keepdims=True)
        return out

    def _L1_xattn_ref(x, latents, gamma_x, beta_x, gamma_l, beta_l, Wq, Wkv, Wo):
        import jax, jax.numpy as jnp
        import numpy as np
        DIM = 128
        HEAD_DIM = 64
        NUM_HEADS = 8
        INNER = HEAD_DIM * NUM_HEADS
        ROT_DIM = HEAD_DIM
        ROPE_BASE = 10000.0
        EPS = 1e-05

        def layer_norm(x, g, b):
            mu = jnp.mean(x, axis=-1, keepdims=True)
            var = jnp.var(x, axis=-1, keepdims=True)
            return (x - mu) * jax.lax.rsqrt(var + EPS) * g + b

        def rope_rotate_k(k):
            n = k.shape[1]
            half = ROT_DIM // 2
            inv_freq = 1.0 / ROPE_BASE ** (jnp.arange(0, ROT_DIM, 2, dtype=jnp.float32) / ROT_DIM)
            theta = jnp.arange(n, dtype=jnp.float32)[:, None] * inv_freq[None, :]
            angles = jnp.concatenate([theta, theta], axis=-1)
            cos = jnp.cos(angles)[None, :, None, :].astype(k.dtype)
            sin = jnp.sin(angles)[None, :, None, :].astype(k.dtype)
            k_rope, k_pass = (k[..., :ROT_DIM], k[..., ROT_DIM:])
            neg_half = jnp.concatenate([-k_rope[..., half:], k_rope[..., :half]], axis=-1)
            k_rope = k_rope * cos + neg_half * sin
            return jnp.concatenate([k_rope, k_pass], axis=-1)
        b, n, _ = x.shape
        m = latents.shape[1]
        h, d = (NUM_HEADS, HEAD_DIM)
        scale = d ** (-0.5)
        xn = layer_norm(x, gamma_x, beta_x)
        ln = layer_norm(latents, gamma_l, beta_l)
        q = (ln @ Wq).reshape(b, m, h, d)
        kv_x = xn @ Wkv
        k_x, v_x = (kv_x[..., :INNER], kv_x[..., INNER:])
        kv_l = ln @ Wkv
        k_l, v_l = (kv_l[..., :INNER], kv_l[..., INNER:])
        k_x = k_x.reshape(b, n, h, d)
        v_x = v_x.reshape(b, n, h, d)
        k_x = rope_rotate_k(k_x)
        q = jnp.transpose(q, (0, 2, 1, 3)) * scale
        k_x = jnp.transpose(k_x, (0, 2, 1, 3))
        v_x = jnp.transpose(v_x, (0, 2, 1, 3))
        k_l = jnp.transpose(k_l.reshape(b, m, h, d), (0, 2, 1, 3))
        v_l = jnp.transpose(v_l.reshape(b, m, h, d), (0, 2, 1, 3))
        k = jnp.concatenate([k_x, k_l], axis=2)
        v = jnp.concatenate([v_x, v_l], axis=2)
        sim = jnp.einsum('bhid,bhjd->bhij', q, k)
        attn = jax.nn.softmax(sim, axis=-1)
        out = jnp.einsum('bhij,bhjd->bhid', attn, v)
        out = jnp.transpose(out, (0, 2, 1, 3)).reshape(b, m, INNER)
        return out @ Wo

    def _L1_ffn_ref(x, Wqkv, q_scale, k_scale, Wo, ln_g, ln_b, W1, b1, W2, b2):
        import jax, jax.numpy as jnp
        import numpy as np
        DIM = 128
        DEPTH = 6
        HEADS = 16
        DIM_HEAD = 64
        WINDOW = 32
        INNER = HEADS * DIM_HEAD
        DIM_INNER = int(DIM * 4 * 2 / 3)
        QK_SCALE = 8.0

        def shift_tokens(t):
            a, s = jnp.split(t, 2, -1)
            s = jnp.pad(s, ((0, 0), (1, 0), (0, 0)))[:, :-1]
            return jnp.concatenate([a, s], -1)

        def l2norm(t):
            return t / jnp.maximum(jnp.linalg.norm(t, axis=-1, keepdims=True), 1e-12)

        def rotate_half(x):
            x1, x2 = jnp.split(x, 2, -1)
            return jnp.concatenate([-x2, x1], -1)

        def rotary_tables(n):
            half = jnp.arange(0, DIM_HEAD, 2, dtype=jnp.float32)
            inv_freq = 1.0 / 10000.0 ** (half / DIM_HEAD)
            t = jnp.arange(n, dtype=jnp.float32)
            freqs = t[:, None] * inv_freq[None, :]
            freqs = jnp.concatenate([freqs, freqs], -1)
            base_scale = (half + 0.4 * DIM_HEAD) / (1.4 * DIM_HEAD)
            power = (t - n // 2) / (WINDOW // 2)
            scale = base_scale[None, :] ** power[:, None]
            scale = jnp.concatenate([scale, scale], -1)
            return (freqs, scale)

        def local_attention(q, k, v):
            b, h, n, d = q.shape
            w = WINDOW
            nw = n // w
            bq = q.reshape(b, h, nw, w, d)
            bk = k.reshape(b, h, nw, w, d)
            bv = v.reshape(b, h, nw, w, d)

            def look(t):
                p = jnp.pad(t, ((0, 0), (0, 0), (1, 0), (0, 0), (0, 0)))
                return jnp.concatenate([p[:, :, :nw], p[:, :, 1:]], axis=3)
            bk2, bv2 = (look(bk), look(bv))
            seq = jnp.arange(n).reshape(nw, w)
            seq_p = jnp.pad(seq, ((1, 0), (0, 0)), constant_values=-1)
            jt = jnp.concatenate([seq_p[:nw], seq_p[1:]], axis=1)
            it = seq[:, :, None]
            jb = jt[:, None, :]
            mask = (it < jb) | (it > jb + w) | (jb == -1)
            sim = jnp.einsum('bhwie,bhwje->bhwij', bq, bk2) * QK_SCALE
            sim = jnp.where(mask, -jnp.finfo(sim.dtype).max, sim)
            attn = jax.nn.softmax(sim, -1)
            out = jnp.einsum('bhwij,bhwje->bhwie', attn, bv2)
            return out.reshape(b, h, n, d)

        def attn_layer(x, Wqkv, qs, ksc, Wo):
            b, n, _ = x.shape
            qkv = x @ Wqkv
            q, k, v = jnp.split(qkv, 3, -1)
            sh = lambda t: t.reshape(b, n, HEADS, DIM_HEAD).transpose(0, 2, 1, 3)
            q, k, v = (sh(q), sh(k), sh(v))
            q = l2norm(q) * qs
            k = l2norm(k) * ksc
            freqs, scale = rotary_tables(n)
            cos, sin = (jnp.cos(freqs), jnp.sin(freqs))
            q = q * cos * scale + rotate_half(q) * sin * scale
            inv = 1.0 / scale
            k = k * cos * inv + rotate_half(k) * sin * inv
            out = local_attention(q, k, v)
            out = out.transpose(0, 2, 1, 3).reshape(b, n, INNER)
            return out @ Wo

        def ffn_layer(x, g, bln, W1, b1, W2, b2):
            mu = x.mean(-1, keepdims=True)
            var = ((x - mu) ** 2).mean(-1, keepdims=True)
            xn = (x - mu) / jnp.sqrt(var + 1e-05) * g + bln
            hg = xn @ W1 + b1
            a, gate = jnp.split(hg, 2, -1)
            return a * jax.nn.gelu(gate, approximate=False) @ W2 + b2
        for i in range(DEPTH):
            x = attn_layer(shift_tokens(x), Wqkv[i], q_scale[i], k_scale[i], Wo[i]) + x
            x = ffn_layer(shift_tokens(x), ln_g[i], ln_b[i], W1[i], b1[i], W2[i], b2[i]) + x
        return x
    x = x + _L0_xattn_ref(_layernorm(x, axis=-1), ctx_1024, ctx_1024, L0_xattn_w_q, L0_xattn_b_q, L0_xattn_w_k, L0_xattn_b_k, L0_xattn_w_v, L0_xattn_b_v, L0_xattn_w_out, L0_xattn_b_out)
    x = x + _L0_ffn_ref(_layernorm(x, axis=-1), L0_ffn_router_w, L0_ffn_router_b, L0_ffn_expert_w)
    x = x + _L1_xattn_ref(ctx_1024, _layernorm(x, axis=-1), L1_xattn_gamma_x, L1_xattn_beta_x, L1_xattn_gamma_l, L1_xattn_beta_l, L1_xattn_Wq, L1_xattn_Wkv, L1_xattn_Wo)
    x = x + _L1_ffn_ref(_layernorm(x, axis=-1), L1_ffn_Wqkv, L1_ffn_q_scale, L1_ffn_k_scale, L1_ffn_Wo, L1_ffn_ln_g, L1_ffn_ln_b, L1_ffn_W1, L1_ffn_b1, L1_ffn_W2, L1_ffn_b2)
    return x

_drawn_inputs = setup_inputs


def setup_inputs(seed=0):
    import zlib

    import numpy as np

    out = dict(_drawn_inputs(seed))
    spreads = {'L0_xattn_b_q': (0.0, 0.1),
     'L0_xattn_b_k': (0.0, 0.8),
     'L0_xattn_b_v': (0.0, 0.1),
     'L0_xattn_b_out': (0.0, 0.1),
     'L1_xattn_gamma_x': (1.0, 0.2),
     'L1_xattn_beta_x': (0.0, 0.1),
     'L1_xattn_gamma_l': (1.0, 0.2),
     'L1_xattn_beta_l': (0.0, 0.1),
     'L1_ffn_q_scale': (1.0, 0.6),
     'L1_ffn_k_scale': (1.0, 0.6),
     'L1_ffn_ln_g': (1.0, 0.6),
     'L1_ffn_ln_b': (0.0, 0.8),
     'L1_ffn_b1': (0.0, 0.8),
     'L1_ffn_b2': (0.0, 0.1)}
    factors = {'L1_ffn_W1': 4.16, 'L1_ffn_W2': 4.093}
    for name, (base, spread) in spreads.items():
        noise = np.random.default_rng([zlib.crc32(name.encode()), seed]).standard_normal(out[name].shape)
        drawn = base * np.exp(spread * noise) if base else spread * noise
        out[name] = jnp.asarray(drawn.astype(out[name].dtype))
    for name, factor in factors.items():
        out[name] = (out[name] * factor).astype(out[name].dtype)
    return out
```

```python
from contextlib import ExitStack

import concourse.bass as bass
from concourse import mybir

F32 = mybir.dt.float32
BF16 = mybir.dt.bfloat16
ALU = mybir.AluOpType
ACT = mybir.ActivationFunctionType
AX = mybir.AxisListType

B, S, D = 16, 128, 128
HALF = D // 2
UNITS = 4 * B
UNROLL = 8
LN_EPS = 1e-5
CREDIT = 1

A_HEADS, A_DIM = 16, 8
EXPERTS, TOP_K, MOE_EPS = 16, 6, 1e-10
C_HEADS, C_DIM = 8, 64
C_INNER = C_HEADS * C_DIM
LAYERS, L_HEADS, L_DIM, WINDOW = 6, 16, 64, 32
L_INNER = L_HEADS * L_DIM
FF = int(D * 4 * 2 / 3)
CHUNKS = [(c, min(128, FF - c)) for c in range(0, FF, 128)]
QK_SCALE = 8.0
MASKED = -1e30

K_IDENT, K_SHIFT, K_COS, K_SIN, K_COST, K_SINT, K_HEAD = 0, 128, 256, 384, 512, 640, 768
K_ALL = K_HEAD + A_HEADS


def drive(eng, stages, units, unroll, per_batch):
    depth = max(skew for skew, _ in stages)
    assert depth <= unroll and units % unroll == 0 and unroll % per_batch == 0

    def slot(first_unit, first_batch, c):
        for skew, fn in stages:
            k = c - skew
            if isinstance(first_unit, int) and not 0 <= first_unit + k < units:
                continue
            fn(first_unit + k, first_batch + k // per_batch, k % unroll)

    for c in range(unroll):
        slot(0, 0, c)
    with eng.Fori(1, units // unroll) as i:
        for c in range(unroll):
            slot(i * unroll, i * (unroll // per_batch), c)
    for c in range(depth):
        slot(units, units // per_batch, c)


def build(nc, t, out):
    with ExitStack() as ctx:
        def sb(name, shape, dt=F32):
            return ctx.enter_context(nc.sbuf_tensor(name, shape, dt))

        def sem(name):
            return ctx.enter_context(nc.semaphore(name))

        def need(eng, s, before, n):
            if isinstance(n, int):
                n = max(n, 0)
                if isinstance(before, int) and before + n <= 0:
                    return
            eng.wait_ge(s, before + n + CREDIT)

        bank = ctx.enter_context(nc.psum_tensor("bank", [128, 8, 512], F32))
        X = sb("X", [128, B, D])
        Y = sb("Y", [128, B, D])
        CTX = sb("CTX", [128, B, D])
        const = sb("const", [128, K_ALL])
        ident = const[:, K_IDENT:K_IDENT + 128]
        shift_t = const[:, K_SHIFT:K_SHIFT + 128]
        cos_t = const[:, K_COST:K_COST + 128]
        sin_t = const[:, K_SINT:K_SINT + 128]
        head_of = const[:, K_HEAD:K_HEAD + A_HEADS]
        cbf = sb("cbf", [128, 384], BF16)
        ident_bf, mask_bf = cbf[:, 0:128], cbf[:, 128:384]
        minus_half = sb("minus_half", [128, 8])

        sm = sb("sm", [128, 2, 512])
        prob = sb("prob", [128, 2, 512])
        probT = sb("probT", [128, 2, 512])
        peak = sb("peak", [128, 2, 4])
        rsum = sb("rsum", [128, 2, 4])
        o = sb("o", [128, 2, 256])

        ln_st = sb("ln_st", [128, 4, 6])
        ln_mv = sb("ln_mv", [128, 4, 2])
        ln_rs = sb("ln_rs", [128, 4])
        n1 = sb("n1", [128, 2, D])
        n2 = sb("n2", [128, 2, D])
        nx = sb("nx", [128, 2, D])

        wa_raw = sb("wa_raw", [128, 4, D])
        waT = sb("waT", [128, 4, D])
        a_bq = sb("a_bq", [128, 1])
        a_bk = sb("a_bk", [128, 1])
        a_bv = sb("a_bv", [128, D])
        a_bo = sb("a_bo", [128, D])
        xcT = sb("xcT", [128, 2, 2, 128])
        a_q = sb("a_q", [128, 2, 128])
        a_k = sb("a_k", [128, 2, 128])
        a_km = sb("a_km", [128, 2, 4, 128])
        a_v = sb("a_v", [128, 2, A_HEADS, A_DIM + 1])
        a_o = sb("a_o", [128, 2, D])
        a_oT = sb("a_oT", [128, 2, D])
        a_y = sb("a_y", [128, 2, D])

        ew = sb("ew", [128, EXPERTS, D])
        rw_raw = sb("rw_raw", [EXPERTS, D])
        rwT = sb("rwT", [128, EXPERTS])
        rb = sb("rb", [128, EXPERTS])
        m_xT = sb("m_xT", [128, 2, 128])
        m_lg = sb("m_lg", [128, 2, EXPERTS])
        m_e = sb("m_e", [128, 2, EXPERTS])
        m_top = sb("m_top", [128, 8])
        m_p = sb("m_p", [128, EXPERTS + 2])
        m_rep = sb("m_rep", [128, EXPERTS + 2])
        m_sel = sb("m_sel", [128, EXPERTS])
        m_gate = sb("m_gate", [128, EXPERTS])
        m_s = sb("m_s", [128, 8])
        m_eps = sb("m_eps", [128, 1])
        m_es = sb("m_es", [128, 2, 1])
        m_prod = sb("m_prod", [128, EXPERTS, D])
        m_acc = sb("m_acc", [128, D])

        c_wq = sb("c_wq", [128, C_INNER])
        c_wkv = sb("c_wkv", [128, 2 * C_INNER])
        c_wks = sb("c_wks", [128, C_INNER])
        c_wo = sb("c_wo", [128, C_INNER // 128, D])
        c_x = sb("c_x", [128, 2, D])
        c_g = sb("c_g", [128, 4])
        c_kvT = sb("c_kvT", [128, 2, 2, 128])
        c_q = sb("c_q", [128, 2, 128])
        c_k = sb("c_k", [128, 2, 256])
        c_r = sb("c_r", [128, 2, 2, 128])
        c_v = sb("c_v", [128, 2, 2, C_HEADS, C_DIM + 1])
        c_oT = sb("c_oT", [128, 2, 4, 128])

        l_w = sb("l_w", [128, 3 * L_INNER])
        l_wo = sb("l_wo", [128, L_INNER // 128, D])
        l_sc = sb("l_sc", [128, LAYERS, 2, L_DIM])
        l_tab = sb("l_tab", [128, LAYERS, 2, 2, L_DIM])
        xin = sb("xin", [128, 2, D])
        xsT = sb("xsT", [128, 2, 128])
        l_rot = sb("l_rot", [128, 2, 2, 512])
        l_sq = sb("l_sq", [128, 512])
        l_ss = sb("l_ss", [128, 2, 8])
        l_rn = sb("l_rn", [128, 2, 8])
        l_qk = sb("l_qk", [128, 2, 512])
        l_qkT = sb("l_qkT", [128, 2, 512])
        l_v = sb("l_v", [128, UNROLL, 4, L_DIM + 1])
        l_oT = sb("l_oT", [128, 2, 8, 128])

        f_w1 = sb("f_w1", [128, 2 * FF])
        f_w2 = sb("f_w2", [128, len(CHUNKS), D])
        f_g = sb("f_g", [128, 2])
        f_b1 = sb("f_b1", [128, 2, len(CHUNKS)])
        f_b2 = sb("f_b2", [128, D])
        f_st = sb("f_st", [128, 4, 6])
        f_mv = sb("f_mv", [128, 4, 2])
        f_rs = sb("f_rs", [128, 4])
        f_n = sb("f_n", [128, 4, D])
        f_nT = sb("f_nT", [128, 2, 512])
        f_ge = sb("f_ge", [128, 2, 512])
        f_h = sb("f_h", [128, 2, len(CHUNKS), 512])

        ld_const, ld_x, ld_ctx, ld_a = (sem(n) for n in ("ld_const", "ld_x", "ld_ctx", "ld_a"))
        ld_m, ld_c, ld_sc, ld_lw, ld_fw = (sem(n) for n in ("ld_m", "ld_c", "ld_sc", "ld_lw", "ld_fw"))
        preset = sem("preset")
        tables = sem("tables")
        passed = {nc.vector.engine: sem("passed_dve"), nc.gpsimd.engine: sem("passed_pool")}
        w_turned, w_copied = sem("w_turned"), sem("w_copied")
        summed, stored = sem("summed"), sem("stored")

        stage_all = []

        def stage_sems(prefix, names):
            made = {n: sem(prefix + n) for n in names.split()}
            stage_all.extend(made.values())
            return made

        core = "s_done peaked sub_done exp_done turned probT_done pv_done rsum_done o_done "
        a = stage_sems("a_", core + "stats ln_stat pool_ln ln_rstd n_done x_turned xT_done proj qk_done v_done "
                 "km_done o_turned oT_done out_done biased res_done")
        m = stage_sems("m_", "stats ln_stat pool_ln ln_rstd n_done turned xT_done logits lg_chain shifted exp_done "
                 "experts g_chain gate_done prod_done reduced res_done")
        c = stage_sems("c_", core + "stats ln_stat pool_ln ln_rstd n1_done stats2 ln_stat2 pool_ln2 ln_rstd2 n_done "
                 "x_turned kvT_done v_proj v_done qk_proj rot_done evac_done rope_done o_turned oT_done out_done "
                 "res_done y_copied y_stats y_stat y_pool y_rstd y_done")
        l = stage_sems("l_", core + "xin_done x_turned xs_done qk_proj v_proj rot_done sq_done ss_done pool_ss rn_done "
                 "add_done qk_done qk_turned qkT_done v_done o_turned oT_done out_done res_done")
        f = stage_sems("f_", "xs stats stat pool_st rstd n_done turned nT_done hidden gelu_done h_done out_mm yb_done "
                 "y_done")

        block = ctx.enter_context(nc.Block())

        def apart(eng):
            eng.sem_inc(passed[eng.engine], 1)

        def one(t3, b):
            return t3[:, bass.ds(b, 1), :].rearrange("p a n -> p (a n)")

        @block.sync
        def _(sp):
            sp.dma_start(const[:], t["const"]).then_inc(ld_const, 16)
            sp.dma_start(X[:], t["x"].rearrange("b s d -> s b d")).then_inc(ld_x, 16)
            for k, n in enumerate(("w_q", "w_k", "w_v", "w_out")):
                sp.dma_start(wa_raw[:, k, :], t["L0_xattn_" + n]).then_inc(ld_a, 16)
            sp.dma_start(CTX[:], t["ctx_1024"].rearrange("b s d -> s b d")).then_inc(ld_ctx, 16)
            for dst, n in ((a_bq, "b_q"), (a_bk, "b_k")):
                sp.dma_start(dst[:], t["L0_xattn_" + n].rearrange("(p a) -> p a", a=1)).then_inc(ld_a, 16)
            for dst, n in ((a_bv, "b_v"), (a_bo, "b_out")):
                sp.dma_start(dst[:], t["L0_xattn_" + n].partition_broadcast(128)).then_inc(ld_a, 16)
            sp.dma_start(rw_raw[:], t["L0_ffn_router_w"]).then_inc(ld_m, 16)
            sp.dma_start(rb[:], t["L0_ffn_router_b"].partition_broadcast(128)).then_inc(ld_m, 16)
            sp.dma_start(ew[:], t["L0_ffn_expert_w"].rearrange("e h d -> h e d")).then_inc(ld_m, 16)
            sp.dma_start(cbf[:], t["const_bf"]).then_inc(ld_c, 16)
            sp.dma_start(c_wq[:], t["L1_xattn_Wq"]).then_inc(ld_c, 16)
            sp.dma_start(c_wkv[:], t["L1_xattn_Wkv"]).then_inc(ld_c, 16)
            heads = "p (h s n) -> p h s n"
            for s in range(2):
                sp.dma_start(c_wks[:].rearrange(heads, s=2, n=C_DIM // 2)[:, :, s],
                             t["L1_xattn_Wkv"][:, 0:C_INNER].rearrange(heads, s=2, n=C_DIM // 2)[:, :, 1 - s])\
                  .then_inc(ld_c, 16)
            sp.dma_start(c_wo[:], t["L1_xattn_Wo"].rearrange("(c p) n -> p c n", p=128)).then_inc(ld_c, 16)
            for k, n in enumerate(("gamma_x", "beta_x", "gamma_l", "beta_l")):
                sp.dma_start(c_g[:, k:k + 1], t["L1_xattn_" + n].rearrange("(p a) -> p a", a=1)).then_inc(ld_c, 16)
            for k, n in enumerate(("q_scale", "k_scale")):
                sp.dma_start(l_sc[:, :, k, :], t["L1_ffn_" + n].partition_broadcast(128)).then_inc(ld_sc, 16)
            with sp.Fori(0, LAYERS) as ly:
                def layer(n):
                    x = t["L1_ffn_" + n]
                    v = x[bass.ds(ly, 1)]
                    return v.rearrange("a b c -> (a b) c") if len(x.shape) == 3 else v.rearrange("a b -> (a b)")

                need(sp, l["out_done"], 0, ly * B)
                sp.dma_start(l_w[:], layer("Wqkv")).then_inc(ld_lw, 16)
                sp.dma_start(l_wo[:], layer("Wo").rearrange("(c p) n -> p c n", p=128)).then_inc(ld_lw, 16)
                need(sp, f["y_done"], 0, ly * 4)
                sp.dma_start(f_w1[:], layer("W1")).then_inc(ld_fw, 16)
                full = FF // 128 * 128
                sp.dma_start(f_w2[:, 0:full // 128, :],
                             layer("W2")[0:full].rearrange("(c p) n -> p c n", p=128)).then_inc(ld_fw, 16)
                sp.dma_start(f_w2[0:FF - full, full // 128, :], layer("W2")[full:FF]).then_inc(ld_fw, 16)
                sp.dma_start(f_g[:, 0:1], layer("ln_g").rearrange("(p a) -> p a", a=1)).then_inc(ld_fw, 16)
                sp.dma_start(f_g[:, 1:2], layer("ln_b").rearrange("(p a) -> p a", a=1)).then_inc(ld_fw, 16)
                for s in range(2):
                    for k, (c0, n) in enumerate(CHUNKS):
                        sp.dma_start(f_b1[0:n, s, k:k + 1], layer("b1")[s * FF + c0:s * FF + c0 + n]
                                     .rearrange("(p a) -> p a", a=1)).then_inc(ld_fw, 16)
                sp.dma_start(f_b2[:], layer("b2").partition_broadcast(128)).then_inc(ld_fw, 16)
            sp.wait_ge(summed, 4)
            sp.dma_start(out.rearrange("b s d -> s b d"), X[:]).then_inc(stored, 16)
            sp.wait_ge(stored, 16)

        FW_DMAS = 5 + 2 * len(CHUNKS) + 1

        @block.gpsimd
        def _(pool):
            pool.memset(minus_half[:], -0.5)
            pool.memset(a_v[:, :, :, A_DIM:], 1.0)
            pool.memset(c_v[:, :, :, :, C_DIM:], 1.0)
            pool.memset(l_v[:, :, :, L_DIM:], 1.0)
            pool.memset(m_p[:, EXPERTS:], -1.0)
            pool.memset(xsT[:, :, 0:1], 0.0).then_inc(preset, 1)
            pool.wait_ge(preset, 1)

            def rstd(dst, var, chain, n, done):
                apart(pool)
                pool.tensor_scalar(dst, var, LN_EPS, None, ALU.add).then_inc(chain, 1)
                need(pool, chain, 0, n + 1)
                pool.tensor_tensor(dst, dst, minus_half[:, 0:dst.shape[1]], ALU.pow).then_inc(done, 1)

            def a_rstd(u, b, j):
                if j % 4 == 0:
                    need(pool, a["ln_stat"], 0, b + 1)
                    rstd(ln_rs[:, 0:1], ln_mv[:, 0, 1:2], a["pool_ln"], b, a["ln_rstd"])

            def a_mask_k(u, b, j):
                g = j % 4
                need(pool, a["qk_done"], 0, b + 1)
                need(pool, a["s_done"], 0, u - 1)
                pool.tensor_tensor(a_km[:, j % 2], a_k[:, j // 4, None, :].broadcast_to([128, 4, 128]),
                                   head_of[:, 4 * g:4 * g + 4, None].broadcast_to([128, 4, 128]),
                                   ALU.mult).then_inc(a["km_done"], 1)

            pool.wait_ge(ld_const, 16)
            drive(pool, [(3, a_mask_k), (0, a_rstd)], UNITS, UNROLL, 4)

            pool.wait_ge(ld_sc, 32)
            for k, at in enumerate((K_COS, K_SIN)):
                base = const[:, at:at + 2 * L_DIM]
                if k == 0:
                    v = l_sc[:]
                    ins = pool.tensor_tensor(
                        l_tab[:, :, 0].rearrange("p l q n -> p l (q n)"), v.rearrange("p l q n -> p l (q n)"),
                        base[:, None, :].broadcast_to([128, LAYERS, 2 * L_DIM]), ALU.mult)
                else:
                    for q in range(2):
                        ins = pool.tensor_tensor(
                            l_tab[:, :, 1, q].rearrange("p l (s n) -> p l s n", s=2),
                            l_sc[:, :, q].rearrange("p l (s n) -> p l s n", s=2)[:, :, ::-1, :],
                            base[:, q * L_DIM:(q + 1) * L_DIM].rearrange("p (s n) -> p s n", s=2)[:, None]
                            .broadcast_to([128, LAYERS, 2, L_DIM // 2]), ALU.mult)
            ins.then_inc(tables, 1)

            def m_rstd(u, b, j):
                need(pool, m["ln_stat"], 0, b + 1)
                rstd(ln_rs[:, j:j + 1], ln_mv[:, j, 1:2], m["pool_ln"], b, m["ln_rstd"])

            drive(pool, [(0, m_rstd)], B, 2, 1)

            def c_rstd(u, b, j):
                if j % 4 == 0:
                    need(pool, c["ln_stat"], 0, b + 1)
                    rstd(ln_rs[:, 0:2], ln_mv[:, 0:2, 1], c["pool_ln"], b, c["ln_rstd"])

            def c_rstd2(u, b, j):
                if j % 4 == 0:
                    need(pool, c["ln_stat2"], 0, b + 1)
                    rstd(ln_rs[:, 2:3], ln_mv[:, 2, 1:2], c["pool_ln2"], b, c["ln_rstd2"])

            def y_rstd(u, b, j):
                if j % 4 == 3:
                    need(pool, c["y_stat"], 0, b + 1)
                    rstd(ln_rs[:, 3:4], ln_mv[:, 3, 1:2], c["y_pool"], b, c["y_rstd"])

            drive(pool, [(0, c_rstd), (1, c_rstd2), (7, y_rstd)], UNITS, UNROLL, 4)

            with pool.Fori(0, LAYERS) as ly:
                ub = ly * UNITS

                def l_norm(u, b, j):
                    k = j % 2
                    need(pool, l["rot_done"], ub, u + 1)
                    need(pool, l["qk_turned"], ub, u - 1)
                    pool.tensor_tensor(l_qk[:, k], l_rot[:, k, 0], l_rot[:, k, 1], ALU.add).then_inc(l["add_done"], 1)
                    need(pool, l["ss_done"], ub, u + 1)
                    apart(pool)
                    pool.tensor_scalar(l_rn[:, k], l_ss[:, k], 1e-24, None, ALU.max).then_inc(l["pool_ss"], 1)
                    need(pool, l["pool_ss"], ub, u + 1)
                    pool.tensor_tensor(l_rn[:, k], l_rn[:, k], minus_half[:], ALU.pow).then_inc(l["rn_done"], 1)
                    need(pool, l["add_done"], ub, u + 1)
                    need(pool, l["rn_done"], ub, u + 1)
                    v = l_qk[:, k].rearrange("p (h n) -> p h n", n=L_DIM)
                    pool.tensor_tensor(v, v, l_rn[:, k, :, None].broadcast_to([128, 8, L_DIM]),
                                       ALU.mult).then_inc(l["qk_done"], 1)

                drive(pool, [(1, l_norm)], UNITS, UNROLL, 4)

                fb = ly * 4
                pool.wait_ge(ld_fw, (ly + 1) * (16 * FW_DMAS))
                for g in range(4):
                    yg = Y[:, 4 * g:4 * g + 4, :]
                    need(pool, f["stat"], 0, fb + g + 1)
                    apart(pool)
                    pool.tensor_scalar(f_rs[:], f_mv[:, :, 1], LN_EPS, None, ALU.add).then_inc(f["pool_st"], 1)
                    need(pool, f["pool_st"], 0, fb + g + 1)
                    pool.tensor_tensor(f_rs[:], f_rs[:], minus_half[:, 0:4], ALU.pow).then_inc(f["rstd"], 1)
                    need(pool, f["xs"], 0, fb + g + 1)
                    pool.tensor_tensor(yg, yg, f_b2[:, None, :].broadcast_to([128, 4, D]),
                                       ALU.add).then_inc(f["yb_done"], 1)

        @block.tensor
        def _(pe):
            def turn(s, base, u, j):
                need(pe, s["exp_done"], base, u + 1)
                need(pe, s["probT_done"], base, u)
                for h in range(4):
                    ins = pe.transpose(bank[:, 5, h * 128:(h + 1) * 128], prob[:, j % 2, h * 128:(h + 1) * 128],
                                       ident)
                ins.then_inc(s["turned"], 1)

            pe.wait_ge(ld_const, 16)
            pe.wait_ge(ld_a, 16 * 8)
            for k in range(4):
                pe.transpose(bank[:, 2, k * 128:(k + 1) * 128], wa_raw[:, k, :], ident)
            pe.wait_ge(ld_m, 48)
            pe.transpose(bank[:, 1, 0:EXPERTS], rw_raw[:], ident[0:EXPERTS, 0:EXPERTS]).then_inc(w_turned, 1)
            pe.wait_ge(w_copied, 1)
            pe.wait_ge(preset, 1)

            def a_turn_x(u, b, j):
                if j % 4 == 0:
                    k = j // 4
                    need(pe, a["n_done"], 0, b + 1)
                    need(pe, a["xT_done"], 0, b)
                    pe.transpose(bank[:, 2, 0:128], n1[:, k], ident)
                    pe.transpose(bank[:, 2, 128:256], nx[:, k], ident).then_inc(a["x_turned"], 1)

            def a_project(u, b, j):
                if j % 4 == 0:
                    k = j // 4
                    need(pe, a["xT_done"], 0, b + 1)
                    need(pe, a["qk_done"], 0, b)
                    need(pe, a["v_done"], 0, b)
                    pe.matmul(bank[:, 0, 0:128], waT[:, 0], xcT[:, k, 0], start=True, stop=True)
                    pe.matmul(bank[:, 0, 128:256], waT[:, 1], xcT[:, k, 1], start=True, stop=True)
                    pe.matmul(bank[:, 1, 0:128], xcT[:, k, 1], waT[:, 2], start=True, stop=True)\
                      .then_inc(a["proj"], 1)

            def a_scores(u, b, j):
                need(pe, a["km_done"], 0, u + 1)
                need(pe, a["qk_done"], 0, b + 1)
                need(pe, a["sub_done"], 0, u - 1)
                pe.matmul(bank[:, 3 + j % 2, :], a_q[:, j // 4], a_km[:, j % 2].rearrange("p h n -> p (h n)"),
                          start=True, stop=True).then_inc(a["s_done"], 1)

            def a_pv(u, b, j):
                need(pe, a["probT_done"], 0, u + 1)
                need(pe, a["v_done"], 0, b + 1)
                need(pe, a["o_done"], 0, u)
                for h in range(4):
                    w = A_DIM + 1
                    ins = pe.matmul(bank[:, 6, h * w:(h + 1) * w], probT[:, j % 2, h * 128:(h + 1) * 128],
                                    a_v[:, j // 4, j % 4 * 4 + h, :], start=True, stop=True)
                ins.then_inc(a["pv_done"], 1)

            def a_output(u, b, j):
                if j % 4 == 3:
                    k = j // 4
                    need(pe, a["o_done"], 0, u + 1)
                    need(pe, a["res_done"], 0, b)
                    pe.transpose(bank[:, 7, 0:128], a_o[:, k], ident).then_inc(a["o_turned"], 1)
                    need(pe, a["oT_done"], 0, b + 1)
                    pe.matmul(bank[:, 7, 128:256], a_oT[:, k], waT[:, 3], start=True, stop=True)\
                      .then_inc(a["out_done"], 1)

            drive(pe, [(4, a_scores), (6, lambda u, b, j: turn(a, 0, u, j)), (2, a_turn_x), (7, a_output),
                       (6, a_pv), (2, a_project)], UNITS, UNROLL, 4)

            def m_turn(u, b, j):
                need(pe, m["n_done"], 0, b + 1)
                need(pe, m["xT_done"], 0, b)
                pe.transpose(bank[:, 2, 0:128], n1[:, j], ident).then_inc(m["turned"], 1)

            def m_logits(u, b, j):
                need(pe, m["xT_done"], 0, b + 1)
                need(pe, m["shifted"], 0, b)
                pe.matmul(bank[:, 0, 0:EXPERTS], m_xT[:, j], rwT[:], start=True, stop=True).then_inc(m["logits"], 1)

            def m_experts(u, b, j):
                need(pe, m["xT_done"], 0, b + 1)
                need(pe, m["prod_done"], 0, b)
                for q in range(4):
                    ins = pe.matmul(bank[:, 3 + q, :], m_xT[:, j],
                                    ew[:, 4 * q:4 * q + 4, :].rearrange("p e n -> p (e n)"), start=True, stop=True)
                ins.then_inc(m["experts"], 1)

            drive(pe, [(1, m_turn), (1, m_logits), (1, m_experts)], B, 2, 1)

            pe.wait_ge(ld_c, 16 * 10)

            def c_turn_x(u, b, j):
                if j % 4 == 0:
                    k = j // 4
                    need(pe, c["n_done"], 0, b + 1)
                    need(pe, c["kvT_done"], 0, b)
                    pe.transpose(bank[:, 2, 0:128], nx[:, k], ident)
                    pe.transpose(bank[:, 2, 128:256], n2[:, k], ident).then_inc(c["x_turned"], 1)

            def c_values(u, b, j):
                tile = j % 4
                if tile < 2:
                    need(pe, c["kvT_done"], 0, b + 1)
                    need(pe, c["v_done"], 0, b * 2 + tile)
                    pe.matmul(bank[:, 1, :], c_kvT[:, j // 4, tile], c_wkv[:, C_INNER:], start=True, stop=True)\
                      .then_inc(c["v_proj"], 1)

            def c_project(u, b, j):
                k, p = j // 4, j % 4
                w = slice(128 * p, 128 * p + 128)
                need(pe, c["kvT_done"], 0, b + 1)
                need(pe, c["evac_done"], 0, u)
                both = c_kvT[:, k].rearrange("p t n -> p (t n)")
                pe.matmul(bank[:, 0, 0:128], c_wq[:, w], c_kvT[:, k, 1], start=True, stop=True)
                pe.matmul(bank[:, 0, 128:384], c_wkv[:, w], both, start=True, stop=True)
                pe.matmul(bank[:, 0, 384:512], c_wks[:, w], c_kvT[:, k, 0], start=True, stop=True)\
                  .then_inc(c["qk_proj"], 1)

            def c_scores(u, b, j):
                need(pe, c["evac_done"], 0, u + 1)
                need(pe, c["rope_done"], 0, u + 1)
                need(pe, c["sub_done"], 0, u)
                for h in range(2):
                    r = slice(64 * h, 64 * h + 64)
                    ins = pe.matmul(bank[:, 3 + h, 0:256], c_q[r, j % 2], c_k[r, j % 2], start=True, stop=True)
                ins.then_inc(c["s_done"], 1)

            def c_pv(u, b, j):
                need(pe, c["probT_done"], 0, u + 1)
                need(pe, c["v_done"], 0, b * 2 + 2)
                need(pe, c["o_done"], 0, u)
                w = C_DIM + 1
                for h in range(2):
                    for tile in range(2):
                        n = h * 2 + tile
                        ins = pe.matmul(bank[:, 6, h * w:(h + 1) * w], probT[:, j % 2, n * 128:(n + 1) * 128],
                                        c_v[:, j // 4, tile, 2 * (j % 4) + h, :], start=tile == 0, stop=tile == 1)
                ins.then_inc(c["pv_done"], 1)

            def c_output(u, b, j):
                k = j // 4
                need(pe, c["o_done"], 0, u + 1)
                need(pe, c["oT_done"], 0, u)
                need(pe, c["res_done"], 0, b)
                pe.transpose(bank[:, 7, 0:128], o[:, j % 2, 0:128], ident).then_inc(c["o_turned"], 1)
                if j % 4 == 3:
                    need(pe, c["oT_done"], 0, u + 1)
                    for p in range(4):
                        ins = pe.matmul(bank[:, 7, 128:256], c_oT[:, k, p], c_wo[:, p], start=p == 0, stop=p == 3)
                    ins.then_inc(c["out_done"], 1)

            drive(pe, [(3, c_project), (3, c_values), (6, lambda u, b, j: turn(c, 0, u, j)), (4, c_scores),
                       (7, c_output), (6, c_pv), (2, c_turn_x)], UNITS, UNROLL, 4)

            with pe.Fori(0, LAYERS) as ly:
                ub, bb = ly * UNITS, ly * B

                def l_turn_x(u, b, j):
                    if j % 4 == 0:
                        need(pe, l["xin_done"], bb, b + 1)
                        need(pe, l["oT_done"], ub, u - 5)
                        need(pe, l["res_done"], bb, b - 2)
                        need(pe, l["xs_done"], bb * 2, b * 2)
                        pe.transpose(bank[:, 7, 384:512], xin[:, j // 4], ident).then_inc(l["x_turned"], 1)

                def l_project(u, b, j):
                    g = j % 4
                    w = l_w[:].rearrange("p (t n) -> p t n", t=3)
                    need(pe, l["xs_done"], bb * 2, b * 2 + 2)
                    need(pe, l["sq_done"], ub, u)
                    pe.matmul(bank[:, 0, :].rearrange("p (q n) -> p q n", q=2), xsT[:, j // 4],
                              w[:, 0:2, 256 * g:256 * g + 256], start=True, stop=True).then_inc(l["qk_proj"], 1)
                    need(pe, l["v_done"], ub, u)
                    pe.matmul(bank[:, 1, 0:256], xsT[:, j // 4], w[:, 2, 256 * g:256 * g + 256],
                              start=True, stop=True).then_inc(l["v_proj"], 1)

                def l_turn_qk(u, b, j):
                    need(pe, l["qk_done"], ub, u + 1)
                    need(pe, l["qkT_done"], ub, u)
                    for n in range(4):
                        ins = pe.transpose(bank[:, 2, n * 128:(n + 1) * 128],
                                           l_qk[:, j % 2, n * 128:(n + 1) * 128], ident)
                    ins.then_inc(l["qk_turned"], 1)

                def l_scores(u, b, j):
                    need(pe, l["qkT_done"], ub, u + 1)
                    need(pe, l["sub_done"], ub, u)
                    for r in range(2):
                        pe.matmul(bank[:, 3 + r, 0:256], ident_bf, mask_bf, start=True, stop=False,
                                  skip_group_check=True)
                    for p in range(2):
                        for r in range(2):
                            rows = slice(64 * r, 64 * r + 64)
                            ins = pe.matmul(bank[:, 3 + r, 128 * p:128 * p + 128],
                                            l_qkT[rows, j % 2, 128 * p:128 * p + 128],
                                            l_qkT[rows, j % 2, 256 + 128 * p:384 + 128 * p],
                                            start=False, stop=True, skip_group_check=True)
                    ins.then_inc(l["s_done"], 1)

                def l_pv(u, b, j):
                    need(pe, l["probT_done"], ub, u + 1)
                    need(pe, l["v_done"], ub, u + 1)
                    need(pe, l["o_done"], ub, u)
                    w = L_DIM + 1
                    for h in range(4):
                        n = h % 2 * 2 + h // 2
                        ins = pe.matmul(bank[:, 6, h * w:(h + 1) * w], probT[:, j % 2, n * 128:(n + 1) * 128],
                                        l_v[:, j, h, :], start=True, stop=True)
                    ins.then_inc(l["pv_done"], 1)

                def l_turn_o(u, b, j):
                    r = j % 4
                    need(pe, l["o_done"], ub, u + 1)
                    need(pe, l["oT_done"], ub, u)
                    need(pe, l["res_done"], bb, b)
                    turned = b + (r + 5) // 4 + 1
                    if isinstance(turned, int):
                        turned = min(turned, B)
                    need(pe, l["xs_done"], bb * 2, turned * 2)
                    for p in range(2):
                        ins = pe.transpose(bank[:, 7, p * 128:(p + 1) * 128], o[:, j % 2, p * 128:(p + 1) * 128],
                                           ident)
                    ins.then_inc(l["o_turned"], 1)

                def l_output(u, b, j):
                    if j % 4 == 3:
                        need(pe, l["oT_done"], ub, u + 1)
                        turned = b + 3
                        if isinstance(turned, int):
                            turned = min(turned, B)
                        need(pe, l["xs_done"], bb * 2, turned * 2)
                        for p in range(8):
                            ins = pe.matmul(bank[:, 7, 256:384], l_oT[:, j // 4, p], l_wo[:, p],
                                            start=p == 0, stop=p == 7)
                        ins.then_inc(l["out_done"], 1)

                pe.wait_ge(ld_lw, (ly + 1) * 32)
                drive(pe, [(1, l_project), (3, l_turn_qk), (5, lambda u, b, j: turn(l, ub, u, j)), (3, l_scores),
                           (6, l_turn_o), (0, l_turn_x), (5, l_pv), (6, l_output)], UNITS, UNROLL, 4)

                fb = ly * 4
                need(pe, l["res_done"], 0, (ly + 1) * B)
                pe.wait_ge(ld_fw, (ly + 1) * (16 * FW_DMAS))

                def f_shift(g):
                    v = bank[:, 0, :].rearrange("p (a n) -> p a n", a=4)
                    yg = Y[:, 4 * g:4 * g + 4, :]
                    need(pe, f["n_done"], 0, fb + g)
                    pe.matmul(v[:, :, 0:HALF], ident, yg[:, :, 0:HALF], start=True, stop=True)
                    pe.matmul(v[:, :, HALF:], shift_t, yg[:, :, HALF:], start=True, stop=True).then_inc(f["xs"], 1)

                def f_turn(g):
                    need(pe, f["n_done"], 0, fb + g + 1)
                    need(pe, f["nT_done"], 0, fb + g)
                    for n in range(4):
                        ins = pe.transpose(bank[:, 2, n * 128:(n + 1) * 128], f_n[:, n], ident)
                    ins.then_inc(f["turned"], 1)

                def f_hidden(g, k):
                    c0, n = CHUNKS[k]
                    i = len(CHUNKS) * g + k
                    need(pe, f["nT_done"], 0, fb + g + 1)
                    need(pe, f["h_done"], ly * 12, i - 1)
                    at = 3 + i % 2 * 2
                    pe.matmul(bank[0:n, at, :], f_w1[:, FF + c0:FF + c0 + n], f_nT[:, g % 2], start=True, stop=True)
                    pe.matmul(bank[0:n, at + 1, :], f_w1[:, c0:c0 + n], f_nT[:, g % 2], start=True, stop=True)\
                      .then_inc(f["hidden"], 1)

                def f_out(g):
                    need(pe, f["h_done"], 0, ly * 12 + 3 * g + 3)
                    need(pe, f["y_done"], 0, fb + g)
                    for q in range(4):
                        for k, (c0, n) in enumerate(CHUNKS):
                            ins = pe.matmul(bank[:, 7, q * 128:(q + 1) * 128], f_h[0:n, g % 2, k, q * 128:(q + 1) * 128],
                                            f_w2[0:n, k, :], start=k == 0, stop=k == len(CHUNKS) - 1)
                    ins.then_inc(f["out_mm"], 1)

                f_shift(0)
                f_turn(0)
                for g in range(4):
                    f_hidden(g, 0)
                    if g < 3:
                        f_shift(g + 1)
                    f_hidden(g, 1)
                    if g < 3:
                        f_turn(g + 1)
                    f_hidden(g, 2)
                    f_out(g)

        @block.scalar
        def _(act):
            def exp(s, base, u, j, scale):
                need(act, s["sub_done"], base, u + 1)
                need(act, s["turned"], base, u - 1)
                act.activation(prob[:, j % 2, :], sm[:, j % 2, :], ACT.Exp, scale=scale).then_inc(s["exp_done"], 1)

            def copy_prob(s, base, u, j):
                need(act, s["turned"], base, u + 1)
                need(act, s["pv_done"], base, u - 1)
                act.activation(probT[:, j % 2, :], bank[:, 5, :], ACT.Copy).then_inc(s["probT_done"], 1)

            for s in stage_all:
                act.sem_inc(s, CREDIT)
            act.wait_ge(w_turned, 1)
            act.activation(waT[:].rearrange("p a n -> p (a n)"), bank[:, 2, :], ACT.Copy)
            act.activation(rwT[:], bank[:, 1, 0:EXPERTS], ACT.Copy).then_inc(w_copied, 1)

            def a_copy_x(u, b, j):
                if j % 4 == 0:
                    need(act, a["x_turned"], 0, b + 1)
                    need(act, a["proj"], 0, b - 1)
                    act.activation(xcT[:, j // 4].rearrange("p a n -> p (a n)"), bank[:, 2, 0:256], ACT.Copy)\
                       .then_inc(a["xT_done"], 1)

            def a_copy_qk(u, b, j):
                if j % 4 == 0:
                    k = j // 4
                    need(act, a["proj"], 0, b + 1)
                    need(act, a["s_done"], 0, u - 4)
                    need(act, a["km_done"], 0, u - 4)
                    act.activation(a_q[:, k], bank[:, 0, 0:128], ACT.Identity, bias=a_bq[:])
                    act.activation(a_k[:, k], bank[:, 0, 128:256], ACT.Identity, bias=a_bk[:])\
                       .then_inc(a["qk_done"], 1)

            def a_copy_o(u, b, j):
                if j % 4 == 3:
                    need(act, a["o_turned"], 0, b + 1)
                    need(act, a["out_done"], 0, b)
                    act.activation(a_oT[:, j // 4], bank[:, 7, 0:128], ACT.Copy).then_inc(a["oT_done"], 1)

            act.wait_ge(ld_a, 16 * 8)
            drive(act, [(6, lambda u, b, j: copy_prob(a, 0, u, j)), (2, a_copy_x), (7, a_copy_o),
                        (2, a_copy_qk), (4, lambda u, b, j: exp(a, 0, u, j, A_DIM ** -0.5))], UNITS, UNROLL, 4)

            def m_copy_x(u, b, j):
                need(act, m["turned"], 0, b + 1)
                need(act, m["experts"], 0, b - 1)
                act.activation(m_xT[:, j], bank[:, 2, 0:128], ACT.Copy).then_inc(m["xT_done"], 1)

            def m_exp(u, b, j):
                need(act, m["shifted"], 0, b + 1)
                need(act, m["gate_done"], 0, b - 1)
                act.activation(m_e[:, j], m_lg[:, j], ACT.Exp, accum_out=m_es[:, j]).then_inc(m["exp_done"], 1)

            drive(act, [(1, m_copy_x), (1, m_exp)], B, 2, 1)

            act.wait_ge(ld_c, 16 * 10)

            def c_copy_x(u, b, j):
                if j % 4 == 0:
                    k = j // 4
                    need(act, c["x_turned"], 0, b + 1)
                    need(act, c["qk_proj"], 0, u - 4)
                    need(act, c["v_proj"], 0, b * 2 - 2)
                    for tile in range(2):
                        ins = act.activation(c_kvT[:, k, tile], bank[:, 2, tile * 128:(tile + 1) * 128], ACT.Identity,
                                             bias=c_g[:, 2 * tile + 1:2 * tile + 2],
                                             scale=c_g[:, 2 * tile:2 * tile + 1])
                    ins.then_inc(c["kvT_done"], 1)

            def c_copy_v(u, b, j):
                tile = j % 4
                if tile < 2:
                    need(act, c["v_proj"], 0, b * 2 + tile + 1)
                    need(act, c["pv_done"], 0, u - tile - 4)
                    act.activation(c_v[:, j // 4, tile, :, 0:C_DIM],
                                   bank[:, 1, :].rearrange("p (h n) -> p h n", n=C_DIM), ACT.Copy)\
                       .then_inc(c["v_done"], 1)

            def c_copy_qk(u, b, j):
                need(act, c["qk_proj"], 0, u + 1)
                need(act, c["rot_done"], 0, u + 1)
                need(act, c["s_done"], 0, u - 1)
                act.activation(c_q[:, j % 2], bank[:, 0, 0:128], ACT.Copy, scale=C_DIM ** -0.5)
                act.activation(c_k[:, j % 2, 128:256], bank[:, 0, 256:384], ACT.Copy).then_inc(c["evac_done"], 1)

            def c_copy_o(u, b, j):
                need(act, c["o_turned"], 0, u + 1)
                need(act, c["out_done"], 0, b)
                act.activation(c_oT[:, j // 4, j % 4], bank[:, 7, 0:128], ACT.Copy).then_inc(c["oT_done"], 1)

            drive(act, [(3, c_copy_qk), (3, c_copy_v), (6, lambda u, b, j: copy_prob(c, 0, u, j)), (7, c_copy_o),
                        (2, c_copy_x), (4, lambda u, b, j: exp(c, 0, u, j, 1.0))], UNITS, UNROLL, 4)

            with act.Fori(0, LAYERS) as ly:
                ub, bb = ly * UNITS, ly * B

                def l_copy_x(u, b, j):
                    if j % 4 == 0:
                        k = j // 4
                        need(act, l["x_turned"], bb, b + 1)
                        need(act, l["v_proj"], ub, u - 4)
                        act.activation(xsT[0:HALF, k], bank[0:HALF, 7, 384:512], ACT.Copy).then_inc(l["xs_done"], 1)
                        act.activation(xsT[HALF:, k, 1:], bank[HALF:, 7, 384:511], ACT.Copy).then_inc(l["xs_done"], 1)

                def l_copy_v(u, b, j):
                    need(act, l["v_proj"], ub, u + 1)
                    need(act, l["pv_done"], ub, u - 7)
                    act.activation(l_v[:, j, :, 0:L_DIM],
                                   bank[:, 1, 0:256].rearrange("p (h n) -> p h n", n=L_DIM), ACT.Copy)\
                       .then_inc(l["v_done"], 1)

                def l_square(u, b, j):
                    need(act, l["rot_done"], ub, u + 1)
                    need(act, l["ss_done"], ub, u)
                    act.activation(l_sq[:], bank[:, 0, :], ACT.Square).then_inc(l["sq_done"], 1)

                def l_copy_qk(u, b, j):
                    need(act, l["qk_turned"], ub, u + 1)
                    need(act, l["s_done"], ub, u - 1)
                    act.activation(l_qkT[:, j % 2], bank[:, 2, :], ACT.Copy).then_inc(l["qkT_done"], 1)

                def l_copy_o(u, b, j):
                    g = j % 4
                    need(act, l["o_turned"], ub, u + 1)
                    need(act, l["out_done"], bb, b)
                    act.activation(l_oT[:, j // 4, 2 * g:2 * g + 2].rearrange("p a n -> p (a n)"),
                                   bank[:, 7, 0:256], ACT.Copy).then_inc(l["oT_done"], 1)

                drive(act, [(1, l_copy_v), (3, l_copy_qk), (5, lambda u, b, j: copy_prob(l, ub, u, j)),
                            (1, l_square), (6, l_copy_o), (0, l_copy_x),
                            (3, lambda u, b, j: exp(l, ub, u, j, QK_SCALE))], UNITS, UNROLL, 4)

                fb = ly * 4
                act.wait_ge(ld_fw, (ly + 1) * (16 * FW_DMAS))

                def f_copy_n(g):
                    need(act, f["turned"], 0, fb + g + 1)
                    need(act, f["hidden"], ly * 12, 3 * (g - 1))
                    act.activation(f_nT[:, g % 2], bank[:, 2, :], ACT.Identity, bias=f_g[:, 1:2],
                                   scale=f_g[:, 0:1]).then_inc(f["nT_done"], 1)

                def f_gelu(g, k):
                    n = CHUNKS[k][1]
                    i = len(CHUNKS) * g + k
                    need(act, f["hidden"], 0, ly * 12 + i + 1)
                    need(act, f["h_done"], ly * 12, i - 1)
                    act.activation(f_ge[0:n, i % 2], bank[0:n, 3 + i % 2 * 2, :], ACT.Gelu,
                                   bias=f_b1[0:n, 1, k:k + 1]).then_inc(f["gelu_done"], 1)

                f_copy_n(0)
                for g in range(4):
                    f_gelu(g, 0)
                    f_gelu(g, 1)
                    if g < 3:
                        f_copy_n(g + 1)
                    f_gelu(g, 2)

        @block.vector
        def _(dve):
            def normalise(dst, src, k, done):
                dve.tensor_scalar(dst, src, ln_mv[:, k, 0:1], ln_rs[:, k:k + 1], ALU.subtract, ALU.mult)\
                   .then_inc(done, 1)

            def shift_scores(s, base, u, j, scores, blocks):
                k, (_, p, q, w) = j % 2, scores.shape
                need(dve, s["s_done"], base, u + 1)
                dve.tensor_reduce(peak[:, k, 0:blocks], scores, AX.X, ALU.max).then_inc(s["peaked"], 1)
                need(dve, s["exp_done"], base, u - 1)
                need(dve, s["peaked"], base, u + 1)
                peaks = peak[:, k, 0:blocks].rearrange("p (a b) -> p a b", a=p)[:, :, :, None]
                dve.tensor_tensor(sm[:, k].rearrange("p (a b n) -> p a b n", a=p, b=q), scores,
                                  peaks.broadcast_to([128, p, q, w]), ALU.subtract).then_inc(s["sub_done"], 1)

            def divide(s, base, u, j, heads, width, dst):
                ov = bank[:, 6, 0:heads * (width + 1)].rearrange("p (h n) -> p h n", h=heads)
                need(dve, s["pv_done"], base, u + 1)
                dve.reciprocal(rsum[:, j % 2, 0:heads], ov[:, :, width]).then_inc(s["rsum_done"], 1)
                need(dve, s["rsum_done"], base, u + 1)
                dve.tensor_tensor(dst, ov[:, :, 0:width], rsum[:, j % 2, 0:heads, None]
                                  .broadcast_to([128, heads, width]), ALU.mult).then_inc(s["o_done"], 1)

            dve.wait_ge(ld_x, 16)
            dve.wait_ge(ld_ctx, 16)
            dve.wait_ge(ld_a, 16 * 8)
            dve.wait_ge(preset, 1)

            def a_stats(u, b, j):
                if j % 4 == 0:
                    need(dve, a["x_turned"], 0, b - 1)
                    dve.tensor_scalar(nx[:, j // 4], one(CTX, b), 1.0, None, ALU.mult)
                    dve.bn_stats(ln_st[:, 0], one(X, b)).then_inc(a["stats"], 1)
                    need(dve, a["stats"], 0, b + 1)
                    apart(dve)
                    dve.bn_aggr(ln_mv[:, 0], ln_st[:, 0]).then_inc(a["ln_stat"], 1)

            def a_norm(u, b, j):
                if j % 4 == 0:
                    need(dve, a["ln_rstd"], 0, b + 1)
                    normalise(n1[:, j // 4], one(X, b), 0, a["n_done"])

            def a_values(u, b, j):
                if j % 4 == 0:
                    need(dve, a["proj"], 0, b + 1)
                    need(dve, a["pv_done"], 0, u - 4)
                    dve.tensor_tensor(a_v[:, j // 4, :, 0:A_DIM],
                                      bank[:, 1, 0:128].rearrange("p (h n) -> p h n", n=A_DIM),
                                      a_bv[:].rearrange("p (h n) -> p h n", n=A_DIM), ALU.add).then_inc(a["v_done"], 1)

            def a_shift(u, b, j):
                shift_scores(a, 0, u, j, bank[:, 3 + j % 2, :].rearrange("p (a b n) -> p a b n", a=1, b=4), 4)

            def a_divide(u, b, j):
                g = j % 4
                if g == 0:
                    need(dve, a["o_turned"], 0, b - 1)
                divide(a, 0, u, j, 4, A_DIM,
                       a_o[:, j // 4, 32 * g:32 * g + 32].rearrange("p (h n) -> p h n", n=A_DIM))

            def a_residual(u, b, j):
                if j % 4 == 3:
                    k = j // 4
                    need(dve, a["out_done"], 0, b + 1)
                    dve.tensor_tensor(a_y[:, k], bank[:, 7, 128:256], a_bo[:], ALU.add).then_inc(a["biased"], 1)
                    need(dve, a["biased"], 0, b + 1)
                    dve.tensor_tensor(one(X, b), one(X, b), a_y[:, k], ALU.add).then_inc(a["res_done"], 1)

            drive(dve, [(0, a_stats), (4, a_shift), (6, a_divide), (1, a_norm), (2, a_values), (8, a_residual)],
                  UNITS, UNROLL, 4)

            need(dve, a["res_done"], 0, B)
            dve.wait_ge(ld_m, 48)

            def m_stats(u, b, j):
                dve.bn_stats(ln_st[:, j], one(X, b)).then_inc(m["stats"], 1)
                need(dve, m["stats"], 0, b + 1)
                apart(dve)
                dve.bn_aggr(ln_mv[:, j], ln_st[:, j]).then_inc(m["ln_stat"], 1)

            def m_norm(u, b, j):
                need(dve, m["ln_rstd"], 0, b + 1)
                normalise(n1[:, j], one(X, b), j, m["n_done"])

            def m_shift(u, b, j):
                n = b * 2
                need(dve, m["logits"], 0, b + 1)
                dve.tensor_tensor(m_lg[:, j], bank[:, 0, 0:EXPERTS], rb[:], ALU.add).then_inc(m["lg_chain"], 1)
                need(dve, m["lg_chain"], 0, n + 1)
                apart(dve)
                dve.max(m_top[:], m_lg[:, j]).then_inc(m["lg_chain"], 1)
                need(dve, m["lg_chain"], 0, n + 2)
                dve.tensor_scalar(m_lg[:, j], m_lg[:, j], m_top[:, 0:1], None, ALU.subtract).then_inc(m["shifted"], 1)

            def m_gates(u, b, j):
                steps = 10
                n = [b * steps]

                def link(ins):
                    ins.then_inc(m["g_chain"], 1)
                    n[0] = n[0] + 1
                    need(dve, m["g_chain"], 0, n[0])
                    apart(dve)

                need(dve, m["exp_done"], 0, b + 1)
                link(dve.reciprocal(m_s[:, 0:1], m_es[:, j]))
                link(dve.tensor_scalar(m_p[:, 0:EXPERTS], m_e[:, j], m_s[:, 0:1], None, ALU.mult))
                link(dve.max(m_top[:], m_p[:, 0:EXPERTS]))
                link(dve.memset(m_top[:, TOP_K:], -1.0))
                link(dve.match_replace(m_rep[:], m_top[:], m_p[:], 0.0))
                link(dve.scalar_tensor_tensor(m_sel[:], m_p[:, 0:EXPERTS], 1.0, m_rep[:, 0:EXPERTS], ALU.mult,
                                              ALU.subtract, accum_out=m_s[:, 1:2]))
                link(dve.tensor_scalar(m_s[:, 2:3], m_s[:, 1:2], MOE_EPS, None, ALU.add))
                link(dve.reciprocal(m_s[:, 3:4], m_s[:, 2:3]))
                link(dve.tensor_scalar(m_gate[:], m_sel[:], m_s[:, 3:4], 0.0, ALU.mult, ALU.add,
                                       accum_out=m_s[:, 4:5]))
                link(dve.tensor_scalar(m_s[:, 5:6], m_s[:, 4:5], MOE_EPS, None, ALU.max))
                dve.tensor_scalar(m_eps[:], m_s[:, 4:5], MOE_EPS, None, ALU.mult)
                dve.reciprocal(m_s[:, 6:7], m_s[:, 5:6]).then_inc(m["gate_done"], 1)

            def m_combine(u, b, j):
                need(dve, m["gate_done"], 0, b + 1)
                need(dve, m["experts"], 0, b + 1)
                for q in range(4):
                    ins = dve.tensor_tensor(m_prod[:, 4 * q:4 * q + 4, :],
                                            bank[:, 3 + q, :].rearrange("p (e n) -> p e n", e=4),
                                            m_gate[:, 4 * q:4 * q + 4, None].broadcast_to([128, 4, D]), ALU.mult)
                ins.then_inc(m["prod_done"], 1)
                need(dve, m["prod_done"], 0, b + 1)
                dve.tensor_reduce(m_acc[:], m_prod[:].rearrange("p e n -> p n e"), AX.X, ALU.add)\
                   .then_inc(m["reduced"], 1)
                need(dve, m["reduced"], 0, b * 2 + 1)
                dve.tensor_scalar(m_acc[:], m_acc[:], m_s[:, 6:7], m_eps[:], ALU.mult, ALU.add)\
                   .then_inc(m["reduced"], 1)
                need(dve, m["reduced"], 0, b * 2 + 2)
                dve.tensor_tensor(one(X, b), one(X, b), m_acc[:], ALU.add).then_inc(m["res_done"], 1)

            drive(dve, [(2, m_gates), (0, m_stats), (1, m_norm), (2, m_combine), (1, m_shift)], B, 2, 1)

            need(dve, m["res_done"], 0, B)
            dve.wait_ge(ld_const, 16)

            def c_stats(u, b, j):
                if j % 4 == 0:
                    dve.bn_stats(ln_st[:, 0], one(X, b))
                    dve.bn_stats(ln_st[:, 1], one(CTX, b)).then_inc(c["stats"], 1)
                    need(dve, c["stats"], 0, b + 1)
                    apart(dve)
                    dve.bn_aggr(ln_mv[:, 0], ln_st[:, 0])
                    dve.bn_aggr(ln_mv[:, 1], ln_st[:, 1]).then_inc(c["ln_stat"], 1)

            def c_norm(u, b, j):
                if j % 4 == 0:
                    k = j // 4
                    need(dve, c["x_turned"], 0, b - 1)
                    need(dve, c["ln_rstd"], 0, b + 1)
                    dve.tensor_scalar(nx[:, k], one(CTX, b), ln_mv[:, 1, 0:1], ln_rs[:, 1:2], ALU.subtract,
                                      ALU.mult)
                    normalise(n1[:, k], one(X, b), 0, c["n1_done"])
                    need(dve, c["n1_done"], 0, b + 1)
                    dve.bn_stats(ln_st[:, 2], n1[:, k]).then_inc(c["stats2"], 1)
                    need(dve, c["stats2"], 0, b + 1)
                    apart(dve)
                    dve.bn_aggr(ln_mv[:, 2], ln_st[:, 2]).then_inc(c["ln_stat2"], 1)

            def c_norm2(u, b, j):
                if j % 4 == 0:
                    need(dve, c["ln_rstd2"], 0, b + 1)
                    normalise(n2[:, j // 4], n1[:, j // 4], 2, c["n_done"])

            def c_rotate(u, b, j):
                k = j % 2
                need(dve, c["qk_proj"], 0, u + 1)
                dve.tensor_tensor(c_r[:, k, 0], bank[:, 0, 128:256], cos_t, ALU.mult)
                dve.tensor_tensor(c_r[:, k, 1], bank[:, 0, 384:512], sin_t, ALU.mult).then_inc(c["rot_done"], 1)
                need(dve, c["rot_done"], 0, u + 1)
                need(dve, c["s_done"], 0, u - 1)
                dve.tensor_tensor(c_k[:, k, 0:128], c_r[:, k, 0], c_r[:, k, 1], ALU.add).then_inc(c["rope_done"], 1)

            def c_shift(u, b, j):
                shift_scores(c, 0, u, j, bank[:, 3:5, 0:256].rearrange("p a (b n) -> p a b n", b=1), 2)

            def c_divide(u, b, j):
                need(dve, c["o_turned"], 0, u - 1)
                divide(c, 0, u, j, 2, C_DIM, o[:, j % 2, 0:128].rearrange("p (h n) -> p h n", n=C_DIM))

            def c_residual(u, b, j):
                if j % 4 == 3:
                    k = j // 4
                    need(dve, c["out_done"], 0, b + 1)
                    dve.tensor_tensor(one(X, b), one(X, b), bank[:, 7, 128:256], ALU.add).then_inc(c["res_done"], 1)
                    need(dve, c["res_done"], 0, b + 1)
                    dve.tensor_scalar(c_x[:, k], one(X, b), 1.0, None, ALU.mult).then_inc(c["y_copied"], 1)
                    need(dve, c["y_copied"], 0, b + 1)
                    dve.bn_stats(ln_st[:, 3], c_x[:, k]).then_inc(c["y_stats"], 1)
                    need(dve, c["y_stats"], 0, b + 1)
                    apart(dve)
                    dve.bn_aggr(ln_mv[:, 3], ln_st[:, 3]).then_inc(c["y_stat"], 1)

            def y_norm(u, b, j):
                if j % 4 == 3:
                    need(dve, c["y_rstd"], 0, b + 1)
                    normalise(one(Y, b), c_x[:, j // 4], 3, c["y_done"])

            drive(dve, [(3, c_rotate), (2, c_norm2), (4, c_shift), (6, c_divide), (7, c_residual),
                        (0, c_stats), (1, c_norm), (8, y_norm)], UNITS, UNROLL, 4)
            need(dve, c["y_done"], 0, B)
            dve.wait_ge(tables, 1)

            with dve.Fori(0, LAYERS) as ly:
                ub, bb = ly * UNITS, ly * B

                def table(k):
                    return l_tab[:, bass.ds(ly, 1), k].rearrange("p a q n -> p (a q) n")

                def l_copy_in(u, b, j):
                    if j % 4 == 0:
                        need(dve, l["x_turned"], bb, b - 1)
                        dve.tensor_scalar(xin[:, j // 4], one(Y, b), 1.0, None, ALU.mult).then_inc(l["xin_done"], 1)

                def l_rotate(u, b, j):
                    k = j % 2
                    need(dve, l["add_done"], ub, u - 1)
                    need(dve, l["qk_proj"], ub, u + 1)
                    shape = [128, 2, 4, L_DIM]
                    dve.tensor_tensor(l_rot[:, k, 0].rearrange("p (q h n) -> p q h n", q=2, h=4),
                                      bank[:, 0, :].rearrange("p (q h n) -> p q h n", q=2, h=4),
                                      table(0)[:, :, None, :].broadcast_to(shape), ALU.mult)
                    shape = [128, 2, 4, 2, L_DIM // 2]
                    dve.tensor_tensor(
                        l_rot[:, k, 1].rearrange("p (q h s n) -> p q h s n", q=2, h=4, s=2),
                        bank[:, 0, :].rearrange("p (q h s n) -> p q h s n", q=2, h=4, s=2)[:, :, :, ::-1, :],
                        table(1).rearrange("p q (s n) -> p q s n", s=2)[:, :, None].broadcast_to(shape),
                        ALU.mult).then_inc(l["rot_done"], 1)

                def l_sum_squares(u, b, j):
                    k = j % 2
                    need(dve, l["sq_done"], ub, u + 1)
                    need(dve, l["pool_ss"], ub, u - 1)
                    dve.tensor_reduce(l_ss[:, k], l_sq[:].rearrange("p (h n) -> p h n", n=L_DIM), AX.X, ALU.add)\
                       .then_inc(l["ss_done"], 1)

                def l_shift(u, b, j):
                    shift_scores(l, ub, u, j, bank[:, 3:5, 0:256].rearrange("p a (b n) -> p a b n", b=2), 4)

                def l_divide(u, b, j):
                    need(dve, l["o_turned"], ub, u - 1)
                    divide(l, ub, u, j, 4, L_DIM, o[:, j % 2].rearrange("p (h n) -> p h n", n=L_DIM))

                def l_residual(u, b, j):
                    if j % 4 == 3:
                        need(dve, l["out_done"], bb, b + 1)
                        dve.tensor_tensor(one(Y, b), one(Y, b), bank[:, 7, 256:384], ALU.add).then_inc(l["res_done"], 1)

                need(dve, f["y_done"], 0, ly * 4)
                drive(dve, [(0, l_copy_in), (1, l_rotate), (3, l_shift), (1, l_sum_squares), (5, l_divide),
                            (6, l_residual)], UNITS, UNROLL, 4)

                fb = ly * 4
                dve.wait_ge(ld_fw, (ly + 1) * (16 * FW_DMAS))

                def f_stats(g):
                    need(dve, f["xs"], 0, fb + g + 1)
                    v = bank[:, 0, :].rearrange("p (a n) -> p a n", a=4)
                    apart(dve)
                    for q in range(4):
                        ins = dve.bn_stats(f_st[:, q], v[:, q])
                    ins.then_inc(f["stats"], 1)
                    need(dve, f["stats"], 0, fb + g + 1)
                    apart(dve)
                    for q in range(4):
                        ins = dve.bn_aggr(f_mv[:, q], f_st[:, q])
                    ins.then_inc(f["stat"], 1)

                def f_norm(g):
                    v = bank[:, 0, :].rearrange("p (a n) -> p a n", a=4)
                    need(dve, f["rstd"], 0, fb + g + 1)
                    need(dve, f["turned"], 0, fb + g)
                    for q in range(4):
                        ins = dve.tensor_scalar(f_n[:, q], v[:, q], f_mv[:, q, 0:1], f_rs[:, q:q + 1],
                                                ALU.subtract, ALU.mult)
                    ins.then_inc(f["n_done"], 1)

                def f_gated(g, k):
                    n = CHUNKS[k][1]
                    i = len(CHUNKS) * g + k
                    need(dve, f["gelu_done"], 0, ly * 12 + i + 1)
                    need(dve, f["out_mm"], fb, g - 1)
                    dve.scalar_tensor_tensor(f_h[0:n, g % 2, k], bank[0:n, 4 + i % 2 * 2, :], f_b1[0:n, 0, k:k + 1],
                                             f_ge[0:n, i % 2], ALU.add, ALU.mult).then_inc(f["h_done"], 1)

                def f_residual(g):
                    yg = Y[:, 4 * g:4 * g + 4, :].rearrange("p a n -> p (a n)")
                    need(dve, f["out_mm"], 0, fb + g + 1)
                    need(dve, f["yb_done"], 0, fb + g + 1)
                    dve.tensor_tensor(yg, yg, bank[:, 7, :], ALU.add).then_inc(f["y_done"], 1)

                f_stats(0)
                f_norm(0)
                for g in range(4):
                    f_gated(g, 0)
                    if g < 3:
                        f_stats(g + 1)
                        f_norm(g + 1)
                    f_gated(g, 1)
                    f_gated(g, 2)
                    f_residual(g)

            need(dve, f["y_done"], 0, LAYERS * 4)
            for g in range(4):
                s = slice(4 * g, 4 * g + 4)
                dve.tensor_tensor(X[:, s, :], X[:, s, :], Y[:, s, :], ALU.add).then_inc(summed, 1)


_INS = ["x", "ctx_1024", "L0_xattn_w_q", "L0_xattn_b_q", "L0_xattn_w_k", "L0_xattn_b_k", "L0_xattn_w_v",
        "L0_xattn_b_v", "L0_xattn_w_out", "L0_xattn_b_out", "L0_ffn_router_w", "L0_ffn_router_b",
        "L0_ffn_expert_w", "L1_xattn_gamma_x", "L1_xattn_beta_x", "L1_xattn_gamma_l", "L1_xattn_beta_l",
        "L1_xattn_Wq", "L1_xattn_Wkv", "L1_xattn_Wo", "L1_ffn_Wqkv", "L1_ffn_q_scale", "L1_ffn_k_scale",
        "L1_ffn_Wo", "L1_ffn_ln_g", "L1_ffn_ln_b", "L1_ffn_W1", "L1_ffn_b1", "L1_ffn_W2", "L1_ffn_b2"]


def constants():
    import numpy as np
    from concourse import mybir as _mybir

    f = np.float32
    const = np.zeros((128, K_ALL), f)
    const[:, K_IDENT:K_IDENT + 128] = np.eye(128)
    const[:, K_SHIFT:K_SHIFT + 128] = np.eye(128, k=1)

    half = np.arange(0, L_DIM, 2, dtype=f)
    inv = f(1.0) / f(10000.0) ** (half / f(L_DIM))
    t = np.arange(S, dtype=f)
    freqs = t[:, None] * inv[None, :]
    freqs = np.concatenate([freqs, freqs], -1)
    base = (half + f(0.4 * L_DIM)) / f(1.4 * L_DIM)
    scale = base[None, :] ** ((t - S // 2) / f(WINDOW // 2))[:, None]
    scale = np.concatenate([scale, scale], -1)
    sign = np.where(np.arange(L_DIM) < L_DIM // 2, f(-1.0), f(1.0))[None, :]
    for q, s in enumerate((scale, f(1.0) / scale)):
        const[:, K_COS + q * L_DIM:K_COS + (q + 1) * L_DIM] = np.cos(freqs) * s
        const[:, K_SIN + q * L_DIM:K_SIN + (q + 1) * L_DIM] = np.sin(freqs) * s * sign
    const[:, K_COST:K_COST + 128] = np.tile(np.cos(freqs).T, (2, 1))
    const[:, K_SINT:K_SINT + 128] = np.tile((np.sin(freqs) * sign).T, (2, 1))
    const[np.arange(128), K_HEAD + np.arange(128) // A_DIM] = 1.0

    i, j = np.arange(128)[:, None], np.arange(128)[None, :]
    mask = np.where((i < j) | (i > j + WINDOW), f(MASKED), f(0.0))
    bf = np.concatenate([np.eye(128, dtype=f), mask, mask], 1).astype(_mybir.dt.np(_mybir.dt.bfloat16))
    return {"const": const, "const_bf": bf}


def kernel(**inputs):
    import numpy as _np
    import concourse.bacc as _bacc
    from concourse import mybir as _mybir
    from concourse.bass_utils import run_bass_kernel_spmd as _run

    nc = _bacc.Bacc("TRN2", target_bir_lowering=False, num_devices=1)
    given = {n: _np.ascontiguousarray(inputs[n]) for n in _INS} | constants()
    arrays, args = {}, {}
    for name, a in given.items():
        arrays[f"in_{name}_dram"] = a
        args[name] = nc.dram_tensor(f"in_{name}_dram", a.shape, _mybir.dt.from_np(a.dtype),
                                    kind="ExternalInput").ap()
    out = nc.dram_tensor("out_0_dram", (B, S, D), F32, kind="ExternalOutput").ap()
    build(nc, args, out)
    r = _run(nc, [arrays], core_ids=[0])
    return r.results[0]["out_0_dram"]
```

```python
from contextlib import ExitStack

import concourse.bass as bass
from concourse import mybir

F32 = mybir.dt.float32
BF16 = mybir.dt.bfloat16
ALU = mybir.AluOpType
ACT = mybir.ActivationFunctionType
AX = mybir.AxisListType

B, S, D = 16, 128, 128
HALF = D // 2
UNITS = 4 * B
UNROLL = 8
LN_EPS = 1e-5
CREDIT = 1

A_HEADS, A_DIM = 16, 8
EXPERTS, TOP_K, MOE_EPS = 16, 6, 1e-10
C_HEADS, C_DIM = 8, 64
C_INNER = C_HEADS * C_DIM
LAYERS, L_HEADS, L_DIM, WINDOW = 6, 16, 64, 32
L_INNER = L_HEADS * L_DIM
FF = int(D * 4 * 2 / 3)
CHUNKS = [(c, min(128, FF - c)) for c in range(0, FF, 128)]
QK_SCALE = 8.0
MASKED = -1e30

K_IDENT, K_SHIFT, K_COS, K_SIN, K_COST, K_SINT, K_HEAD = 0, 128, 256, 384, 512, 640, 768
K_ALL = K_HEAD + A_HEADS


class Pipeline:

    def __init__(self, eng, stages, units, unroll, per_batch):
        self.eng, self.stages, self.units, self.unroll, self.per_batch = eng, stages, units, unroll, per_batch
        self.depth = max(skew for skew, _ in stages)
        assert self.depth <= unroll and units % unroll == 0 and unroll % per_batch == 0

    def slot(self, first_unit, first_batch, c):
        for skew, fn in self.stages:
            k = c - skew
            if isinstance(first_unit, int) and not 0 <= first_unit + k < self.units:
                continue
            fn(first_unit + k, first_batch + k // self.per_batch, k % self.unroll)

    def start(self, *slots):
        for c in slots:
            self.slot(0, 0, c)

    def steady(self):
        with self.eng.Fori(1, self.units // self.unroll) as i:
            for c in range(self.unroll):
                self.slot(i * self.unroll, i * (self.unroll // self.per_batch), c)

    def finish(self, *slots):
        for c in slots:
            self.slot(self.units, self.units // self.per_batch, c)


def drive(eng, stages, units, unroll, per_batch):
    pipe = Pipeline(eng, stages, units, unroll, per_batch)
    pipe.start(*range(unroll))
    pipe.steady()
    pipe.finish(*range(pipe.depth))


def build(nc, t, out):
    with ExitStack() as ctx:
        def sb(name, shape, dt=F32):
            return ctx.enter_context(nc.sbuf_tensor(name, shape, dt))

        def sem(name):
            return ctx.enter_context(nc.semaphore(name))

        def upto(before, n):
            return before + (max(n, 0) if isinstance(n, int) else n) + CREDIT

        bank = ctx.enter_context(nc.psum_tensor("bank", [128, 8, 512], F32))
        X = sb("X", [128, B, D])
        Y = sb("Y", [128, B, D])
        CTX = sb("CTX", [128, B, D])
        const = sb("const", [128, K_ALL])
        ident = const[:, K_IDENT:K_IDENT + 128]
        shift_t = const[:, K_SHIFT:K_SHIFT + 128]
        cos_t = const[:, K_COST:K_COST + 128]
        sin_t = const[:, K_SINT:K_SINT + 128]
        head_of = const[:, K_HEAD:K_HEAD + A_HEADS]
        cbf = sb("cbf", [128, 384], BF16)
        ident_bf, mask_bf = cbf[:, 0:128], cbf[:, 128:384]
        minus_half = sb("minus_half", [128, 8])

        sm = sb("sm", [128, 2, 512])
        prob = sb("prob", [128, 2, 512])
        probT = sb("probT", [128, 2, 512])
        peak = sb("peak", [128, 2, 4])
        rsum = sb("rsum", [128, 2, 4])
        o = sb("o", [128, 2, 256])

        ln_st = sb("ln_st", [128, 4, 6])
        ln_mv = sb("ln_mv", [128, 4, 2])
        ln_rs = sb("ln_rs", [128, 4])
        n1 = sb("n1", [128, 2, D])
        n2 = sb("n2", [128, 2, D])
        nx = sb("nx", [128, 2, D])

        wa_raw = sb("wa_raw", [128, 4, D])
        waT = sb("waT", [128, 4, D])
        a_bq = sb("a_bq", [128, 1])
        a_bk = sb("a_bk", [128, 1])
        a_bv = sb("a_bv", [128, D])
        a_bo = sb("a_bo", [128, D])
        xcT = sb("xcT", [128, 2, 2, 128])
        a_q = sb("a_q", [128, 2, 128])
        a_k = sb("a_k", [128, 2, 128])
        a_km = sb("a_km", [128, 2, 4, 128])
        a_v = sb("a_v", [128, 2, A_HEADS, A_DIM + 1])
        a_o = sb("a_o", [128, 2, D])
        a_oT = sb("a_oT", [128, 2, D])
        a_y = sb("a_y", [128, 2, D])

        ew = sb("ew", [128, EXPERTS, D])
        rw_raw = sb("rw_raw", [EXPERTS, D])
        rwT = sb("rwT", [128, EXPERTS])
        rb = sb("rb", [128, EXPERTS])
        m_xT = sb("m_xT", [128, 2, 128])
        m_lg = sb("m_lg", [128, 2, EXPERTS])
        m_e = sb("m_e", [128, 2, EXPERTS])
        m_top = sb("m_top", [128, 8])
        m_p = sb("m_p", [128, EXPERTS + 2])
        m_rep = sb("m_rep", [128, EXPERTS + 2])
        m_sel = sb("m_sel", [128, EXPERTS])
        m_gate = sb("m_gate", [128, EXPERTS])
        m_s = sb("m_s", [128, 8])
        m_eps = sb("m_eps", [128, 1])
        m_es = sb("m_es", [128, 2, 1])
        m_prod = sb("m_prod", [128, EXPERTS, D])
        m_acc = sb("m_acc", [128, D])

        c_wq = sb("c_wq", [128, C_INNER])
        c_wkv = sb("c_wkv", [128, 2 * C_INNER])
        c_wks = sb("c_wks", [128, C_INNER])
        c_wo = sb("c_wo", [128, C_INNER // 128, D])
        c_x = sb("c_x", [128, 2, D])
        c_g = sb("c_g", [128, 4])
        c_kvT = sb("c_kvT", [128, 2, 2, 128])
        c_q = sb("c_q", [128, 2, 128])
        c_k = sb("c_k", [128, 2, 256])
        c_r = sb("c_r", [128, 2, 2, 128])
        c_v = sb("c_v", [128, 2, 2, C_HEADS, C_DIM + 1])
        c_oT = sb("c_oT", [128, 2, 4, 128])

        l_w = sb("l_w", [128, 3 * L_INNER])
        l_wo = sb("l_wo", [128, L_INNER // 128, D])
        l_sc = sb("l_sc", [128, LAYERS, 2, L_DIM])
        l_tab = sb("l_tab", [128, LAYERS, 2, 2, L_DIM])
        xin = sb("xin", [128, 2, D])
        xsT = sb("xsT", [128, 2, 128])
        l_rot = sb("l_rot", [128, 2, 2, 512])
        l_sq = sb("l_sq", [128, 512])
        l_ss = sb("l_ss", [128, 2, 8])
        l_rn = sb("l_rn", [128, 2, 8])
        l_qk = sb("l_qk", [128, 2, 512])
        l_qkT = sb("l_qkT", [128, 2, 512])
        l_v = sb("l_v", [128, UNROLL, 4, L_DIM + 1])
        l_oT = sb("l_oT", [128, 2, 8, 128])

        f_w1 = sb("f_w1", [128, 2 * FF])
        f_w2 = sb("f_w2", [128, len(CHUNKS), D])
        f_g = sb("f_g", [128, 2])
        f_b1 = sb("f_b1", [128, 2, len(CHUNKS)])
        f_b2 = sb("f_b2", [128, D])
        f_st = sb("f_st", [128, 4, 6])
        f_mv = sb("f_mv", [128, 4, 2])
        f_rs = sb("f_rs", [128, 4])
        f_n = sb("f_n", [128, 4, D])
        f_nT = sb("f_nT", [128, 2, 512])
        f_ge = sb("f_ge", [128, 2, 512])
        f_h = sb("f_h", [128, 2, len(CHUNKS), 512])

        ld_const, ld_x, ld_ctx, ld_a = (sem(n) for n in ("ld_const", "ld_x", "ld_ctx", "ld_a"))
        ld_m, ld_c, ld_sc, ld_lw, ld_fw = (sem(n) for n in ("ld_m", "ld_c", "ld_sc", "ld_lw", "ld_fw"))
        preset = sem("preset")
        tables = sem("tables")
        passed = {nc.vector.engine: sem("passed_dve"), nc.gpsimd.engine: sem("passed_pool")}
        w_turned, w_copied = sem("w_turned"), sem("w_copied")
        summed, stored = sem("summed"), sem("stored")

        stage_all = []

        def stage_sems(prefix, names):
            made = {n: sem(prefix + n) for n in names.split()}
            stage_all.extend(made.values())
            return made

        core = "s_done peaked sub_done exp_done turned probT_done pv_done rsum_done o_done "
        a = stage_sems("a_", core + "stats ln_stat pool_ln ln_rstd n_done x_turned xT_done proj qk_done v_done "
                 "km_done o_turned oT_done out_done biased res_done")
        m = stage_sems("m_", "stats ln_stat pool_ln ln_rstd n_done turned xT_done logits lg_chain shifted exp_done "
                 "experts g_chain gate_done prod_done reduced res_done")
        c = stage_sems("c_", core + "stats ln_stat pool_ln ln_rstd n1_done stats2 ln_stat2 pool_ln2 ln_rstd2 n_done "
                 "x_turned kvT_done v_proj v_done qk_proj rot_done evac_done rope_done o_turned oT_done out_done "
                 "res_done y_copied y_stats y_stat y_pool y_rstd y_done")
        l = stage_sems("l_", core + "xin_done x_turned xs_done qk_proj v_proj rot_done sq_done ss_done pool_ss rn_done "
                 "add_done qk_done qk_turned qkT_done v_done o_turned oT_done out_done res_done")
        f = stage_sems("f_", "xs stats stat pool_st rstd n_done turned nT_done hidden gelu_done h_done out_mm yb_done "
                 "y_done")

        block = ctx.enter_context(nc.Block())

        def apart(eng):
            eng.sem_inc(passed[eng.engine], 1)

        def one(t3, b):
            return t3[:, bass.ds(b, 1), :].rearrange("p a n -> p (a n)")

        @block.sync
        def _(sp):
            sp.dma_start(const[:], t["const"]).then_inc(ld_const, 16)
            sp.dma_start(X[:], t["x"].rearrange("b s d -> s b d")).then_inc(ld_x, 16)
            for k, n in enumerate(("w_q", "w_k", "w_v", "w_out")):
                sp.dma_start(wa_raw[:, k, :], t["L0_xattn_" + n]).then_inc(ld_a, 16)
            sp.dma_start(CTX[:], t["ctx_1024"].rearrange("b s d -> s b d")).then_inc(ld_ctx, 16)
            for dst, n in ((a_bq, "b_q"), (a_bk, "b_k")):
                sp.dma_start(dst[:], t["L0_xattn_" + n].rearrange("(p a) -> p a", a=1)).then_inc(ld_a, 16)
            for dst, n in ((a_bv, "b_v"), (a_bo, "b_out")):
                sp.dma_start(dst[:], t["L0_xattn_" + n].partition_broadcast(128)).then_inc(ld_a, 16)
            sp.dma_start(rw_raw[:], t["L0_ffn_router_w"]).then_inc(ld_m, 16)
            sp.dma_start(rb[:], t["L0_ffn_router_b"].partition_broadcast(128)).then_inc(ld_m, 16)
            sp.dma_start(ew[:], t["L0_ffn_expert_w"].rearrange("e h d -> h e d")).then_inc(ld_m, 16)
            sp.dma_start(cbf[:], t["const_bf"]).then_inc(ld_c, 16)
            sp.dma_start(c_wq[:], t["L1_xattn_Wq"]).then_inc(ld_c, 16)
            sp.dma_start(c_wkv[:], t["L1_xattn_Wkv"]).then_inc(ld_c, 16)
            heads = "p (h s n) -> p h s n"
            for s in range(2):
                sp.dma_start(c_wks[:].rearrange(heads, s=2, n=C_DIM // 2)[:, :, s],
                             t["L1_xattn_Wkv"][:, 0:C_INNER].rearrange(heads, s=2, n=C_DIM // 2)[:, :, 1 - s])\
                  .then_inc(ld_c, 16)
            sp.dma_start(c_wo[:], t["L1_xattn_Wo"].rearrange("(c p) n -> p c n", p=128)).then_inc(ld_c, 16)
            for k, n in enumerate(("gamma_x", "beta_x", "gamma_l", "beta_l")):
                sp.dma_start(c_g[:, k:k + 1], t["L1_xattn_" + n].rearrange("(p a) -> p a", a=1)).then_inc(ld_c, 16)
            for k, n in enumerate(("q_scale", "k_scale")):
                sp.dma_start(l_sc[:, :, k, :], t["L1_ffn_" + n].partition_broadcast(128)).then_inc(ld_sc, 16)
            with sp.Fori(0, LAYERS) as ly:
                def layer(n):
                    x = t["L1_ffn_" + n]
                    v = x[bass.ds(ly, 1)]
                    return v.rearrange("a b c -> (a b) c") if len(x.shape) == 3 else v.rearrange("a b -> (a b)")

                sp.wait_ge(l["out_done"], upto(0, ly * B))
                sp.dma_start(l_w[:], layer("Wqkv")).then_inc(ld_lw, 16)
                sp.dma_start(l_wo[:], layer("Wo").rearrange("(c p) n -> p c n", p=128)).then_inc(ld_lw, 16)
                sp.wait_ge(f["y_done"], upto(0, ly * 4))
                sp.dma_start(f_w1[:], layer("W1")).then_inc(ld_fw, 16)
                full = FF // 128 * 128
                sp.dma_start(f_w2[:, 0:full // 128, :],
                             layer("W2")[0:full].rearrange("(c p) n -> p c n", p=128)).then_inc(ld_fw, 16)
                sp.dma_start(f_w2[0:FF - full, full // 128, :], layer("W2")[full:FF]).then_inc(ld_fw, 16)
                sp.dma_start(f_g[:, 0:1], layer("ln_g").rearrange("(p a) -> p a", a=1)).then_inc(ld_fw, 16)
                sp.dma_start(f_g[:, 1:2], layer("ln_b").rearrange("(p a) -> p a", a=1)).then_inc(ld_fw, 16)
                for s in range(2):
                    for k, (c0, n) in enumerate(CHUNKS):
                        sp.dma_start(f_b1[0:n, s, k:k + 1], layer("b1")[s * FF + c0:s * FF + c0 + n]
                                     .rearrange("(p a) -> p a", a=1)).then_inc(ld_fw, 16)
                sp.dma_start(f_b2[:], layer("b2").partition_broadcast(128)).then_inc(ld_fw, 16)
            sp.wait_ge(summed, 4)
            sp.dma_start(out.rearrange("b s d -> s b d"), X[:]).then_inc(stored, 16)
            sp.wait_ge(stored, 16)

        FW_DMAS = 5 + 2 * len(CHUNKS) + 1

        @block.gpsimd
        def _(pool):
            pool.memset(minus_half[:], -0.5)
            pool.memset(a_v[:, :, :, A_DIM:], 1.0)
            pool.memset(c_v[:, :, :, :, C_DIM:], 1.0)
            pool.memset(l_v[:, :, :, L_DIM:], 1.0)
            pool.memset(m_p[:, EXPERTS:], -1.0)
            pool.memset(xsT[:, :, 0:1], 0.0).then_inc(preset, 1)
            pool.wait_ge(preset, 1)

            def rstd(dst, var, chain, n, done):
                apart(pool)
                pool.tensor_scalar(dst, var, LN_EPS, None, ALU.add).then_inc(chain, 1)
                pool.wait_ge(chain, upto(0, n + 1))
                pool.tensor_tensor(dst, dst, minus_half[:, 0:dst.shape[1]], ALU.pow).then_inc(done, 1)

            def a_rstd(u, b, j):
                if j % 4 == 0:
                    pool.wait_ge(a["ln_stat"], upto(0, b + 1))
                    rstd(ln_rs[:, 0:1], ln_mv[:, 0, 1:2], a["pool_ln"], b, a["ln_rstd"])

            def a_mask_k(u, b, j):
                g = j % 4
                pool.wait_ge(a["qk_done"], upto(0, b + 1))
                pool.wait_ge(a["s_done"], upto(0, u - 1))
                pool.tensor_tensor(a_km[:, j % 2], a_k[:, j // 4, None, :].broadcast_to([128, 4, 128]),
                                   head_of[:, 4 * g:4 * g + 4, None].broadcast_to([128, 4, 128]),
                                   ALU.mult).then_inc(a["km_done"], 1)

            pool.wait_ge(ld_const, 16)
            drive(pool, [(3, a_mask_k), (0, a_rstd)], UNITS, UNROLL, 4)

            pool.wait_ge(ld_sc, 32)
            for k, at in enumerate((K_COS, K_SIN)):
                base = const[:, at:at + 2 * L_DIM]
                if k == 0:
                    v = l_sc[:]
                    ins = pool.tensor_tensor(
                        l_tab[:, :, 0].rearrange("p l q n -> p l (q n)"), v.rearrange("p l q n -> p l (q n)"),
                        base[:, None, :].broadcast_to([128, LAYERS, 2 * L_DIM]), ALU.mult)
                else:
                    for q in range(2):
                        ins = pool.tensor_tensor(
                            l_tab[:, :, 1, q].rearrange("p l (s n) -> p l s n", s=2),
                            l_sc[:, :, q].rearrange("p l (s n) -> p l s n", s=2)[:, :, ::-1, :],
                            base[:, q * L_DIM:(q + 1) * L_DIM].rearrange("p (s n) -> p s n", s=2)[:, None]
                            .broadcast_to([128, LAYERS, 2, L_DIM // 2]), ALU.mult)
            ins.then_inc(tables, 1)

            def m_rstd(u, b, j):
                pool.wait_ge(m["ln_stat"], upto(0, b + 1))
                rstd(ln_rs[:, j:j + 1], ln_mv[:, j, 1:2], m["pool_ln"], b, m["ln_rstd"])

            drive(pool, [(0, m_rstd)], B, 2, 1)

            def c_rstd(u, b, j):
                if j % 4 == 0:
                    pool.wait_ge(c["ln_stat"], upto(0, b + 1))
                    rstd(ln_rs[:, 0:2], ln_mv[:, 0:2, 1], c["pool_ln"], b, c["ln_rstd"])

            def c_rstd2(u, b, j):
                if j % 4 == 0:
                    pool.wait_ge(c["ln_stat2"], upto(0, b + 1))
                    rstd(ln_rs[:, 2:3], ln_mv[:, 2, 1:2], c["pool_ln2"], b, c["ln_rstd2"])

            def y_rstd(u, b, j):
                if j % 4 == 3:
                    pool.wait_ge(c["y_stat"], upto(0, b + 1))
                    rstd(ln_rs[:, 3:4], ln_mv[:, 3, 1:2], c["y_pool"], b, c["y_rstd"])

            drive(pool, [(0, c_rstd), (1, c_rstd2), (7, y_rstd)], UNITS, UNROLL, 4)

            def attention(ly):
                ub = ly * UNITS

                def l_norm(u, b, j):
                    k = j % 2
                    pool.wait_ge(l["rot_done"], upto(ub, u + 1))
                    pool.wait_ge(l["qk_turned"], upto(ub, u - 1))
                    pool.tensor_tensor(l_qk[:, k], l_rot[:, k, 0], l_rot[:, k, 1], ALU.add).then_inc(l["add_done"], 1)
                    pool.wait_ge(l["ss_done"], upto(ub, u + 1))
                    apart(pool)
                    pool.tensor_scalar(l_rn[:, k], l_ss[:, k], 1e-24, None, ALU.max).then_inc(l["pool_ss"], 1)
                    pool.wait_ge(l["pool_ss"], upto(ub, u + 1))
                    pool.tensor_tensor(l_rn[:, k], l_rn[:, k], minus_half[:], ALU.pow).then_inc(l["rn_done"], 1)
                    pool.wait_ge(l["add_done"], upto(ub, u + 1))
                    pool.wait_ge(l["rn_done"], upto(ub, u + 1))
                    v = l_qk[:, k].rearrange("p (h n) -> p h n", n=L_DIM)
                    pool.tensor_tensor(v, v, l_rn[:, k, :, None].broadcast_to([128, 8, L_DIM]),
                                       ALU.mult).then_inc(l["qk_done"], 1)

                return Pipeline(pool, [(1, l_norm)], UNITS, UNROLL, 4)

            def feed_forward(ly):
                fb = ly * 4
                pool.wait_ge(ld_fw, (ly + 1) * (16 * FW_DMAS))
                for g in range(4):
                    yg = Y[:, 4 * g:4 * g + 4, :]
                    pool.wait_ge(f["stat"], upto(0, fb + g + 1))
                    apart(pool)
                    pool.tensor_scalar(f_rs[:], f_mv[:, :, 1], LN_EPS, None, ALU.add).then_inc(f["pool_st"], 1)
                    pool.wait_ge(f["pool_st"], upto(0, fb + g + 1))
                    pool.tensor_tensor(f_rs[:], f_rs[:], minus_half[:, 0:4], ALU.pow).then_inc(f["rstd"], 1)
                    pool.wait_ge(f["xs"], upto(0, fb + g + 1))
                    pool.tensor_tensor(yg, yg, f_b2[:, None, :].broadcast_to([128, 4, D]),
                                       ALU.add).then_inc(f["yb_done"], 1)

            def rest_of_layer(ly, att, nxt):
                att.steady()
                att.finish(0)
                feed_forward(ly)
                if nxt is not None:
                    nxt.start(*range(UNROLL))

            attention(0).start(*range(UNROLL))
            with pool.Fori(0, LAYERS - 1) as ly:
                rest_of_layer(ly, attention(ly), attention(ly + 1))
            rest_of_layer(LAYERS - 1, attention(LAYERS - 1), None)

        @block.tensor
        def _(pe):
            def turn(s, base, u, j):
                pe.wait_ge(s["exp_done"], upto(base, u + 1))
                pe.wait_ge(s["probT_done"], upto(base, u))
                for h in range(4):
                    ins = pe.transpose(bank[:, 5, h * 128:(h + 1) * 128], prob[:, j % 2, h * 128:(h + 1) * 128],
                                       ident)
                ins.then_inc(s["turned"], 1)

            pe.wait_ge(ld_const, 16)
            pe.wait_ge(ld_a, 16 * 8)
            for k in range(4):
                pe.transpose(bank[:, 2, k * 128:(k + 1) * 128], wa_raw[:, k, :], ident)
            pe.wait_ge(ld_m, 48)
            pe.transpose(bank[:, 1, 0:EXPERTS], rw_raw[:], ident[0:EXPERTS, 0:EXPERTS]).then_inc(w_turned, 1)
            pe.wait_ge(w_copied, 1)
            pe.wait_ge(preset, 1)

            def a_turn_x(u, b, j):
                if j % 4 == 0:
                    k = j // 4
                    pe.wait_ge(a["n_done"], upto(0, b + 1))
                    pe.wait_ge(a["xT_done"], upto(0, b))
                    pe.transpose(bank[:, 2, 0:128], n1[:, k], ident)
                    pe.transpose(bank[:, 2, 128:256], nx[:, k], ident).then_inc(a["x_turned"], 1)

            def a_project(u, b, j):
                if j % 4 == 0:
                    k = j // 4
                    pe.wait_ge(a["xT_done"], upto(0, b + 1))
                    pe.wait_ge(a["qk_done"], upto(0, b))
                    pe.wait_ge(a["v_done"], upto(0, b))
                    pe.matmul(bank[:, 0, 0:128], waT[:, 0], xcT[:, k, 0], start=True, stop=True)
                    pe.matmul(bank[:, 0, 128:256], waT[:, 1], xcT[:, k, 1], start=True, stop=True)
                    pe.matmul(bank[:, 1, 0:128], xcT[:, k, 1], waT[:, 2], start=True, stop=True)\
                      .then_inc(a["proj"], 1)

            def a_scores(u, b, j):
                pe.wait_ge(a["km_done"], upto(0, u + 1))
                pe.wait_ge(a["qk_done"], upto(0, b + 1))
                pe.wait_ge(a["sub_done"], upto(0, u - 1))
                pe.matmul(bank[:, 3 + j % 2, :], a_q[:, j // 4], a_km[:, j % 2].rearrange("p h n -> p (h n)"),
                          start=True, stop=True).then_inc(a["s_done"], 1)

            def a_pv(u, b, j):
                pe.wait_ge(a["probT_done"], upto(0, u + 1))
                pe.wait_ge(a["v_done"], upto(0, b + 1))
                pe.wait_ge(a["o_done"], upto(0, u))
                for h in range(4):
                    w = A_DIM + 1
                    ins = pe.matmul(bank[:, 6, h * w:(h + 1) * w], probT[:, j % 2, h * 128:(h + 1) * 128],
                                    a_v[:, j // 4, j % 4 * 4 + h, :], start=True, stop=True)
                ins.then_inc(a["pv_done"], 1)

            def a_output(u, b, j):
                if j % 4 == 3:
                    k = j // 4
                    pe.wait_ge(a["o_done"], upto(0, u + 1))
                    pe.wait_ge(a["res_done"], upto(0, b))
                    pe.transpose(bank[:, 7, 0:128], a_o[:, k], ident).then_inc(a["o_turned"], 1)
                    pe.wait_ge(a["oT_done"], upto(0, b + 1))
                    pe.matmul(bank[:, 7, 128:256], a_oT[:, k], waT[:, 3], start=True, stop=True)\
                      .then_inc(a["out_done"], 1)

            drive(pe, [(4, a_scores), (6, lambda u, b, j: turn(a, 0, u, j)), (2, a_turn_x), (7, a_output),
                       (6, a_pv), (2, a_project)], UNITS, UNROLL, 4)

            def m_turn(u, b, j):
                pe.wait_ge(m["n_done"], upto(0, b + 1))
                pe.wait_ge(m["xT_done"], upto(0, b))
                pe.transpose(bank[:, 2, 0:128], n1[:, j], ident).then_inc(m["turned"], 1)

            def m_logits(u, b, j):
                pe.wait_ge(m["xT_done"], upto(0, b + 1))
                pe.wait_ge(m["shifted"], upto(0, b))
                pe.matmul(bank[:, 0, 0:EXPERTS], m_xT[:, j], rwT[:], start=True, stop=True).then_inc(m["logits"], 1)

            def m_experts(u, b, j):
                pe.wait_ge(m["xT_done"], upto(0, b + 1))
                pe.wait_ge(m["prod_done"], upto(0, b))
                for q in range(4):
                    ins = pe.matmul(bank[:, 3 + q, :], m_xT[:, j],
                                    ew[:, 4 * q:4 * q + 4, :].rearrange("p e n -> p (e n)"), start=True, stop=True)
                ins.then_inc(m["experts"], 1)

            drive(pe, [(1, m_turn), (1, m_logits), (1, m_experts)], B, 2, 1)

            pe.wait_ge(ld_c, 16 * 10)

            def c_turn_x(u, b, j):
                if j % 4 == 0:
                    k = j // 4
                    pe.wait_ge(c["n_done"], upto(0, b + 1))
                    pe.wait_ge(c["kvT_done"], upto(0, b))
                    pe.transpose(bank[:, 2, 0:128], nx[:, k], ident)
                    pe.transpose(bank[:, 2, 128:256], n2[:, k], ident).then_inc(c["x_turned"], 1)

            def c_values(u, b, j):
                tile = j % 4
                if tile < 2:
                    pe.wait_ge(c["kvT_done"], upto(0, b + 1))
                    pe.wait_ge(c["v_done"], upto(0, b * 2 + tile))
                    pe.matmul(bank[:, 1, :], c_kvT[:, j // 4, tile], c_wkv[:, C_INNER:], start=True, stop=True)\
                      .then_inc(c["v_proj"], 1)

            def c_project(u, b, j):
                k, p = j // 4, j % 4
                w = slice(128 * p, 128 * p + 128)
                pe.wait_ge(c["kvT_done"], upto(0, b + 1))
                pe.wait_ge(c["evac_done"], upto(0, u))
                both = c_kvT[:, k].rearrange("p t n -> p (t n)")
                pe.matmul(bank[:, 0, 0:128], c_wq[:, w], c_kvT[:, k, 1], start=True, stop=True)
                pe.matmul(bank[:, 0, 128:384], c_wkv[:, w], both, start=True, stop=True)
                pe.matmul(bank[:, 0, 384:512], c_wks[:, w], c_kvT[:, k, 0], start=True, stop=True)\
                  .then_inc(c["qk_proj"], 1)

            def c_scores(u, b, j):
                pe.wait_ge(c["evac_done"], upto(0, u + 1))
                pe.wait_ge(c["rope_done"], upto(0, u + 1))
                pe.wait_ge(c["sub_done"], upto(0, u))
                for h in range(2):
                    r = slice(64 * h, 64 * h + 64)
                    ins = pe.matmul(bank[:, 3 + h, 0:256], c_q[r, j % 2], c_k[r, j % 2], start=True, stop=True)
                ins.then_inc(c["s_done"], 1)

            def c_pv(u, b, j):
                pe.wait_ge(c["probT_done"], upto(0, u + 1))
                pe.wait_ge(c["v_done"], upto(0, b * 2 + 2))
                pe.wait_ge(c["o_done"], upto(0, u))
                w = C_DIM + 1
                for h in range(2):
                    for tile in range(2):
                        n = h * 2 + tile
                        ins = pe.matmul(bank[:, 6, h * w:(h + 1) * w], probT[:, j % 2, n * 128:(n + 1) * 128],
                                        c_v[:, j // 4, tile, 2 * (j % 4) + h, :], start=tile == 0, stop=tile == 1)
                ins.then_inc(c["pv_done"], 1)

            def c_output(u, b, j):
                k = j // 4
                pe.wait_ge(c["o_done"], upto(0, u + 1))
                pe.wait_ge(c["oT_done"], upto(0, u))
                pe.wait_ge(c["res_done"], upto(0, b))
                pe.transpose(bank[:, 7, 0:128], o[:, j % 2, 0:128], ident).then_inc(c["o_turned"], 1)
                if j % 4 == 3:
                    pe.wait_ge(c["oT_done"], upto(0, u + 1))
                    for p in range(4):
                        ins = pe.matmul(bank[:, 7, 128:256], c_oT[:, k, p], c_wo[:, p], start=p == 0, stop=p == 3)
                    ins.then_inc(c["out_done"], 1)

            drive(pe, [(3, c_project), (3, c_values), (6, lambda u, b, j: turn(c, 0, u, j)), (4, c_scores),
                       (7, c_output), (6, c_pv), (2, c_turn_x)], UNITS, UNROLL, 4)

            def attention(ly):
                ub, bb = ly * UNITS, ly * B

                def l_turn_x(u, b, j):
                    if j % 4 == 0:
                        pe.wait_ge(l["xin_done"], upto(bb, b + 1))
                        pe.wait_ge(l["oT_done"], upto(ub, u - 5))
                        pe.wait_ge(l["res_done"], upto(bb, b - 2))
                        pe.wait_ge(l["xs_done"], upto(bb * 2, b * 2))
                        pe.transpose(bank[:, 7, 384:512], xin[:, j // 4], ident).then_inc(l["x_turned"], 1)

                def l_project(u, b, j):
                    g = j % 4
                    w = l_w[:].rearrange("p (t n) -> p t n", t=3)
                    pe.wait_ge(l["xs_done"], upto(bb * 2, b * 2 + 2))
                    pe.wait_ge(l["rot_done"], upto(ub, u))
                    pe.matmul(bank[:, 0, :].rearrange("p (q n) -> p q n", q=2), xsT[:, j // 4],
                              w[:, 0:2, 256 * g:256 * g + 256], start=True, stop=True).then_inc(l["qk_proj"], 1)
                    pe.wait_ge(l["v_done"], upto(ub, u))
                    pe.matmul(bank[:, 1, 0:256], xsT[:, j // 4], w[:, 2, 256 * g:256 * g + 256],
                              start=True, stop=True).then_inc(l["v_proj"], 1)

                def l_turn_qk(u, b, j):
                    pe.wait_ge(l["qk_done"], upto(ub, u + 1))
                    pe.wait_ge(l["qkT_done"], upto(ub, u))
                    for n in range(4):
                        ins = pe.transpose(bank[:, 2, n * 128:(n + 1) * 128],
                                           l_qk[:, j % 2, n * 128:(n + 1) * 128], ident)
                    ins.then_inc(l["qk_turned"], 1)

                def l_scores(u, b, j):
                    pe.wait_ge(l["qkT_done"], upto(ub, u + 1))
                    pe.wait_ge(l["sub_done"], upto(ub, u))
                    for r in range(2):
                        pe.matmul(bank[:, 3 + r, 0:256], ident_bf, mask_bf, start=True, stop=False,
                                  skip_group_check=True)
                    for p in range(2):
                        for r in range(2):
                            rows = slice(64 * r, 64 * r + 64)
                            ins = pe.matmul(bank[:, 3 + r, 128 * p:128 * p + 128],
                                            l_qkT[rows, j % 2, 128 * p:128 * p + 128],
                                            l_qkT[rows, j % 2, 256 + 128 * p:384 + 128 * p],
                                            start=False, stop=True, skip_group_check=True)
                    ins.then_inc(l["s_done"], 1)

                def l_pv(u, b, j):
                    pe.wait_ge(l["probT_done"], upto(ub, u + 1))
                    pe.wait_ge(l["v_done"], upto(ub, u + 1))
                    pe.wait_ge(l["o_done"], upto(ub, u))
                    w = L_DIM + 1
                    for h in range(4):
                        n = h % 2 * 2 + h // 2
                        ins = pe.matmul(bank[:, 6, h * w:(h + 1) * w], probT[:, j % 2, n * 128:(n + 1) * 128],
                                        l_v[:, j, h, :], start=True, stop=True)
                    ins.then_inc(l["pv_done"], 1)

                def l_turn_o(u, b, j):
                    r = j % 4
                    pe.wait_ge(l["o_done"], upto(ub, u + 1))
                    pe.wait_ge(l["oT_done"], upto(ub, u))
                    pe.wait_ge(l["res_done"], upto(bb, b))
                    turned = b + (r + 5) // 4 + 1
                    if isinstance(turned, int):
                        turned = min(turned, B)
                    pe.wait_ge(l["xs_done"], upto(bb * 2, turned * 2))
                    for p in range(2):
                        ins = pe.transpose(bank[:, 7, p * 128:(p + 1) * 128], o[:, j % 2, p * 128:(p + 1) * 128],
                                           ident)
                    ins.then_inc(l["o_turned"], 1)

                def l_output(u, b, j):
                    if j % 4 == 3:
                        pe.wait_ge(l["oT_done"], upto(ub, u + 1))
                        turned = b + 3
                        if isinstance(turned, int):
                            turned = min(turned, B)
                        pe.wait_ge(l["xs_done"], upto(bb * 2, turned * 2))
                        for p in range(8):
                            ins = pe.matmul(bank[:, 7, 256:384], l_oT[:, j // 4, p], l_wo[:, p],
                                            start=p == 0, stop=p == 7)
                        ins.then_inc(l["out_done"], 1)

                return Pipeline(pe, [(5, lambda u, b, j: turn(l, ub, u, j)), (4, l_scores), (3, l_turn_qk), (6, l_turn_o),
                           (5, l_pv), (6, l_output), (0, l_turn_x), (1, l_project)],
                                UNITS, UNROLL, 4)

            def feed_forward(ly, last):
                fb, ub = ly * 4, ly * UNITS

                def f_shift(g):
                    v = bank[:, 1, :].rearrange("p (a n) -> p a n", a=4)
                    yg = Y[:, 4 * g:4 * g + 4, :]
                    pe.wait_ge(l["res_done"], upto(0, ly * B + 4 * g + 4))
                    if g == 0:
                        pe.wait_ge(l["v_done"], upto(ub, UNITS))
                    else:
                        pe.wait_ge(f["n_done"], upto(0, fb + g))
                    pe.matmul(v[:, :, 0:HALF], ident, yg[:, :, 0:HALF], start=True, stop=True)
                    pe.matmul(v[:, :, HALF:], shift_t, yg[:, :, HALF:], start=True, stop=True).then_inc(f["xs"], 1)

                def f_turn(g):
                    pe.wait_ge(f["n_done"], upto(0, fb + g + 1))
                    if g == 0:
                        pe.wait_ge(l["qkT_done"], upto(ub, UNITS))
                    pe.wait_ge(f["nT_done"], upto(0, fb + g))
                    for n in range(4):
                        ins = pe.transpose(bank[:, 2, n * 128:(n + 1) * 128], f_n[:, n], ident)
                    ins.then_inc(f["turned"], 1)

                def f_hidden(g, k):
                    c0, n = CHUNKS[k]
                    i = len(CHUNKS) * g + k
                    pe.wait_ge(f["nT_done"], upto(0, fb + g + 1))
                    pe.wait_ge(f["h_done"], upto(ly * 12, i - 1))
                    if i == 0:
                        pe.wait_ge(l["sub_done"], upto(ub, UNITS))
                    if i == 1:
                        pe.wait_ge(l["probT_done"], upto(ub, UNITS))
                        pe.wait_ge(l["o_done"], upto(ub, UNITS))
                    at = 3 + i % 2 * 2
                    pe.matmul(bank[0:n, at, :], f_w1[:, FF + c0:FF + c0 + n], f_nT[:, g % 2], start=True, stop=True)
                    pe.matmul(bank[0:n, at + 1, :], f_w1[:, c0:c0 + n], f_nT[:, g % 2], start=True, stop=True)\
                      .then_inc(f["hidden"], 1)

                def f_out(g):
                    pe.wait_ge(f["h_done"], upto(0, ly * 12 + 3 * g + 3))
                    if g == 0:
                        pe.wait_ge(l["res_done"], upto(0, (ly + 1) * B))
                    pe.wait_ge(f["y_done"], upto(0, fb + g))
                    if g > 1 and not last:
                        pe.wait_ge(l["xs_done"], upto((ly + 1) * B * 2, 2))
                    for q in range(4):
                        for k, (c0, n) in enumerate(CHUNKS):
                            ins = pe.matmul(bank[:, 7, q * 128:(q + 1) * 128], f_h[0:n, g % 2, k, q * 128:(q + 1) * 128],
                                            f_w2[0:n, k, :], start=k == 0, stop=k == len(CHUNKS) - 1)
                    ins.then_inc(f["out_mm"], 1)

                return f_shift, f_turn, f_hidden, f_out

            def rest_of_layer(ly, att, nxt):
                shift, turn_n, hidden, output = feed_forward(ly, nxt is None)
                att.steady()
                att.finish(0, 1)
                shift(0)
                att.finish(2, 3)
                pe.wait_ge(ld_fw, (ly + 1) * (16 * FW_DMAS))
                turn_n(0)
                shift(1)
                att.finish(4)
                hidden(0, 0)
                att.finish(5, 6)
                for g in range(4):
                    if g > 0:
                        hidden(g, 0)
                        output(g - 1)
                    if g == 3 and nxt is not None:
                        pe.wait_ge(ld_lw, (ly + 2) * 32)
                        nxt.start(1)
                    hidden(g, 1)
                    if g == 3 and nxt is not None:
                        nxt.start(2)
                    hidden(g, 2)
                    if g < 3:
                        turn_n(g + 1)
                    if g < 2:
                        shift(g + 2)
                    if g == 2 and nxt is not None:
                        pe.wait_ge(f["y_done"], upto(0, ly * 4 + 2))
                        nxt.start(0)
                if nxt is not None:
                    nxt.start(3)
                output(3)
                if nxt is not None:
                    pe.wait_ge(f["y_done"], upto(0, ly * 4 + 4))
                    nxt.start(4, 5, 6, 7)

            pe.wait_ge(ld_lw, 32)
            attention(0).start(*range(UNROLL))
            with pe.Fori(0, LAYERS - 1) as ly:
                rest_of_layer(ly, attention(ly), attention(ly + 1))
            rest_of_layer(LAYERS - 1, attention(LAYERS - 1), None)

        @block.scalar
        def _(act):
            def exp(s, base, u, j, scale):
                act.wait_ge(s["sub_done"], upto(base, u + 1))
                act.wait_ge(s["turned"], upto(base, u - 1))
                act.activation(prob[:, j % 2, :], sm[:, j % 2, :], ACT.Exp, scale=scale).then_inc(s["exp_done"], 1)

            def copy_prob(s, base, u, j):
                act.wait_ge(s["turned"], upto(base, u + 1))
                act.wait_ge(s["pv_done"], upto(base, u - 1))
                act.activation(probT[:, j % 2, :], bank[:, 5, :], ACT.Copy).then_inc(s["probT_done"], 1)

            for s in stage_all:
                act.sem_inc(s, CREDIT)
            act.wait_ge(w_turned, 1)
            act.activation(waT[:].rearrange("p a n -> p (a n)"), bank[:, 2, :], ACT.Copy)
            act.activation(rwT[:], bank[:, 1, 0:EXPERTS], ACT.Copy).then_inc(w_copied, 1)

            def a_copy_x(u, b, j):
                if j % 4 == 0:
                    act.wait_ge(a["x_turned"], upto(0, b + 1))
                    act.wait_ge(a["proj"], upto(0, b - 1))
                    act.activation(xcT[:, j // 4].rearrange("p a n -> p (a n)"), bank[:, 2, 0:256], ACT.Copy)\
                       .then_inc(a["xT_done"], 1)

            def a_copy_qk(u, b, j):
                if j % 4 == 0:
                    k = j // 4
                    act.wait_ge(a["proj"], upto(0, b + 1))
                    act.wait_ge(a["s_done"], upto(0, u - 4))
                    act.wait_ge(a["km_done"], upto(0, u - 4))
                    act.activation(a_q[:, k], bank[:, 0, 0:128], ACT.Identity, bias=a_bq[:])
                    act.activation(a_k[:, k], bank[:, 0, 128:256], ACT.Identity, bias=a_bk[:])\
                       .then_inc(a["qk_done"], 1)

            def a_copy_o(u, b, j):
                if j % 4 == 3:
                    act.wait_ge(a["o_turned"], upto(0, b + 1))
                    act.wait_ge(a["out_done"], upto(0, b))
                    act.activation(a_oT[:, j // 4], bank[:, 7, 0:128], ACT.Copy).then_inc(a["oT_done"], 1)

            act.wait_ge(ld_a, 16 * 8)
            drive(act, [(6, lambda u, b, j: copy_prob(a, 0, u, j)), (2, a_copy_x), (7, a_copy_o),
                        (2, a_copy_qk), (4, lambda u, b, j: exp(a, 0, u, j, A_DIM ** -0.5))], UNITS, UNROLL, 4)

            def m_copy_x(u, b, j):
                act.wait_ge(m["turned"], upto(0, b + 1))
                act.wait_ge(m["experts"], upto(0, b - 1))
                act.activation(m_xT[:, j], bank[:, 2, 0:128], ACT.Copy).then_inc(m["xT_done"], 1)

            def m_exp(u, b, j):
                act.wait_ge(m["shifted"], upto(0, b + 1))
                act.wait_ge(m["gate_done"], upto(0, b - 1))
                act.activation(m_e[:, j], m_lg[:, j], ACT.Exp, accum_out=m_es[:, j]).then_inc(m["exp_done"], 1)

            drive(act, [(1, m_copy_x), (1, m_exp)], B, 2, 1)

            act.wait_ge(ld_c, 16 * 10)

            def c_copy_x(u, b, j):
                if j % 4 == 0:
                    k = j // 4
                    act.wait_ge(c["x_turned"], upto(0, b + 1))
                    act.wait_ge(c["qk_proj"], upto(0, u - 4))
                    act.wait_ge(c["v_proj"], upto(0, b * 2 - 2))
                    for tile in range(2):
                        ins = act.activation(c_kvT[:, k, tile], bank[:, 2, tile * 128:(tile + 1) * 128], ACT.Identity,
                                             bias=c_g[:, 2 * tile + 1:2 * tile + 2],
                                             scale=c_g[:, 2 * tile:2 * tile + 1])
                    ins.then_inc(c["kvT_done"], 1)

            def c_copy_v(u, b, j):
                tile = j % 4
                if tile < 2:
                    act.wait_ge(c["v_proj"], upto(0, b * 2 + tile + 1))
                    act.wait_ge(c["pv_done"], upto(0, u - tile - 4))
                    act.activation(c_v[:, j // 4, tile, :, 0:C_DIM],
                                   bank[:, 1, :].rearrange("p (h n) -> p h n", n=C_DIM), ACT.Copy)\
                       .then_inc(c["v_done"], 1)

            def c_copy_qk(u, b, j):
                act.wait_ge(c["qk_proj"], upto(0, u + 1))
                act.wait_ge(c["rot_done"], upto(0, u + 1))
                act.wait_ge(c["s_done"], upto(0, u - 1))
                act.activation(c_q[:, j % 2], bank[:, 0, 0:128], ACT.Copy, scale=C_DIM ** -0.5)
                act.activation(c_k[:, j % 2, 128:256], bank[:, 0, 256:384], ACT.Copy).then_inc(c["evac_done"], 1)

            def c_copy_o(u, b, j):
                act.wait_ge(c["o_turned"], upto(0, u + 1))
                act.wait_ge(c["out_done"], upto(0, b))
                act.activation(c_oT[:, j // 4, j % 4], bank[:, 7, 0:128], ACT.Copy).then_inc(c["oT_done"], 1)

            drive(act, [(3, c_copy_qk), (3, c_copy_v), (6, lambda u, b, j: copy_prob(c, 0, u, j)), (7, c_copy_o),
                        (2, c_copy_x), (4, lambda u, b, j: exp(c, 0, u, j, 1.0))], UNITS, UNROLL, 4)

            def attention(ly):
                ub, bb = ly * UNITS, ly * B

                def l_copy_x(u, b, j):
                    if j % 4 == 0:
                        k = j // 4
                        act.wait_ge(l["x_turned"], upto(bb, b + 1))
                        act.wait_ge(l["v_proj"], upto(ub, u - 4))
                        act.activation(xsT[0:HALF, k], bank[0:HALF, 7, 384:512], ACT.Copy).then_inc(l["xs_done"], 1)
                        act.activation(xsT[HALF:, k, 1:], bank[HALF:, 7, 384:511], ACT.Copy).then_inc(l["xs_done"], 1)

                def l_copy_v(u, b, j):
                    act.wait_ge(l["v_proj"], upto(ub, u + 1))
                    act.wait_ge(l["pv_done"], upto(ub, u - 7))
                    act.activation(l_v[:, j, :, 0:L_DIM],
                                   bank[:, 1, 0:256].rearrange("p (h n) -> p h n", n=L_DIM), ACT.Copy)\
                       .then_inc(l["v_done"], 1)

                def l_square(u, b, j):
                    act.wait_ge(l["qk_proj"], upto(ub, u + 1))
                    act.wait_ge(l["ss_done"], upto(ub, u))
                    act.activation(l_sq[:], bank[:, 0, :], ACT.Square).then_inc(l["sq_done"], 1)

                def l_copy_qk(u, b, j):
                    act.wait_ge(l["qk_turned"], upto(ub, u + 1))
                    act.wait_ge(l["s_done"], upto(ub, u - 1))
                    act.activation(l_qkT[:, j % 2], bank[:, 2, :], ACT.Copy).then_inc(l["qkT_done"], 1)

                def l_copy_o(u, b, j):
                    g = j % 4
                    act.wait_ge(l["o_turned"], upto(ub, u + 1))
                    act.wait_ge(l["out_done"], upto(bb, b))
                    act.activation(l_oT[:, j // 4, 2 * g:2 * g + 2].rearrange("p a n -> p (a n)"),
                                   bank[:, 7, 0:256], ACT.Copy).then_inc(l["oT_done"], 1)

                return Pipeline(act, [(5, lambda u, b, j: copy_prob(l, ub, u, j)), (3, l_copy_qk), (6, l_copy_o),
                                 (4, lambda u, b, j: exp(l, ub, u, j, QK_SCALE)), (0, l_copy_x),
                                 (1, l_square), (1, l_copy_v)], UNITS, UNROLL, 4)

            def feed_forward(ly):
                fb = ly * 4

                def f_copy_n(g):
                    act.wait_ge(f["turned"], upto(0, fb + g + 1))
                    act.wait_ge(f["hidden"], upto(ly * 12, 3 * (g - 1)))
                    act.activation(f_nT[:, g % 2], bank[:, 2, :], ACT.Identity, bias=f_g[:, 1:2],
                                   scale=f_g[:, 0:1]).then_inc(f["nT_done"], 1)

                def f_gelu(g, k):
                    n = CHUNKS[k][1]
                    i = len(CHUNKS) * g + k
                    act.wait_ge(f["hidden"], upto(0, ly * 12 + i + 1))
                    act.wait_ge(f["h_done"], upto(ly * 12, i - 1))
                    act.activation(f_ge[0:n, i % 2], bank[0:n, 3 + i % 2 * 2, :], ACT.Gelu,
                                   bias=f_b1[0:n, 1, k:k + 1]).then_inc(f["gelu_done"], 1)

                return f_copy_n, f_gelu

            def rest_of_layer(ly, att, nxt):
                copy_n, gelu = feed_forward(ly)
                att.steady()
                att.finish(0, 1, 2, 3)
                act.wait_ge(ld_fw, (ly + 1) * (16 * FW_DMAS))
                copy_n(0)
                att.finish(4)
                gelu(0, 0)
                att.finish(5, 6)
                for g in range(4):
                    if g > 0:
                        gelu(g, 0)
                    if g == 3 and nxt is not None:
                        nxt.start(1)
                    gelu(g, 1)
                    if g == 3 and nxt is not None:
                        nxt.start(2)
                    gelu(g, 2)
                    if g < 3:
                        copy_n(g + 1)
                    if g == 2 and nxt is not None:
                        nxt.start(0)
                if nxt is not None:
                    nxt.start(3, 4, 5, 6, 7)

            attention(0).start(*range(UNROLL))
            with act.Fori(0, LAYERS - 1) as ly:
                rest_of_layer(ly, attention(ly), attention(ly + 1))
            rest_of_layer(LAYERS - 1, attention(LAYERS - 1), None)

        @block.vector
        def _(dve):
            def normalise(dst, src, k, done):
                dve.tensor_scalar(dst, src, ln_mv[:, k, 0:1], ln_rs[:, k:k + 1], ALU.subtract, ALU.mult)\
                   .then_inc(done, 1)

            def shift_scores(s, base, u, j, scores, blocks):
                k, (_, p, q, w) = j % 2, scores.shape
                dve.wait_ge(s["s_done"], upto(base, u + 1))
                dve.tensor_reduce(peak[:, k, 0:blocks], scores, AX.X, ALU.max).then_inc(s["peaked"], 1)
                dve.wait_ge(s["exp_done"], upto(base, u - 1))
                dve.wait_ge(s["peaked"], upto(base, u + 1))
                peaks = peak[:, k, 0:blocks].rearrange("p (a b) -> p a b", a=p)[:, :, :, None]
                dve.tensor_tensor(sm[:, k].rearrange("p (a b n) -> p a b n", a=p, b=q), scores,
                                  peaks.broadcast_to([128, p, q, w]), ALU.subtract).then_inc(s["sub_done"], 1)

            def divide(s, base, u, j, heads, width, dst):
                ov = bank[:, 6, 0:heads * (width + 1)].rearrange("p (h n) -> p h n", h=heads)
                dve.wait_ge(s["pv_done"], upto(base, u + 1))
                dve.reciprocal(rsum[:, j % 2, 0:heads], ov[:, :, width]).then_inc(s["rsum_done"], 1)
                dve.wait_ge(s["rsum_done"], upto(base, u + 1))
                dve.tensor_tensor(dst, ov[:, :, 0:width], rsum[:, j % 2, 0:heads, None]
                                  .broadcast_to([128, heads, width]), ALU.mult).then_inc(s["o_done"], 1)

            dve.wait_ge(ld_x, 16)
            dve.wait_ge(ld_ctx, 16)
            dve.wait_ge(ld_a, 16 * 8)
            dve.wait_ge(preset, 1)

            def a_stats(u, b, j):
                if j % 4 == 0:
                    dve.wait_ge(a["x_turned"], upto(0, b - 1))
                    dve.tensor_scalar(nx[:, j // 4], one(CTX, b), 1.0, None, ALU.mult)
                    dve.bn_stats(ln_st[:, 0], one(X, b)).then_inc(a["stats"], 1)
                    dve.wait_ge(a["stats"], upto(0, b + 1))
                    apart(dve)
                    dve.bn_aggr(ln_mv[:, 0], ln_st[:, 0]).then_inc(a["ln_stat"], 1)

            def a_norm(u, b, j):
                if j % 4 == 0:
                    dve.wait_ge(a["ln_rstd"], upto(0, b + 1))
                    normalise(n1[:, j // 4], one(X, b), 0, a["n_done"])

            def a_values(u, b, j):
                if j % 4 == 0:
                    dve.wait_ge(a["proj"], upto(0, b + 1))
                    dve.wait_ge(a["pv_done"], upto(0, u - 4))
                    dve.tensor_tensor(a_v[:, j // 4, :, 0:A_DIM],
                                      bank[:, 1, 0:128].rearrange("p (h n) -> p h n", n=A_DIM),
                                      a_bv[:].rearrange("p (h n) -> p h n", n=A_DIM), ALU.add).then_inc(a["v_done"], 1)

            def a_shift(u, b, j):
                shift_scores(a, 0, u, j, bank[:, 3 + j % 2, :].rearrange("p (a b n) -> p a b n", a=1, b=4), 4)

            def a_divide(u, b, j):
                g = j % 4
                if g == 0:
                    dve.wait_ge(a["o_turned"], upto(0, b - 1))
                divide(a, 0, u, j, 4, A_DIM,
                       a_o[:, j // 4, 32 * g:32 * g + 32].rearrange("p (h n) -> p h n", n=A_DIM))

            def a_residual(u, b, j):
                if j % 4 == 3:
                    k = j // 4
                    dve.wait_ge(a["out_done"], upto(0, b + 1))
                    dve.tensor_tensor(a_y[:, k], bank[:, 7, 128:256], a_bo[:], ALU.add).then_inc(a["biased"], 1)
                    dve.wait_ge(a["biased"], upto(0, b + 1))
                    dve.tensor_tensor(one(X, b), one(X, b), a_y[:, k], ALU.add).then_inc(a["res_done"], 1)

            drive(dve, [(0, a_stats), (4, a_shift), (6, a_divide), (1, a_norm), (2, a_values), (8, a_residual)],
                  UNITS, UNROLL, 4)

            dve.wait_ge(a["res_done"], upto(0, B))
            dve.wait_ge(ld_m, 48)

            def m_stats(u, b, j):
                dve.bn_stats(ln_st[:, j], one(X, b)).then_inc(m["stats"], 1)
                dve.wait_ge(m["stats"], upto(0, b + 1))
                apart(dve)
                dve.bn_aggr(ln_mv[:, j], ln_st[:, j]).then_inc(m["ln_stat"], 1)

            def m_norm(u, b, j):
                dve.wait_ge(m["ln_rstd"], upto(0, b + 1))
                normalise(n1[:, j], one(X, b), j, m["n_done"])

            def m_shift(u, b, j):
                n = b * 2
                dve.wait_ge(m["logits"], upto(0, b + 1))
                dve.tensor_tensor(m_lg[:, j], bank[:, 0, 0:EXPERTS], rb[:], ALU.add).then_inc(m["lg_chain"], 1)
                dve.wait_ge(m["lg_chain"], upto(0, n + 1))
                apart(dve)
                dve.max(m_top[:], m_lg[:, j]).then_inc(m["lg_chain"], 1)
                dve.wait_ge(m["lg_chain"], upto(0, n + 2))
                dve.tensor_scalar(m_lg[:, j], m_lg[:, j], m_top[:, 0:1], None, ALU.subtract).then_inc(m["shifted"], 1)

            def m_gates(u, b, j):
                steps = 10
                n = [b * steps]

                def link(ins):
                    ins.then_inc(m["g_chain"], 1)
                    n[0] = n[0] + 1
                    dve.wait_ge(m["g_chain"], upto(0, n[0]))
                    apart(dve)

                dve.wait_ge(m["exp_done"], upto(0, b + 1))
                link(dve.reciprocal(m_s[:, 0:1], m_es[:, j]))
                link(dve.tensor_scalar(m_p[:, 0:EXPERTS], m_e[:, j], m_s[:, 0:1], None, ALU.mult))
                link(dve.max(m_top[:], m_p[:, 0:EXPERTS]))
                link(dve.memset(m_top[:, TOP_K:], -1.0))
                link(dve.match_replace(m_rep[:], m_top[:], m_p[:], 0.0))
                link(dve.scalar_tensor_tensor(m_sel[:], m_p[:, 0:EXPERTS], 1.0, m_rep[:, 0:EXPERTS], ALU.mult,
                                              ALU.subtract, accum_out=m_s[:, 1:2]))
                link(dve.tensor_scalar(m_s[:, 2:3], m_s[:, 1:2], MOE_EPS, None, ALU.add))
                link(dve.reciprocal(m_s[:, 3:4], m_s[:, 2:3]))
                link(dve.tensor_scalar(m_gate[:], m_sel[:], m_s[:, 3:4], 0.0, ALU.mult, ALU.add,
                                       accum_out=m_s[:, 4:5]))
                link(dve.tensor_scalar(m_s[:, 5:6], m_s[:, 4:5], MOE_EPS, None, ALU.max))
                dve.tensor_scalar(m_eps[:], m_s[:, 4:5], MOE_EPS, None, ALU.mult)
                dve.reciprocal(m_s[:, 6:7], m_s[:, 5:6]).then_inc(m["gate_done"], 1)

            def m_combine(u, b, j):
                dve.wait_ge(m["gate_done"], upto(0, b + 1))
                dve.wait_ge(m["experts"], upto(0, b + 1))
                for q in range(4):
                    ins = dve.tensor_tensor(m_prod[:, 4 * q:4 * q + 4, :],
                                            bank[:, 3 + q, :].rearrange("p (e n) -> p e n", e=4),
                                            m_gate[:, 4 * q:4 * q + 4, None].broadcast_to([128, 4, D]), ALU.mult)
                ins.then_inc(m["prod_done"], 1)
                dve.wait_ge(m["prod_done"], upto(0, b + 1))
                dve.tensor_reduce(m_acc[:], m_prod[:].rearrange("p e n -> p n e"), AX.X, ALU.add)\
                   .then_inc(m["reduced"], 1)
                dve.wait_ge(m["reduced"], upto(0, b * 2 + 1))
                dve.tensor_scalar(m_acc[:], m_acc[:], m_s[:, 6:7], m_eps[:], ALU.mult, ALU.add)\
                   .then_inc(m["reduced"], 1)
                dve.wait_ge(m["reduced"], upto(0, b * 2 + 2))
                dve.tensor_tensor(one(X, b), one(X, b), m_acc[:], ALU.add).then_inc(m["res_done"], 1)

            drive(dve, [(2, m_gates), (0, m_stats), (1, m_norm), (2, m_combine), (1, m_shift)], B, 2, 1)

            dve.wait_ge(m["res_done"], upto(0, B))
            dve.wait_ge(ld_const, 16)

            def c_stats(u, b, j):
                if j % 4 == 0:
                    dve.bn_stats(ln_st[:, 0], one(X, b))
                    dve.bn_stats(ln_st[:, 1], one(CTX, b)).then_inc(c["stats"], 1)
                    dve.wait_ge(c["stats"], upto(0, b + 1))
                    apart(dve)
                    dve.bn_aggr(ln_mv[:, 0], ln_st[:, 0])
                    dve.bn_aggr(ln_mv[:, 1], ln_st[:, 1]).then_inc(c["ln_stat"], 1)

            def c_norm(u, b, j):
                if j % 4 == 0:
                    k = j // 4
                    dve.wait_ge(c["x_turned"], upto(0, b - 1))
                    dve.wait_ge(c["ln_rstd"], upto(0, b + 1))
                    dve.tensor_scalar(nx[:, k], one(CTX, b), ln_mv[:, 1, 0:1], ln_rs[:, 1:2], ALU.subtract,
                                      ALU.mult)
                    normalise(n1[:, k], one(X, b), 0, c["n1_done"])
                    dve.wait_ge(c["n1_done"], upto(0, b + 1))
                    dve.bn_stats(ln_st[:, 2], n1[:, k]).then_inc(c["stats2"], 1)
                    dve.wait_ge(c["stats2"], upto(0, b + 1))
                    apart(dve)
                    dve.bn_aggr(ln_mv[:, 2], ln_st[:, 2]).then_inc(c["ln_stat2"], 1)

            def c_norm2(u, b, j):
                if j % 4 == 0:
                    dve.wait_ge(c["ln_rstd2"], upto(0, b + 1))
                    normalise(n2[:, j // 4], n1[:, j // 4], 2, c["n_done"])

            def c_rotate(u, b, j):
                k = j % 2
                dve.wait_ge(c["qk_proj"], upto(0, u + 1))
                dve.tensor_tensor(c_r[:, k, 0], bank[:, 0, 128:256], cos_t, ALU.mult)
                dve.tensor_tensor(c_r[:, k, 1], bank[:, 0, 384:512], sin_t, ALU.mult).then_inc(c["rot_done"], 1)
                dve.wait_ge(c["rot_done"], upto(0, u + 1))
                dve.wait_ge(c["s_done"], upto(0, u - 1))
                dve.tensor_tensor(c_k[:, k, 0:128], c_r[:, k, 0], c_r[:, k, 1], ALU.add).then_inc(c["rope_done"], 1)

            def c_shift(u, b, j):
                shift_scores(c, 0, u, j, bank[:, 3:5, 0:256].rearrange("p a (b n) -> p a b n", b=1), 2)

            def c_divide(u, b, j):
                dve.wait_ge(c["o_turned"], upto(0, u - 1))
                divide(c, 0, u, j, 2, C_DIM, o[:, j % 2, 0:128].rearrange("p (h n) -> p h n", n=C_DIM))

            def c_residual(u, b, j):
                if j % 4 == 3:
                    k = j // 4
                    dve.wait_ge(c["out_done"], upto(0, b + 1))
                    dve.tensor_tensor(one(X, b), one(X, b), bank[:, 7, 128:256], ALU.add).then_inc(c["res_done"], 1)
                    dve.wait_ge(c["res_done"], upto(0, b + 1))
                    dve.tensor_scalar(c_x[:, k], one(X, b), 1.0, None, ALU.mult).then_inc(c["y_copied"], 1)
                    dve.wait_ge(c["y_copied"], upto(0, b + 1))
                    dve.bn_stats(ln_st[:, 3], c_x[:, k]).then_inc(c["y_stats"], 1)
                    dve.wait_ge(c["y_stats"], upto(0, b + 1))
                    apart(dve)
                    dve.bn_aggr(ln_mv[:, 3], ln_st[:, 3]).then_inc(c["y_stat"], 1)

            def y_norm(u, b, j):
                if j % 4 == 3:
                    dve.wait_ge(c["y_rstd"], upto(0, b + 1))
                    normalise(one(Y, b), c_x[:, j // 4], 3, c["y_done"])

            drive(dve, [(3, c_rotate), (2, c_norm2), (4, c_shift), (6, c_divide), (7, c_residual),
                        (0, c_stats), (1, c_norm), (8, y_norm)], UNITS, UNROLL, 4)
            dve.wait_ge(c["y_done"], upto(0, B))
            dve.wait_ge(tables, 1)

            def attention(ly):
                ub, bb = ly * UNITS, ly * B

                def table(k):
                    return l_tab[:, bass.ds(ly, 1), k].rearrange("p a q n -> p (a q) n")

                def l_copy_in(u, b, j):
                    if j % 4 == 0:
                        dve.wait_ge(l["x_turned"], upto(bb, b - 1))
                        dve.tensor_scalar(xin[:, j // 4], one(Y, b), 1.0, None, ALU.mult).then_inc(l["xin_done"], 1)

                def l_rotate(u, b, j):
                    k = j % 2
                    dve.wait_ge(l["add_done"], upto(ub, u - 1))
                    dve.wait_ge(l["sq_done"], upto(ub, u + 1))
                    shape = [128, 2, 4, L_DIM]
                    dve.tensor_tensor(l_rot[:, k, 0].rearrange("p (q h n) -> p q h n", q=2, h=4),
                                      bank[:, 0, :].rearrange("p (q h n) -> p q h n", q=2, h=4),
                                      table(0)[:, :, None, :].broadcast_to(shape), ALU.mult)
                    shape = [128, 2, 4, 2, L_DIM // 2]
                    dve.tensor_tensor(
                        l_rot[:, k, 1].rearrange("p (q h s n) -> p q h s n", q=2, h=4, s=2),
                        bank[:, 0, :].rearrange("p (q h s n) -> p q h s n", q=2, h=4, s=2)[:, :, :, ::-1, :],
                        table(1).rearrange("p q (s n) -> p q s n", s=2)[:, :, None].broadcast_to(shape),
                        ALU.mult).then_inc(l["rot_done"], 1)

                def l_sum_squares(u, b, j):
                    k = j % 2
                    dve.wait_ge(l["sq_done"], upto(ub, u + 1))
                    dve.wait_ge(l["pool_ss"], upto(ub, u - 1))
                    dve.tensor_reduce(l_ss[:, k], l_sq[:].rearrange("p (h n) -> p h n", n=L_DIM), AX.X, ALU.add)\
                       .then_inc(l["ss_done"], 1)

                def l_shift(u, b, j):
                    shift_scores(l, ub, u, j, bank[:, 3:5, 0:256].rearrange("p a (b n) -> p a b n", b=2), 4)

                def l_divide(u, b, j):
                    dve.wait_ge(l["o_turned"], upto(ub, u - 1))
                    divide(l, ub, u, j, 4, L_DIM, o[:, j % 2].rearrange("p (h n) -> p h n", n=L_DIM))

                def l_residual(u, b, j):
                    if j % 4 == 3:
                        dve.wait_ge(l["out_done"], upto(bb, b + 1))
                        dve.tensor_tensor(one(Y, b), one(Y, b), bank[:, 7, 256:384], ALU.add).then_inc(l["res_done"], 1)

                return Pipeline(dve, [(0, l_copy_in), (4, l_shift), (5, l_divide), (6, l_residual), (1, l_rotate),
                                 (1, l_sum_squares)], UNITS, UNROLL, 4)

            def feed_forward(ly):
                fb = ly * 4

                def f_stats(g):
                    dve.wait_ge(f["xs"], upto(0, fb + g + 1))
                    v = bank[:, 1, :].rearrange("p (a n) -> p a n", a=4)
                    apart(dve)
                    for q in range(4):
                        ins = dve.bn_stats(f_st[:, q], v[:, q])
                    ins.then_inc(f["stats"], 1)
                    dve.wait_ge(f["stats"], upto(0, fb + g + 1))
                    apart(dve)
                    for q in range(4):
                        ins = dve.bn_aggr(f_mv[:, q], f_st[:, q])
                    ins.then_inc(f["stat"], 1)

                def f_norm(g):
                    v = bank[:, 1, :].rearrange("p (a n) -> p a n", a=4)
                    dve.wait_ge(f["rstd"], upto(0, fb + g + 1))
                    dve.wait_ge(f["turned"], upto(0, fb + g))
                    for q in range(4):
                        ins = dve.tensor_scalar(f_n[:, q], v[:, q], f_mv[:, q, 0:1], f_rs[:, q:q + 1],
                                                ALU.subtract, ALU.mult)
                    ins.then_inc(f["n_done"], 1)

                def f_gated(g, k):
                    n = CHUNKS[k][1]
                    i = len(CHUNKS) * g + k
                    dve.wait_ge(f["gelu_done"], upto(0, ly * 12 + i + 1))
                    dve.wait_ge(f["out_mm"], upto(fb, g - 1))
                    dve.scalar_tensor_tensor(f_h[0:n, g % 2, k], bank[0:n, 4 + i % 2 * 2, :], f_b1[0:n, 0, k:k + 1],
                                             f_ge[0:n, i % 2], ALU.add, ALU.mult).then_inc(f["h_done"], 1)

                def f_residual(g):
                    yg = Y[:, 4 * g:4 * g + 4, :].rearrange("p a n -> p (a n)")
                    dve.wait_ge(f["out_mm"], upto(0, fb + g + 1))
                    dve.wait_ge(f["yb_done"], upto(0, fb + g + 1))
                    dve.tensor_tensor(yg, yg, bank[:, 7, :], ALU.add).then_inc(f["y_done"], 1)

                return f_stats, f_norm, f_gated, f_residual

            def rest_of_layer(ly, att, nxt):
                stats, norm, gated, residual = feed_forward(ly)
                att.steady()
                att.finish(0, 1)
                stats(0)
                att.finish(2)
                norm(0)
                att.finish(3)
                stats(1)
                att.finish(4)
                dve.wait_ge(ld_fw, (ly + 1) * (16 * FW_DMAS))
                gated(0, 0)
                att.finish(5, 6)
                for g in range(4):
                    if 0 < g < 3:
                        stats(g + 1)
                    if g > 0:
                        gated(g, 0)
                        residual(g - 1)
                    if g == 2 and nxt is not None:
                        dve.wait_ge(f["y_done"], upto(0, ly * 4 + 1))
                        nxt.start(0)
                    if g == 3 and nxt is not None:
                        nxt.start(1)
                    if g < 3:
                        norm(g + 1)
                    gated(g, 1)
                    if g == 3 and nxt is not None:
                        nxt.start(2)
                    gated(g, 2)
                if nxt is not None:
                    nxt.start(3)
                residual(3)
                if nxt is not None:
                    dve.wait_ge(f["y_done"], upto(0, ly * 4 + 4))
                    nxt.start(4, 5, 6, 7)

            attention(0).start(*range(UNROLL))
            with dve.Fori(0, LAYERS - 1) as ly:
                rest_of_layer(ly, attention(ly), attention(ly + 1))
            rest_of_layer(LAYERS - 1, attention(LAYERS - 1), None)

            dve.wait_ge(f["y_done"], upto(0, LAYERS * 4))
            for g in range(4):
                s = slice(4 * g, 4 * g + 4)
                dve.tensor_tensor(X[:, s, :], X[:, s, :], Y[:, s, :], ALU.add).then_inc(summed, 1)


_INS = ["x", "ctx_1024", "L0_xattn_w_q", "L0_xattn_b_q", "L0_xattn_w_k", "L0_xattn_b_k", "L0_xattn_w_v",
        "L0_xattn_b_v", "L0_xattn_w_out", "L0_xattn_b_out", "L0_ffn_router_w", "L0_ffn_router_b",
        "L0_ffn_expert_w", "L1_xattn_gamma_x", "L1_xattn_beta_x", "L1_xattn_gamma_l", "L1_xattn_beta_l",
        "L1_xattn_Wq", "L1_xattn_Wkv", "L1_xattn_Wo", "L1_ffn_Wqkv", "L1_ffn_q_scale", "L1_ffn_k_scale",
        "L1_ffn_Wo", "L1_ffn_ln_g", "L1_ffn_ln_b", "L1_ffn_W1", "L1_ffn_b1", "L1_ffn_W2", "L1_ffn_b2"]


def constants():
    import numpy as np
    from concourse import mybir as _mybir

    f = np.float32
    const = np.zeros((128, K_ALL), f)
    const[:, K_IDENT:K_IDENT + 128] = np.eye(128)
    const[:, K_SHIFT:K_SHIFT + 128] = np.eye(128, k=1)

    half = np.arange(0, L_DIM, 2, dtype=f)
    inv = f(1.0) / f(10000.0) ** (half / f(L_DIM))
    t = np.arange(S, dtype=f)
    freqs = t[:, None] * inv[None, :]
    freqs = np.concatenate([freqs, freqs], -1)
    base = (half + f(0.4 * L_DIM)) / f(1.4 * L_DIM)
    scale = base[None, :] ** ((t - S // 2) / f(WINDOW // 2))[:, None]
    scale = np.concatenate([scale, scale], -1)
    sign = np.where(np.arange(L_DIM) < L_DIM // 2, f(-1.0), f(1.0))[None, :]
    for q, s in enumerate((scale, f(1.0) / scale)):
        const[:, K_COS + q * L_DIM:K_COS + (q + 1) * L_DIM] = np.cos(freqs) * s
        const[:, K_SIN + q * L_DIM:K_SIN + (q + 1) * L_DIM] = np.sin(freqs) * s * sign
    const[:, K_COST:K_COST + 128] = np.tile(np.cos(freqs).T, (2, 1))
    const[:, K_SINT:K_SINT + 128] = np.tile((np.sin(freqs) * sign).T, (2, 1))
    const[np.arange(128), K_HEAD + np.arange(128) // A_DIM] = 1.0

    i, j = np.arange(128)[:, None], np.arange(128)[None, :]
    mask = np.where((i < j) | (i > j + WINDOW), f(MASKED), f(0.0))
    bf = np.concatenate([np.eye(128, dtype=f), mask, mask], 1).astype(_mybir.dt.np(_mybir.dt.bfloat16))
    return {"const": const, "const_bf": bf}


def kernel(**inputs):
    import numpy as _np
    import concourse.bacc as _bacc
    from concourse import mybir as _mybir
    from concourse.bass_utils import run_bass_kernel_spmd as _run

    nc = _bacc.Bacc("TRN2", target_bir_lowering=False, num_devices=1)
    given = {n: _np.ascontiguousarray(inputs[n]) for n in _INS} | constants()
    arrays, args = {}, {}
    for name, a in given.items():
        arrays[f"in_{name}_dram"] = a
        args[name] = nc.dram_tensor(f"in_{name}_dram", a.shape, _mybir.dt.from_np(a.dtype),
                                    kind="ExternalInput").ap()
    out = nc.dram_tensor("out_0_dram", (B, S, D), F32, kind="ExternalOutput").ap()
    build(nc, args, out)
    r = _run(nc, [arrays], core_ids=[0])
    return r.results[0]["out_0_dram"]
```

```python
from contextlib import ExitStack

import concourse.bass as bass
from concourse import mybir

F32 = mybir.dt.float32
BF16 = mybir.dt.bfloat16
F32R = mybir.dt.float32r
ALU = mybir.AluOpType
ACT = mybir.ActivationFunctionType
AX = mybir.AxisListType

B, S, D = 16, 128, 128
HALF = D // 2
UNITS = 4 * B
UNROLL = 8
LN_EPS = 1e-5
CREDIT = 1

A_HEADS, A_DIM = 16, 8
EXPERTS, TOP_K, MOE_EPS = 16, 6, 1e-10
C_HEADS, C_DIM = 8, 64
C_INNER = C_HEADS * C_DIM
LAYERS, L_HEADS, L_DIM, WINDOW = 6, 16, 64, 32
L_INNER = L_HEADS * L_DIM
W_CHUNKS = 3 * L_INNER // 512
PIECES = ((0, 1), (2, 3, 4), (5,))
FF = int(D * 4 * 2 / 3)
CHUNKS = [(c, min(128, FF - c)) for c in range(0, FF, 128)]
QK_SCALE = 8.0
MASKED = -1e30

K_IDENT, K_SHIFT, K_COS, K_SIN, K_COST, K_SINT, K_HEAD = 0, 128, 256, 384, 512, 640, 768
K_ALL = K_HEAD + A_HEADS


class Pipeline:

    def __init__(self, eng, stages, units, unroll, per_batch):
        self.eng, self.stages, self.units, self.unroll, self.per_batch = eng, stages, units, unroll, per_batch
        self.depth = max(skew for skew, _ in stages)
        assert self.depth <= unroll and units % unroll == 0 and unroll % per_batch == 0

    def slot(self, first_unit, first_batch, c):
        for skew, fn in self.stages:
            k = c - skew
            if isinstance(first_unit, int) and not 0 <= first_unit + k < self.units:
                continue
            fn(first_unit + k, first_batch + k // self.per_batch, k % self.unroll)

    def start(self, *slots):
        for c in slots:
            self.slot(0, 0, c)

    def steady(self):
        with self.eng.Fori(1, self.units // self.unroll) as i:
            for c in range(self.unroll):
                self.slot(i * self.unroll, i * (self.unroll // self.per_batch), c)

    def finish(self, *slots):
        for c in slots:
            self.slot(self.units, self.units // self.per_batch, c)


def drive(eng, stages, units, unroll, per_batch):
    pipe = Pipeline(eng, stages, units, unroll, per_batch)
    pipe.start(*range(unroll))
    pipe.steady()
    pipe.finish(*range(pipe.depth))


def build(nc, t, out):
    with ExitStack() as ctx:
        def sb(name, shape, dt=F32):
            return ctx.enter_context(nc.sbuf_tensor(name, shape, dt))

        def sem(name):
            return ctx.enter_context(nc.semaphore(name))

        def upto(before, n):
            return before + (max(n, 0) if isinstance(n, int) else n) + CREDIT

        bank = ctx.enter_context(nc.psum_tensor("bank", [128, 8, 512], F32))
        X = sb("X", [128, B, D])
        Y = sb("Y", [128, B, D])
        early = sb("early", [128, 2 * B * D])
        CTX = early[:, 0:B * D].rearrange("p (b n) -> p b n", n=D)
        ew = early[:, B * D:].rearrange("p (e n) -> p e n", n=D)
        l_raw = early[:, 0:3 * L_INNER]
        const = sb("const", [128, K_ALL])
        ident = const[:, K_IDENT:K_IDENT + 128]
        shift_t = const[:, K_SHIFT:K_SHIFT + 128]
        cos_t = const[:, K_COST:K_COST + 128]
        sin_t = const[:, K_SINT:K_SINT + 128]
        head_of = const[:, K_HEAD:K_HEAD + A_HEADS]
        cbf = sb("cbf", [128, 384], BF16)
        ident_bf, mask_bf = cbf[:, 0:128], cbf[:, 128:384]
        minus_half = sb("minus_half", [128, 8])

        sm = sb("sm", [128, 2, 512])
        prob = sb("prob", [128, 2, 512])
        probT = sb("probT", [128, 2, 512])
        peak = sb("peak", [128, 2, 4])
        rsum = sb("rsum", [128, 2, 4])
        o = sb("o", [128, 2, 256])

        ln_st = sb("ln_st", [128, 4, 6])
        ln_mv = sb("ln_mv", [128, 4, 2])
        ln_rs = sb("ln_rs", [128, 4])
        n1 = sb("n1", [128, 2, D])
        n2 = sb("n2", [128, 2, D])
        nx = sb("nx", [128, 2, D])

        xs_part = sb("xs_part", [128, 2, 2, 128], F32R)
        w_high = sb("w_high", [128, 3 * L_INNER], F32R)
        w_low = sb("w_low", [128, 3 * L_INNER], F32R)
        l_sq = sb("l_sq", [128, 512])
        l_qkT = sb("l_qkT", [128, 2, 512])
        l_oT = sb("l_oT", [128, 2, 8, 128])
        wa_raw = l_sq[:].rearrange("p (k n) -> p k n", n=D)
        waT = sb("waT", [128, 4, D])
        a_bq = sb("a_bq", [128, 1])
        a_bk = sb("a_bk", [128, 1])
        a_bv = sb("a_bv", [128, D])
        a_bo = sb("a_bo", [128, D])
        xcT = sb("xcT", [128, 2, 2, 128])
        a_q = sb("a_q", [128, 2, 128])
        a_k = sb("a_k", [128, 2, 128])
        a_km = sb("a_km", [128, 2, 4, 128])
        a_v = sb("a_v", [128, 2, A_HEADS, A_DIM + 1])
        a_o = sb("a_o", [128, 2, D])
        a_oT = sb("a_oT", [128, 2, D])
        a_y = sb("a_y", [128, 2, D])

        rw_raw = sb("rw_raw", [EXPERTS, D])
        rwT = sb("rwT", [128, EXPERTS])
        rb = sb("rb", [128, EXPERTS])
        m_st = sb("m_st", [128, B, 6])
        m_mv = sb("m_mv", [128, B, 2])
        m_rs = sb("m_rs", [128, B])
        m_xT = sb("m_xT", [128, B, 128])
        m_lg = sb("m_lg", [128, B, EXPERTS])
        m_e = sb("m_e", [128, B, EXPERTS])
        m_row = sb("m_row", [128, 5, B])
        m_top = sb("m_top", [128, B, 8])
        m_p = sb("m_p", [128, B, EXPERTS + 2])
        m_rep = sb("m_rep", [128, B, EXPERTS + 2])
        m_sel = sb("m_sel", [128, B, EXPERTS])
        m_gate = sb("m_gate", [128, B, EXPERTS + 1])
        m_g = sb("m_g", [128, 2, EXPERTS + 1])
        m_x = sb("m_x", [128, 2, 128])
        m_acc = sb("m_acc", [128, 2, D])

        c_most = l_oT[:].rearrange("p a b n -> p (a b n)")
        c_wq = c_most[:, 0:C_INNER]
        c_wkv = c_most[:, C_INNER:3 * C_INNER]
        c_wks = c_most[:, 3 * C_INNER:]
        c_wo = l_qkT[:, 0].rearrange("p (c n) -> p c n", n=D)
        c_x = sb("c_x", [128, 2, D])
        c_g = sb("c_g", [128, 4])
        c_kvT = l_qkT[:, 1].rearrange("p (a b n) -> p a b n", a=2, b=2)
        c_q = sb("c_q", [128, 2, 128])
        c_k = sb("c_k", [128, 2, 256])
        c_r = sb("c_r", [128, 2, 2, 128])
        c_v = sb("c_v", [128, 2, 2, C_HEADS, C_DIM + 1])
        c_oT = sb("c_oT", [128, 2, 4, 128])

        l_wo = sb("l_wo", [128, L_INNER // 128, D])
        l_sc = sb("l_sc", [128, LAYERS, 2, L_DIM])
        l_tab = sb("l_tab", [128, LAYERS, 2, 2, L_DIM])
        xin = sb("xin", [128, 2, D])
        xsT = sb("xsT", [128, 2, 128])
        l_rot = sb("l_rot", [128, 2, 2, 512])
        l_ss = sb("l_ss", [128, 2, 8])
        l_rn = sb("l_rn", [128, 2, 8])
        l_qk = sb("l_qk", [128, 2, 512])
        l_v = sb("l_v", [128, UNROLL, 4, L_DIM + 1])

        f_w1 = sb("f_w1", [128, 2 * FF])
        f_w2 = sb("f_w2", [128, len(CHUNKS), D])
        f_g = sb("f_g", [128, 2])
        f_b1 = sb("f_b1", [128, 2, len(CHUNKS)])
        f_b2 = sb("f_b2", [128, D])
        f_st = sb("f_st", [128, 4, 6])
        f_mv = sb("f_mv", [128, 4, 2])
        f_rs = sb("f_rs", [128, 4])
        f_n = sb("f_n", [128, 4, D])
        f_nT = sb("f_nT", [128, 2, 512])
        f_ge = sb("f_ge", [128, 2, 512])
        f_h = sb("f_h", [128, 2, len(CHUNKS), 512])

        m_n = f_nT[:].rearrange("p g (a n) -> p g a n", a=4)
        m_mix = f_h[:, :, 0:2].rearrange("p j k (e n) -> p j (k e) n", n=D)

        ld_const, ld_x, ld_ctx, ld_a = (sem(n) for n in ("ld_const", "ld_x", "ld_ctx", "ld_a"))
        ld_m, ld_c, ld_sc, ld_raw, ld_lw, ld_fw = (sem(n) for n in ("ld_m", "ld_c", "ld_sc", "ld_raw", "ld_lw", "ld_fw"))
        preset = sem("preset")
        tables = sem("tables")
        passed = {nc.vector.engine: sem("passed_dve"), nc.gpsimd.engine: sem("passed_pool")}
        w_turned, w_copied = sem("w_turned"), sem("w_copied")
        summed, stored = sem("summed"), sem("stored")

        stage_all = []

        def stage_sems(prefix, names):
            made = {n: sem(prefix + n) for n in names.split()}
            stage_all.extend(made.values())
            return made

        core = "s_done peaked sub_done exp_done turned probT_done pv_done rsum_done o_done "
        a = stage_sems("a_", core + "stats ln_stat pool_ln ln_rstd n_done x_turned xT_done proj qk_done v_done "
                 "km_done o_turned oT_done out_done biased res_done")
        m = stage_sems("m_", "stats ln_stat pool_ln ln_rstd n_done turned xT_done logits shifted exp_done g_chain "
                 "gate_done g_copied x_copied low_done high_done scaled mixed sum_chain summed res_done")
        c = stage_sems("c_", core + "stats ln_stat pool_ln ln_rstd n1_done stats2 ln_stat2 pool_ln2 ln_rstd2 n_done "
                 "x_turned kvT_done v_proj v_done qk_proj rot_done evac_done rope_done o_turned oT_done out_done "
                 "res_done y_copied y_stats y_stat y_pool y_rstd y_done")
        l = stage_sems("l_", core + "w_high_done w_split xin_done "
                 "x_turned xs_done x_high_done x_split qk_proj v_proj rot_done sq_done ss_done floored rn_done "
                 "add_done qk_done qk_turned qkT_done v_done o_turned oT_done out_done res_done")
        f = stage_sems("f_", "xs stats stat pool_st rstd n_done turned nT_done hidden gelu_done h_done out_mm yb_done "
                 "y_done")

        block = ctx.enter_context(nc.Block())

        def apart(eng):
            eng.sem_inc(passed[eng.engine], 1)

        def one(t3, b):
            return t3[:, bass.ds(b, 1), :].rearrange("p a n -> p (a n)")

        @block.sync
        def _(sp):
            sp.dma_start(const[:], t["const"]).then_inc(ld_const, 16)
            sp.dma_start(X[:], t["x"].rearrange("b s d -> s b d")).then_inc(ld_x, 16)
            for k, n in enumerate(("w_q", "w_k", "w_v", "w_out")):
                sp.dma_start(wa_raw[:, k, :], t["L0_xattn_" + n]).then_inc(ld_a, 16)
            sp.dma_start(CTX, t["ctx_1024"].rearrange("b s d -> s b d")).then_inc(ld_ctx, 16)
            for dst, n in ((a_bq, "b_q"), (a_bk, "b_k")):
                sp.dma_start(dst[:], t["L0_xattn_" + n].rearrange("(p a) -> p a", a=1)).then_inc(ld_a, 16)
            for dst, n in ((a_bv, "b_v"), (a_bo, "b_out")):
                sp.dma_start(dst[:], t["L0_xattn_" + n].partition_broadcast(128)).then_inc(ld_a, 16)
            sp.dma_start(rw_raw[:], t["L0_ffn_router_w"]).then_inc(ld_m, 16)
            sp.dma_start(rb[:], t["L0_ffn_router_b"].partition_broadcast(128)).then_inc(ld_m, 16)
            sp.dma_start(ew, t["L0_ffn_expert_w"].rearrange("e h d -> h e d")).then_inc(ld_m, 16)
            sp.dma_start(cbf[:], t["const_bf"]).then_inc(ld_c, 16)
            sp.dma_start(c_wq, t["L1_xattn_Wq"]).then_inc(ld_c, 16)
            sp.dma_start(c_wkv, t["L1_xattn_Wkv"]).then_inc(ld_c, 16)
            heads = "p (h s n) -> p h s n"
            for s in range(2):
                sp.dma_start(c_wks.rearrange(heads, s=2, n=C_DIM // 2)[:, :, s],
                             t["L1_xattn_Wkv"][:, 0:C_INNER].rearrange(heads, s=2, n=C_DIM // 2)[:, :, 1 - s])\
                  .then_inc(ld_c, 16)
            sp.dma_start(c_wo, t["L1_xattn_Wo"].rearrange("(c p) n -> p c n", p=128)).then_inc(ld_c, 16)
            for k, n in enumerate(("gamma_x", "beta_x", "gamma_l", "beta_l")):
                sp.dma_start(c_g[:, k:k + 1], t["L1_xattn_" + n].rearrange("(p a) -> p a", a=1)).then_inc(ld_c, 16)
            for k, n in enumerate(("q_scale", "k_scale")):
                sp.dma_start(l_sc[:, :, k, :], t["L1_ffn_" + n].partition_broadcast(128)).then_inc(ld_sc, 16)
            sp.wait_ge(m["high_done"], upto(0, B))
            sp.wait_ge(c["n1_done"], upto(0, B))
            with sp.Fori(0, LAYERS) as ly:
                def layer(n):
                    x = t["L1_ffn_" + n]
                    v = x[bass.ds(ly, 1)]
                    return v.rearrange("a b c -> (a b) c") if len(x.shape) == 3 else v.rearrange("a b -> (a b)")

                sp.wait_ge(l["w_split"], upto(0, ly * W_CHUNKS))
                sp.dma_start(l_raw, layer("Wqkv")).then_inc(ld_raw, 16)
                sp.wait_ge(l["out_done"], upto(0, ly * B))
                sp.dma_start(l_wo[:], layer("Wo").rearrange("(c p) n -> p c n", p=128)).then_inc(ld_lw, 16)
                sp.wait_ge(f["y_done"], upto(0, ly * 4))
                sp.dma_start(f_w1[:], layer("W1")).then_inc(ld_fw, 16)
                full = FF // 128 * 128
                sp.dma_start(f_w2[:, 0:full // 128, :],
                             layer("W2")[0:full].rearrange("(c p) n -> p c n", p=128)).then_inc(ld_fw, 16)
                sp.dma_start(f_w2[0:FF - full, full // 128, :], layer("W2")[full:FF]).then_inc(ld_fw, 16)
                sp.dma_start(f_g[:, 0:1], layer("ln_g").rearrange("(p a) -> p a", a=1)).then_inc(ld_fw, 16)
                sp.dma_start(f_g[:, 1:2], layer("ln_b").rearrange("(p a) -> p a", a=1)).then_inc(ld_fw, 16)
                for s in range(2):
                    for k, (c0, n) in enumerate(CHUNKS):
                        sp.dma_start(f_b1[0:n, s, k:k + 1], layer("b1")[s * FF + c0:s * FF + c0 + n]
                                     .rearrange("(p a) -> p a", a=1)).then_inc(ld_fw, 16)
                sp.dma_start(f_b2[:], layer("b2").partition_broadcast(128)).then_inc(ld_fw, 16)
            for g in range(4):
                sp.wait_ge(summed, g + 1)
                sp.dma_start(out[4 * g:4 * g + 4].rearrange("b s d -> s b d"), X[:, 4 * g:4 * g + 4]).then_inc(stored, 16)
            sp.wait_ge(stored, 64)

        FW_DMAS = 5 + 2 * len(CHUNKS) + 1

        @block.gpsimd
        def _(pool):
            pool.memset(minus_half[:], -0.5)
            pool.memset(a_v[:, :, :, A_DIM:], 1.0)
            pool.memset(c_v[:, :, :, :, C_DIM:], 1.0)
            pool.memset(l_v[:, :, :, L_DIM:], 1.0)
            pool.memset(m_p[:, :, EXPERTS:], -1.0)
            pool.memset(xsT[:, :, 0:1], 0.0).then_inc(preset, 1)
            pool.wait_ge(preset, 1)

            def rstd(dst, var, chain, n, done):
                apart(pool)
                pool.tensor_scalar(dst, var, LN_EPS, None, ALU.add).then_inc(chain, 1)
                pool.wait_ge(chain, upto(0, n + 1))
                pool.tensor_tensor(dst, dst, minus_half[:, 0:dst.shape[1]], ALU.pow).then_inc(done, 1)

            def a_rstd(u, b, j):
                if j % 4 == 0:
                    pool.wait_ge(a["ln_stat"], upto(0, b + 1))
                    rstd(ln_rs[:, 0:1], ln_mv[:, 0, 1:2], a["pool_ln"], b, a["ln_rstd"])

            def a_mask_k(u, b, j):
                g = j % 4
                pool.wait_ge(a["qk_done"], upto(0, b + 1))
                pool.wait_ge(a["s_done"], upto(0, u - 1))
                pool.tensor_tensor(a_km[:, j % 2], a_k[:, j // 4, None, :].broadcast_to([128, 4, 128]),
                                   head_of[:, 4 * g:4 * g + 4, None].broadcast_to([128, 4, 128]),
                                   ALU.mult).then_inc(a["km_done"], 1)

            pool.wait_ge(ld_const, 16)
            drive(pool, [(3, a_mask_k), (0, a_rstd)], UNITS, UNROLL, 4)

            for g in range(4):
                q = slice(4 * g, 4 * g + 4)
                pool.wait_ge(m["ln_stat"], upto(0, g + 1))
                pool.tensor_scalar(m_rs[:, q], m_mv[:, q, 1], LN_EPS, None, ALU.add).then_inc(m["pool_ln"], 1)
                pool.wait_ge(m["pool_ln"], upto(0, g + 1))
                pool.tensor_tensor(m_rs[:, q], m_rs[:, q], minus_half[:, 0:4], ALU.pow).then_inc(m["ln_rstd"], 1)

            def m_sum(u, b, j):
                mix = m_mix[:, j].rearrange("p e n -> p (e n)")
                pool.wait_ge(m["mixed"], upto(0, b + 1))
                pool.tensor_tensor(mix[:, 0:4 * D], mix[:, 0:4 * D], mix[:, 4 * D:], ALU.add)\
                    .then_inc(m["sum_chain"], 1)
                pool.wait_ge(m["sum_chain"], upto(0, b * 2 + 1))
                pool.tensor_tensor(mix[:, 0:2 * D], mix[:, 0:2 * D], mix[:, 2 * D:4 * D], ALU.add)\
                    .then_inc(m["sum_chain"], 1)
                pool.wait_ge(m["sum_chain"], upto(0, b * 2 + 2))
                pool.wait_ge(m["res_done"], upto(0, b - 1))
                pool.tensor_tensor(m_acc[:, j], mix[:, 0:D], mix[:, D:2 * D], ALU.add).then_inc(m["summed"], 1)

            drive(pool, [(1, m_sum)], B, 2, 1)

            pool.wait_ge(ld_sc, 32)
            for k, at in enumerate((K_COS, K_SIN)):
                base = const[:, at:at + 2 * L_DIM]
                if k == 0:
                    v = l_sc[:]
                    ins = pool.tensor_tensor(
                        l_tab[:, :, 0].rearrange("p l q n -> p l (q n)"), v.rearrange("p l q n -> p l (q n)"),
                        base[:, None, :].broadcast_to([128, LAYERS, 2 * L_DIM]), ALU.mult)
                else:
                    for q in range(2):
                        ins = pool.tensor_tensor(
                            l_tab[:, :, 1, q].rearrange("p l (s n) -> p l s n", s=2),
                            l_sc[:, :, q].rearrange("p l (s n) -> p l s n", s=2)[:, :, ::-1, :],
                            base[:, q * L_DIM:(q + 1) * L_DIM].rearrange("p (s n) -> p s n", s=2)[:, None]
                            .broadcast_to([128, LAYERS, 2, L_DIM // 2]), ALU.mult)
            ins.then_inc(tables, 1)

            def c_rstd(u, b, j):
                if j % 4 == 0:
                    pool.wait_ge(c["ln_stat"], upto(0, b + 1))
                    rstd(ln_rs[:, 0:2], ln_mv[:, 0:2, 1], c["pool_ln"], b, c["ln_rstd"])

            def c_rstd2(u, b, j):
                if j % 4 == 0:
                    pool.wait_ge(c["ln_stat2"], upto(0, b + 1))
                    rstd(ln_rs[:, 2:3], ln_mv[:, 2, 1:2], c["pool_ln2"], b, c["ln_rstd2"])

            def y_rstd(u, b, j):
                if j % 4 == 3:
                    pool.wait_ge(c["y_stat"], upto(0, b + 1))
                    rstd(ln_rs[:, 3:4], ln_mv[:, 3, 1:2], c["y_pool"], b, c["y_rstd"])

            second = Pipeline(pool, [(0, c_rstd), (1, c_rstd2), (7, y_rstd)], UNITS, UNROLL, 4)
            second.start(*range(UNROLL))
            second.steady()

            def attention(ly):
                ub = ly * UNITS

                def l_norm(u, b, j):
                    k = j % 2
                    pool.wait_ge(l["rot_done"], upto(ub, u + 1))
                    pool.wait_ge(l["qk_turned"], upto(ub, u - 1))
                    pool.tensor_tensor(l_qk[:, k], l_rot[:, k, 0], l_rot[:, k, 1], ALU.add).then_inc(l["add_done"], 1)
                    pool.wait_ge(l["floored"], upto(ub, u + 1))
                    pool.tensor_tensor(l_rn[:, k], l_ss[:, k], minus_half[:], ALU.pow).then_inc(l["rn_done"], 1)
                    pool.wait_ge(l["add_done"], upto(ub, u + 1))
                    pool.wait_ge(l["rn_done"], upto(ub, u + 1))
                    v = l_qk[:, k].rearrange("p (h n) -> p h n", n=L_DIM)
                    pool.tensor_tensor(v, v, l_rn[:, k, :, None].broadcast_to([128, 8, L_DIM]),
                                       ALU.mult).then_inc(l["qk_done"], 1)

                return Pipeline(pool, [(1, l_norm)], UNITS, UNROLL, 4)

            def feed_forward(ly):
                fb = ly * 4
                pool.wait_ge(ld_fw, (ly + 1) * (16 * FW_DMAS))
                for g in range(4):
                    yg = Y[:, 4 * g:4 * g + 4, :]
                    pool.wait_ge(f["stat"], upto(0, fb + g + 1))
                    apart(pool)
                    pool.tensor_scalar(f_rs[:], f_mv[:, :, 1], LN_EPS, None, ALU.add).then_inc(f["pool_st"], 1)
                    pool.wait_ge(f["pool_st"], upto(0, fb + g + 1))
                    pool.tensor_tensor(f_rs[:], f_rs[:], minus_half[:, 0:4], ALU.pow).then_inc(f["rstd"], 1)
                    pool.wait_ge(f["xs"], upto(0, fb + g + 1))
                    pool.tensor_tensor(yg, yg, f_b2[:, None, :].broadcast_to([128, 4, D]),
                                       ALU.add).then_inc(f["yb_done"], 1)

            def rest_of_layer(ly, att, nxt):
                att.steady()
                att.finish(0)
                feed_forward(ly)
                if nxt is not None:
                    nxt.start(*range(UNROLL))

            first = attention(0)
            second.finish(*range(6))
            first.start(0, 1)
            second.finish(6)
            first.start(*range(2, UNROLL))
            with pool.Fori(0, LAYERS - 1) as ly:
                rest_of_layer(ly, attention(ly), attention(ly + 1))
            rest_of_layer(LAYERS - 1, attention(LAYERS - 1), None)

        @block.tensor
        def _(pe):
            def turn(s, base, u, j):
                pe.wait_ge(s["exp_done"], upto(base, u + 1))
                pe.wait_ge(s["probT_done"], upto(base, u))
                for h in range(4):
                    ins = pe.transpose(bank[:, 5, h * 128:(h + 1) * 128], prob[:, j % 2, h * 128:(h + 1) * 128],
                                       ident)
                ins.then_inc(s["turned"], 1)

            pe.wait_ge(ld_const, 16)
            pe.wait_ge(ld_a, 16 * 8)
            for k in range(4):
                pe.transpose(bank[:, 2, k * 128:(k + 1) * 128], wa_raw[:, k, :], ident)
            pe.wait_ge(ld_m, 48)
            pe.transpose(bank[:, 1, 0:EXPERTS], rw_raw[:], ident[0:EXPERTS, 0:EXPERTS]).then_inc(w_turned, 1)
            pe.wait_ge(w_copied, 1)
            pe.wait_ge(preset, 1)

            def a_turn_x(u, b, j):
                if j % 4 == 0:
                    k = j // 4
                    pe.wait_ge(a["n_done"], upto(0, b + 1))
                    pe.wait_ge(a["xT_done"], upto(0, b))
                    pe.transpose(bank[:, 2, 0:128], n1[:, k], ident)
                    pe.transpose(bank[:, 2, 128:256], nx[:, k], ident).then_inc(a["x_turned"], 1)

            def a_project(u, b, j):
                if j % 4 == 0:
                    k = j // 4
                    pe.wait_ge(a["xT_done"], upto(0, b + 1))
                    pe.wait_ge(a["qk_done"], upto(0, b))
                    pe.wait_ge(a["v_done"], upto(0, b))
                    pe.matmul(bank[:, 0, 0:128], waT[:, 0], xcT[:, k, 0], start=True, stop=True)
                    pe.matmul(bank[:, 0, 128:256], waT[:, 1], xcT[:, k, 1], start=True, stop=True)
                    pe.matmul(bank[:, 1, 0:128], xcT[:, k, 1], waT[:, 2], start=True, stop=True)\
                      .then_inc(a["proj"], 1)

            def a_scores(u, b, j):
                pe.wait_ge(a["km_done"], upto(0, u + 1))
                pe.wait_ge(a["qk_done"], upto(0, b + 1))
                pe.wait_ge(a["sub_done"], upto(0, u - 1))
                pe.matmul(bank[:, 3 + j % 2, :], a_q[:, j // 4], a_km[:, j % 2].rearrange("p h n -> p (h n)"),
                          start=True, stop=True).then_inc(a["s_done"], 1)

            def a_pv(u, b, j):
                pe.wait_ge(a["probT_done"], upto(0, u + 1))
                pe.wait_ge(a["v_done"], upto(0, b + 1))
                pe.wait_ge(a["o_done"], upto(0, u))
                for h in range(4):
                    w = A_DIM + 1
                    ins = pe.matmul(bank[:, 6, h * w:(h + 1) * w], probT[:, j % 2, h * 128:(h + 1) * 128],
                                    a_v[:, j // 4, j % 4 * 4 + h, :], start=True, stop=True)
                ins.then_inc(a["pv_done"], 1)

            def a_turn_o(u, b, j):
                if j % 4 == 3:
                    pe.wait_ge(a["o_done"], upto(0, u + 1))
                    pe.wait_ge(a["res_done"], upto(0, b))
                    pe.transpose(bank[:, 7, 0:128], a_o[:, j // 4], ident).then_inc(a["o_turned"], 1)

            def a_output(u, b, j):
                if j % 4 == 3:
                    pe.wait_ge(a["oT_done"], upto(0, b + 1))
                    pe.matmul(bank[:, 7, 128:256], a_oT[:, j // 4], waT[:, 3], start=True, stop=True)\
                      .then_inc(a["out_done"], 1)

            drive(pe, [(2, a_turn_x), (6, lambda u, b, j: turn(a, 0, u, j)), (4, a_scores), (8, a_turn_o), (7, a_pv),
                       (8, a_output), (2, a_project)], UNITS, UNROLL, 4)

            def m_logits(g):
                pe.wait_ge(m["xT_done"], upto(0, g + 1))
                for b in range(4 * g, 4 * g + 4):
                    ins = pe.matmul(bank[:, 0, b * EXPERTS:(b + 1) * EXPERTS], m_xT[:, b], rwT[:], start=True,
                                    stop=True)
                ins.then_inc(m["logits"], 1)

            for g in range(4):
                pe.wait_ge(m["n_done"], upto(0, g + 1))
                pe.wait_ge(m["xT_done"], upto(0, g - 1))
                for n in range(4):
                    ins = pe.transpose(bank[:, 1 + g % 2, n * 128:(n + 1) * 128], m_n[:, g % 2, n], ident)
                ins.then_inc(m["turned"], 1)
                if g > 0:
                    m_logits(g - 1)
            m_logits(3)
            pe.wait_ge(m["shifted"], upto(0, 1))

            def m_experts(u, b, j):
                pe.wait_ge(m["x_copied"], upto(0, b + 1))
                for q in range(4):
                    if q == 0:
                        pe.wait_ge(m["scaled"], upto(0, b - 1))
                    if q == 2:
                        pe.wait_ge(m["mixed"], upto(0, b - 1))
                    ins = pe.matmul(bank[:, 4 * j + q, :], m_x[:, j],
                                    ew[:, 4 * q:4 * q + 4, :].rearrange("p e n -> p (e n)"), start=True, stop=True)
                    if q == 1:
                        ins.then_inc(m["low_done"], 1)
                ins.then_inc(m["high_done"], 1)

            drive(pe, [(0, m_experts)], B, 2, 1)

            pe.wait_ge(ld_c, 16 * 10)

            def c_turn_x(u, b, j):
                if j % 4 == 0:
                    k = j // 4
                    pe.wait_ge(c["n_done"], upto(0, b + 1))
                    pe.wait_ge(c["kvT_done"], upto(0, b))
                    pe.transpose(bank[:, 2, 0:128], nx[:, k], ident)
                    pe.transpose(bank[:, 2, 128:256], n2[:, k], ident).then_inc(c["x_turned"], 1)

            def c_values(u, b, j):
                tile = j % 4
                if tile < 2:
                    pe.wait_ge(c["kvT_done"], upto(0, b + 1))
                    pe.wait_ge(c["v_done"], upto(0, b * 2 + tile))
                    pe.matmul(bank[:, 1, :], c_kvT[:, j // 4, tile], c_wkv[:, C_INNER:], start=True, stop=True)\
                      .then_inc(c["v_proj"], 1)

            def c_project(u, b, j):
                k, p = j // 4, j % 4
                w = slice(128 * p, 128 * p + 128)
                pe.wait_ge(c["kvT_done"], upto(0, b + 1))
                pe.wait_ge(c["evac_done"], upto(0, u))
                both = c_kvT[:, k].rearrange("p t n -> p (t n)")
                pe.matmul(bank[:, 0, 0:128], c_wq[:, w], c_kvT[:, k, 1], start=True, stop=True)
                pe.matmul(bank[:, 0, 128:384], c_wkv[:, w], both, start=True, stop=True)
                pe.matmul(bank[:, 0, 384:512], c_wks[:, w], c_kvT[:, k, 0], start=True, stop=True)\
                  .then_inc(c["qk_proj"], 1)

            def c_scores(u, b, j):
                pe.wait_ge(c["evac_done"], upto(0, u + 1))
                pe.wait_ge(c["rope_done"], upto(0, u + 1))
                pe.wait_ge(c["sub_done"], upto(0, u))
                for h in range(2):
                    r = slice(64 * h, 64 * h + 64)
                    ins = pe.matmul(bank[:, 3 + h, 0:256], c_q[r, j % 2], c_k[r, j % 2], start=True, stop=True)
                ins.then_inc(c["s_done"], 1)

            def c_pv(u, b, j):
                pe.wait_ge(c["probT_done"], upto(0, u + 1))
                pe.wait_ge(c["v_done"], upto(0, b * 2 + 2))
                pe.wait_ge(c["o_done"], upto(0, u))
                w = C_DIM + 1
                for h in range(2):
                    for tile in range(2):
                        n = h * 2 + tile
                        ins = pe.matmul(bank[:, 6, h * w:(h + 1) * w], probT[:, j % 2, n * 128:(n + 1) * 128],
                                        c_v[:, j // 4, tile, 2 * (j % 4) + h, :], start=tile == 0, stop=tile == 1)
                ins.then_inc(c["pv_done"], 1)

            def c_turn_o(u, b, j):
                pe.wait_ge(c["o_done"], upto(0, u + 1))
                pe.wait_ge(c["oT_done"], upto(0, u))
                pe.wait_ge(c["res_done"], upto(0, b))
                pe.transpose(bank[:, 7, 0:128], o[:, j % 2, 0:128], ident).then_inc(c["o_turned"], 1)

            def c_output(u, b, j):
                if j % 4 == 3:
                    pe.wait_ge(c["oT_done"], upto(0, u + 1))
                    for p in range(4):
                        ins = pe.matmul(bank[:, 7, 128:256], c_oT[:, j // 4, p], c_wo[:, p], start=p == 0, stop=p == 3)
                    ins.then_inc(c["out_done"], 1)

            second = Pipeline(pe, [(3, c_turn_x), (5, c_scores), (6, lambda u, b, j: turn(c, 0, u, j)), (7, c_turn_o),
                                   (3, c_project), (6, c_pv), (7, c_output), (3, c_values)], UNITS, UNROLL, 4)
            second.start(*range(UNROLL))
            second.steady()

            def attention(ly):
                ub, bb = ly * UNITS, ly * B

                def l_turn_x(u, b, j):
                    if j % 4 == 0:
                        pe.wait_ge(l["xin_done"], upto(bb, b + 1))
                        pe.wait_ge(l["oT_done"], upto(ub, u - 6))
                        pe.wait_ge(l["res_done"], upto(bb, b - 2))
                        pe.wait_ge(l["xs_done"], upto(bb * 2, b * 2))
                        pe.transpose(bank[:, 7, 384:512], xin[:, j // 4], ident).then_inc(l["x_turned"], 1)

                def l_project(u, b, j):
                    g = j % 4
                    high, low = (w[:].rearrange("p (t n) -> p t n", t=3) for w in (w_high, w_low))
                    passes = ((0, high), (0, low), (1, high))
                    pe.wait_ge(l["x_split"], upto(bb, b + 1))
                    pe.wait_ge(l["rot_done"], upto(ub, u))
                    for n, (part, w) in enumerate(passes):
                        ins = pe.matmul(bank[:, 0, :].rearrange("p (q n) -> p q n", q=2), xs_part[:, part, j // 4],
                                        w[:, 0:2, 256 * g:256 * g + 256], start=n == 0, stop=n == 2)
                    ins.then_inc(l["qk_proj"], 1)
                    pe.wait_ge(l["v_done"], upto(ub, u))
                    for n, (part, w) in enumerate(passes):
                        ins = pe.matmul(bank[:, 1, 0:256], xs_part[:, part, j // 4], w[:, 2, 256 * g:256 * g + 256],
                                        start=n == 0, stop=n == 2)
                    ins.then_inc(l["v_proj"], 1)

                def l_turn_qk(u, b, j):
                    pe.wait_ge(l["qk_done"], upto(ub, u + 1))
                    pe.wait_ge(l["qkT_done"], upto(ub, u))
                    for n in range(4):
                        ins = pe.transpose(bank[:, 2, n * 128:(n + 1) * 128],
                                           l_qk[:, j % 2, n * 128:(n + 1) * 128], ident)
                    ins.then_inc(l["qk_turned"], 1)

                def l_scores(u, b, j):
                    pe.wait_ge(l["qkT_done"], upto(ub, u + 1))
                    pe.wait_ge(l["sub_done"], upto(ub, u))
                    for r in range(2):
                        pe.matmul(bank[:, 3 + r, 0:256], ident_bf, mask_bf, start=True, stop=False,
                                  skip_group_check=True)
                    for p in range(2):
                        for r in range(2):
                            rows = slice(64 * r, 64 * r + 64)
                            ins = pe.matmul(bank[:, 3 + r, 128 * p:128 * p + 128],
                                            l_qkT[rows, j % 2, 128 * p:128 * p + 128],
                                            l_qkT[rows, j % 2, 256 + 128 * p:384 + 128 * p],
                                            start=False, stop=True, skip_group_check=True)
                    ins.then_inc(l["s_done"], 1)

                def l_pv(u, b, j):
                    pe.wait_ge(l["probT_done"], upto(ub, u + 1))
                    pe.wait_ge(l["v_done"], upto(ub, u + 1))
                    pe.wait_ge(l["o_done"], upto(ub, u))
                    w = L_DIM + 1
                    for h in range(4):
                        n = h % 2 * 2 + h // 2
                        ins = pe.matmul(bank[:, 6, h * w:(h + 1) * w], probT[:, j % 2, n * 128:(n + 1) * 128],
                                        l_v[:, j, h, :], start=True, stop=True)
                    ins.then_inc(l["pv_done"], 1)

                def l_turn_o(u, b, j):
                    r = j % 4
                    pe.wait_ge(l["o_done"], upto(ub, u + 1))
                    pe.wait_ge(l["oT_done"], upto(ub, u))
                    pe.wait_ge(l["res_done"], upto(bb, b))
                    turned = b + (r + 6) // 4 + 1
                    if isinstance(turned, int):
                        turned = min(turned, B)
                    pe.wait_ge(l["xs_done"], upto(bb * 2, turned * 2))
                    for p in range(2):
                        ins = pe.transpose(bank[:, 7, p * 128:(p + 1) * 128], o[:, j % 2, p * 128:(p + 1) * 128],
                                           ident)
                    ins.then_inc(l["o_turned"], 1)

                def l_output(u, b, j):
                    if j % 4 == 3:
                        pe.wait_ge(l["oT_done"], upto(ub, u + 1))
                        turned = b + 3
                        if isinstance(turned, int):
                            turned = min(turned, B)
                        pe.wait_ge(l["xs_done"], upto(bb * 2, turned * 2))
                        for p in range(8):
                            ins = pe.matmul(bank[:, 7, 256:384], l_oT[:, j // 4, p], l_wo[:, p],
                                            start=p == 0, stop=p == 7)
                        ins.then_inc(l["out_done"], 1)

                return Pipeline(pe, [(6, lambda u, b, j: turn(l, ub, u, j)), (4, l_scores), (7, l_turn_o), (6, l_pv),
                                     (3, l_turn_qk), (7, l_output), (0, l_turn_x), (1, l_project)],
                                UNITS, UNROLL, 4)

            def feed_forward(ly, last):
                fb, ub = ly * 4, ly * UNITS

                def f_shift(g):
                    v = bank[:, 1, :].rearrange("p (a n) -> p a n", a=4)
                    yg = Y[:, 4 * g:4 * g + 4, :]
                    pe.wait_ge(l["res_done"], upto(0, ly * B + 4 * g + 4))
                    if g == 0:
                        pe.wait_ge(l["v_done"], upto(ub, UNITS))
                    else:
                        pe.wait_ge(f["n_done"], upto(0, fb + g))
                    pe.matmul(v[:, :, 0:HALF], ident, yg[:, :, 0:HALF], start=True, stop=True)
                    pe.matmul(v[:, :, HALF:], shift_t, yg[:, :, HALF:], start=True, stop=True).then_inc(f["xs"], 1)

                def f_turn(g):
                    pe.wait_ge(f["n_done"], upto(0, fb + g + 1))
                    if g == 0:
                        pe.wait_ge(l["qkT_done"], upto(ub, UNITS))
                    pe.wait_ge(f["nT_done"], upto(0, fb + g))
                    for n in range(4):
                        ins = pe.transpose(bank[:, 2, n * 128:(n + 1) * 128], f_n[:, n], ident)
                    ins.then_inc(f["turned"], 1)

                def f_hidden(g, k):
                    c0, n = CHUNKS[k]
                    i = len(CHUNKS) * g + k
                    pe.wait_ge(f["nT_done"], upto(0, fb + g + 1))
                    pe.wait_ge(f["h_done"], upto(ly * 12, i - 1))
                    if i == 0:
                        pe.wait_ge(l["sub_done"], upto(ub, UNITS))
                    if i == 1:
                        pe.wait_ge(l["probT_done"], upto(ub, UNITS))
                        pe.wait_ge(l["o_done"], upto(ub, UNITS))
                    at = 3 + i % 2 * 2
                    pe.matmul(bank[0:n, at, :], f_w1[:, FF + c0:FF + c0 + n], f_nT[:, g % 2], start=True, stop=True)
                    pe.matmul(bank[0:n, at + 1, :], f_w1[:, c0:c0 + n], f_nT[:, g % 2], start=True, stop=True)\
                      .then_inc(f["hidden"], 1)

                def f_out(g):
                    pe.wait_ge(f["h_done"], upto(0, ly * 12 + 3 * g + 3))
                    if g == 0:
                        pe.wait_ge(l["res_done"], upto(0, (ly + 1) * B))
                    pe.wait_ge(f["y_done"], upto(0, fb + g))
                    if g > 1 and not last:
                        pe.wait_ge(l["xs_done"], upto((ly + 1) * B * 2, 2))
                    for q in range(4):
                        for k, (c0, n) in enumerate(CHUNKS):
                            ins = pe.matmul(bank[:, 7, q * 128:(q + 1) * 128], f_h[0:n, g % 2, k, q * 128:(q + 1) * 128],
                                            f_w2[0:n, k, :], start=k == 0, stop=k == len(CHUNKS) - 1)
                    ins.then_inc(f["out_mm"], 1)

                return f_shift, f_turn, f_hidden, f_out

            def rest_of_layer(ly, att, nxt):
                shift, turn_n, hidden, output = feed_forward(ly, nxt is None)
                att.steady()
                att.finish(0, 1)
                shift(0)
                att.finish(2, 3)
                pe.wait_ge(ld_fw, (ly + 1) * (16 * FW_DMAS))
                turn_n(0)
                att.finish(4)
                hidden(0, 0)
                att.finish(5)
                shift(1)
                att.finish(6)
                for g in range(4):
                    if g > 0:
                        hidden(g, 0)
                    if g == 3 and nxt is not None:
                        pe.wait_ge(l["w_split"], upto(0, (ly + 2) * W_CHUNKS))
                        pe.wait_ge(ld_lw, (ly + 2) * 16)
                        nxt.start(1)
                    if g > 0:
                        output(g - 1)
                    hidden(g, 1)
                    if g == 3 and nxt is not None:
                        nxt.start(2)
                    if g < 3:
                        turn_n(g + 1)
                    if g == 2 and nxt is not None:
                        pe.wait_ge(f["y_done"], upto(0, ly * 4 + 2))
                        nxt.start(0)
                    hidden(g, 2)
                    if g < 2:
                        shift(g + 2)
                if nxt is not None:
                    nxt.start(3)
                output(3)
                if nxt is not None:
                    pe.wait_ge(f["y_done"], upto(0, ly * 4 + 4))
                    nxt.start(4, 5, 6, 7)

            first = attention(0)
            second.finish(0, 1, 2, 3)
            pe.wait_ge(c["oT_done"], upto(0, UNITS - 3))
            pe.wait_ge(c["res_done"], upto(0, B - 1))
            first.start(0)
            pe.wait_ge(l["w_split"], upto(0, W_CHUNKS))
            pe.wait_ge(c["evac_done"], upto(0, UNITS))
            pe.wait_ge(c["v_done"], upto(0, 2 * B))
            first.start(1)
            pe.wait_ge(l["xs_done"], upto(0, 2))
            second.finish(4)
            first.start(2)
            second.finish(5, 6)
            pe.wait_ge(c["oT_done"], upto(0, UNITS))
            pe.wait_ge(c["res_done"], upto(0, B))
            pe.wait_ge(ld_lw, 16)
            first.start(*range(3, UNROLL))
            with pe.Fori(0, LAYERS - 1) as ly:
                rest_of_layer(ly, attention(ly), attention(ly + 1))
            rest_of_layer(LAYERS - 1, attention(LAYERS - 1), None)

        @block.scalar
        def _(act):
            def exp(s, base, u, j, scale):
                act.wait_ge(s["sub_done"], upto(base, u + 1))
                act.wait_ge(s["turned"], upto(base, u - 1))
                act.activation(prob[:, j % 2, :], sm[:, j % 2, :], ACT.Exp, scale=scale).then_inc(s["exp_done"], 1)

            def copy_prob(s, base, u, j):
                act.wait_ge(s["turned"], upto(base, u + 1))
                act.wait_ge(s["pv_done"], upto(base, u - 1))
                act.activation(probT[:, j % 2, :], bank[:, 5, :], ACT.Copy).then_inc(s["probT_done"], 1)

            for s in stage_all:
                act.sem_inc(s, CREDIT)
            act.wait_ge(w_turned, 1)
            act.activation(waT[:].rearrange("p a n -> p (a n)"), bank[:, 2, :], ACT.Copy)
            act.activation(rwT[:], bank[:, 1, 0:EXPERTS], ACT.Copy).then_inc(w_copied, 1)

            def a_copy_x(u, b, j):
                if j % 4 == 0:
                    act.wait_ge(a["x_turned"], upto(0, b + 1))
                    act.wait_ge(a["proj"], upto(0, b - 1))
                    act.activation(xcT[:, j // 4].rearrange("p a n -> p (a n)"), bank[:, 2, 0:256], ACT.Copy)\
                       .then_inc(a["xT_done"], 1)

            def a_copy_qk(u, b, j):
                if j % 4 == 0:
                    k = j // 4
                    act.wait_ge(a["proj"], upto(0, b + 1))
                    act.wait_ge(a["s_done"], upto(0, u - 4))
                    act.wait_ge(a["km_done"], upto(0, u - 4))
                    act.activation(a_q[:, k], bank[:, 0, 0:128], ACT.Identity, bias=a_bq[:])
                    act.activation(a_k[:, k], bank[:, 0, 128:256], ACT.Identity, bias=a_bk[:])\
                       .then_inc(a["qk_done"], 1)

            def a_copy_o(u, b, j):
                if j % 4 == 3:
                    act.wait_ge(a["o_turned"], upto(0, b + 1))
                    act.wait_ge(a["out_done"], upto(0, b))
                    act.activation(a_oT[:, j // 4], bank[:, 7, 0:128], ACT.Copy).then_inc(a["oT_done"], 1)

            act.wait_ge(ld_a, 16 * 8)
            drive(act, [(3, a_copy_qk), (2, a_copy_x), (5, lambda u, b, j: exp(a, 0, u, j, A_DIM ** -0.5)),
                        (6, lambda u, b, j: copy_prob(a, 0, u, j)), (8, a_copy_o)], UNITS, UNROLL, 4)

            for g in range(4):
                act.wait_ge(m["turned"], upto(0, g + 1))
                act.activation(m_xT[:, 4 * g:4 * g + 4].rearrange("p a n -> p (a n)"), bank[:, 1 + g % 2, :], ACT.Copy)\
                   .then_inc(m["xT_done"], 1)
            act.wait_ge(m["xT_done"], upto(0, 4))

            def m_copy_x(u, b, j):
                act.wait_ge(m["high_done"], upto(0, b - 1))
                act.activation(m_x[:, j], one(m_xT, b), ACT.Copy).then_inc(m["x_copied"], 1)

            def m_scale(u, b, j):
                act.wait_ge(m["g_copied"], upto(0, b + 1))
                act.wait_ge(m["low_done"], upto(0, b + 1))
                act.wait_ge(m["summed"], upto(0, b - 1))
                for e in range(EXPERTS // 2):
                    y = bank[:, 4 * j + e // 4, e % 4 * D:(e % 4 + 1) * D]
                    if e == 0:
                        ins = act.activation(m_mix[:, j, e], y, ACT.Identity, bias=m_g[:, j, EXPERTS:],
                                             scale=m_g[:, j, e:e + 1])
                    else:
                        ins = act.activation(m_mix[:, j, e], y, ACT.Copy, scale=m_g[:, j, e:e + 1])
                ins.then_inc(m["scaled"], 1)

            def m_exp(u, b, j):
                if isinstance(b, int) and b == 0:
                    act.wait_ge(m["shifted"], upto(0, 1))
                    act.activation(m_e[:].rearrange("p b e -> p (b e)"), m_lg[:].rearrange("p b e -> p (b e)"), ACT.Exp)\
                       .then_inc(m["exp_done"], 1)

            drive(act, [(0, m_copy_x), (0, m_exp), (1, m_scale)], B, 2, 1)

            act.wait_ge(ld_c, 16 * 10)

            def c_copy_x(u, b, j):
                if j % 4 == 0:
                    k = j // 4
                    act.wait_ge(c["x_turned"], upto(0, b + 1))
                    act.wait_ge(c["qk_proj"], upto(0, u - 4))
                    act.wait_ge(c["v_proj"], upto(0, b * 2 - 2))
                    for tile in range(2):
                        ins = act.activation(c_kvT[:, k, tile], bank[:, 2, tile * 128:(tile + 1) * 128], ACT.Identity,
                                             bias=c_g[:, 2 * tile + 1:2 * tile + 2],
                                             scale=c_g[:, 2 * tile:2 * tile + 1])
                    ins.then_inc(c["kvT_done"], 1)

            def c_copy_v(u, b, j):
                tile = j % 4
                if tile < 2:
                    act.wait_ge(c["v_proj"], upto(0, b * 2 + tile + 1))
                    act.wait_ge(c["pv_done"], upto(0, u - tile - 4))
                    act.activation(c_v[:, j // 4, tile, :, 0:C_DIM],
                                   bank[:, 1, :].rearrange("p (h n) -> p h n", n=C_DIM), ACT.Copy)\
                       .then_inc(c["v_done"], 1)

            def c_copy_qk(u, b, j):
                act.wait_ge(c["qk_proj"], upto(0, u + 1))
                act.wait_ge(c["rot_done"], upto(0, u + 1))
                act.wait_ge(c["s_done"], upto(0, u - 1))
                act.activation(c_q[:, j % 2], bank[:, 0, 0:128], ACT.Copy, scale=C_DIM ** -0.5)
                act.activation(c_k[:, j % 2, 128:256], bank[:, 0, 256:384], ACT.Copy).then_inc(c["evac_done"], 1)

            def c_copy_o(u, b, j):
                act.wait_ge(c["o_turned"], upto(0, u + 1))
                act.wait_ge(c["out_done"], upto(0, b))
                act.activation(c_oT[:, j // 4, j % 4], bank[:, 7, 0:128], ACT.Copy).then_inc(c["oT_done"], 1)

            second = Pipeline(act, [(3, c_copy_x), (4, c_copy_qk), (4, c_copy_v),
                                    (6, lambda u, b, j: copy_prob(c, 0, u, j)), (7, c_copy_o),
                                    (5, lambda u, b, j: exp(c, 0, u, j, 1.0))], UNITS, UNROLL, 4)
            second.start(*range(UNROLL))
            second.steady()

            def attention(ly):
                ub, bb = ly * UNITS, ly * B

                def l_copy_x(u, b, j):
                    if j % 4 == 0:
                        k = j // 4
                        act.wait_ge(l["x_turned"], upto(bb, b + 1))
                        act.wait_ge(l["x_split"], upto(bb, b - 1))
                        act.activation(xsT[0:HALF, k], bank[0:HALF, 7, 384:512], ACT.Copy).then_inc(l["xs_done"], 1)
                        act.activation(xsT[HALF:, k, 1:], bank[HALF:, 7, 384:511], ACT.Copy).then_inc(l["xs_done"], 1)

                        act.wait_ge(l["xs_done"], upto(bb * 2, b * 2 + 2))
                        act.wait_ge(l["v_proj"], upto(ub, u - 4))
                        act.activation(xs_part[:, 0, k], xsT[:, k], ACT.Copy).then_inc(l["x_high_done"], 1)

                def l_copy_v(u, b, j):
                    act.wait_ge(l["v_proj"], upto(ub, u + 1))
                    act.wait_ge(l["pv_done"], upto(ub, u - 7))
                    act.activation(l_v[:, j, :, 0:L_DIM],
                                   bank[:, 1, 0:256].rearrange("p (h n) -> p h n", n=L_DIM), ACT.Copy)\
                       .then_inc(l["v_done"], 1)

                def l_square(u, b, j):
                    act.wait_ge(l["qk_proj"], upto(ub, u + 1))
                    act.wait_ge(l["ss_done"], upto(ub, u))
                    act.activation(l_sq[:], bank[:, 0, :], ACT.Square).then_inc(l["sq_done"], 1)

                def l_copy_qk(u, b, j):
                    act.wait_ge(l["qk_turned"], upto(ub, u + 1))
                    act.wait_ge(l["s_done"], upto(ub, u - 1))
                    act.activation(l_qkT[:, j % 2], bank[:, 2, :], ACT.Copy).then_inc(l["qkT_done"], 1)

                def l_copy_o(u, b, j):
                    g = j % 4
                    act.wait_ge(l["o_turned"], upto(ub, u + 1))
                    act.wait_ge(l["out_done"], upto(bb, b))
                    act.activation(l_oT[:, j // 4, 2 * g:2 * g + 2].rearrange("p a n -> p (a n)"),
                                   bank[:, 7, 0:256], ACT.Copy).then_inc(l["oT_done"], 1)

                return Pipeline(act, [(6, lambda u, b, j: copy_prob(l, ub, u, j)), (1, l_copy_x),
                                      (5, lambda u, b, j: exp(l, ub, u, j, QK_SCALE)), (7, l_copy_o), (3, l_copy_qk),
                                      (1, l_square), (1, l_copy_v)], UNITS, UNROLL, 4)

            def feed_forward(ly):
                fb = ly * 4

                def f_copy_n(g):
                    act.wait_ge(f["turned"], upto(0, fb + g + 1))
                    act.wait_ge(f["hidden"], upto(ly * 12, 3 * (g - 1)))
                    act.activation(f_nT[:, g % 2], bank[:, 2, :], ACT.Identity, bias=f_g[:, 1:2],
                                   scale=f_g[:, 0:1]).then_inc(f["nT_done"], 1)

                def f_gelu(g, k):
                    n = CHUNKS[k][1]
                    i = len(CHUNKS) * g + k
                    act.wait_ge(f["hidden"], upto(0, ly * 12 + i + 1))
                    act.wait_ge(f["h_done"], upto(ly * 12, i - 1))
                    act.activation(f_ge[0:n, i % 2], bank[0:n, 3 + i % 2 * 2, :], ACT.Gelu,
                                   bias=f_b1[0:n, 1, k:k + 1]).then_inc(f["gelu_done"], 1)

                return f_copy_n, f_gelu

            def rest_of_layer(ly, att, nxt):
                copy_n, gelu = feed_forward(ly)
                att.steady()
                att.finish(0, 1, 2, 3)
                act.wait_ge(ld_fw, (ly + 1) * (16 * FW_DMAS))
                copy_n(0)
                att.finish(4, 5)
                gelu(0, 0)
                att.finish(6)
                for g in range(4):
                    if g == 3 and nxt is not None:
                        nxt.start(1)
                    if g > 0:
                        gelu(g, 0)
                    gelu(g, 1)
                    if g == 3 and nxt is not None:
                        nxt.start(2)
                    if g < 3:
                        copy_n(g + 1)
                    gelu(g, 2)
                    if g < 3 and nxt is not None:
                        act.wait_ge(ld_raw, (ly + 2) * 16)
                        act.wait_ge(l["v_proj"], upto(0, (ly + 1) * UNITS))
                        for piece in PIECES[g]:
                            high_weights(ly + 1, piece)
                    if g == 2 and nxt is not None:
                        nxt.start(0)
                if nxt is not None:
                    nxt.start(3, 4, 5, 6, 7)

            def high_weights(ly, piece):
                at = slice(512 * piece, 512 * piece + 512)
                act.activation(w_high[:, at], l_raw[:, at], ACT.Copy).then_inc(l["w_high_done"], 1)

            first = attention(0)
            second.finish(0)
            act.wait_ge(ld_raw, 16)
            for k in range(3):
                high_weights(0, 2 * k)
                high_weights(0, 2 * k + 1)
                second.finish(k + 1)
            first.start(0, 1)
            second.finish(4)
            first.start(2)
            second.finish(5, 6)
            first.start(*range(3, UNROLL))
            with act.Fori(0, LAYERS - 1) as ly:
                rest_of_layer(ly, attention(ly), attention(ly + 1))
            rest_of_layer(LAYERS - 1, attention(LAYERS - 1), None)

        @block.vector
        def _(dve):
            def normalise(dst, src, k, done):
                dve.tensor_scalar(dst, src, ln_mv[:, k, 0:1], ln_rs[:, k:k + 1], ALU.subtract, ALU.mult)\
                   .then_inc(done, 1)

            def find_peaks(s, base, u, j, scores, blocks):
                dve.wait_ge(s["s_done"], upto(base, u + 1))
                dve.tensor_reduce(peak[:, j % 2, 0:blocks], scores, AX.X, ALU.max).then_inc(s["peaked"], 1)

            def subtract_peaks(s, base, u, j, scores):
                k, (_, p, q, w) = j % 2, scores.shape
                dve.wait_ge(s["exp_done"], upto(base, u - 1))
                dve.wait_ge(s["peaked"], upto(base, u + 1))
                peaks = peak[:, k, 0:p * q].rearrange("p (a b) -> p a b", a=p)[:, :, :, None]
                dve.tensor_tensor(sm[:, k].rearrange("p (a b n) -> p a b n", a=p, b=q), scores,
                                  peaks.broadcast_to([128, p, q, w]), ALU.subtract).then_inc(s["sub_done"], 1)

            def shift_scores(s, base, u, j, scores, blocks):
                find_peaks(s, base, u, j, scores, blocks)
                subtract_peaks(s, base, u, j, scores)

            def invert_sums(s, base, u, j, heads, width):
                ov = bank[:, 6, 0:heads * (width + 1)].rearrange("p (h n) -> p h n", h=heads)
                dve.wait_ge(s["pv_done"], upto(base, u + 1))
                dve.reciprocal(rsum[:, j % 2, 0:heads], ov[:, :, width]).then_inc(s["rsum_done"], 1)

            def divide(s, base, u, j, heads, width, dst):
                ov = bank[:, 6, 0:heads * (width + 1)].rearrange("p (h n) -> p h n", h=heads)
                dve.wait_ge(s["rsum_done"], upto(base, u + 1))
                dve.tensor_tensor(dst, ov[:, :, 0:width], rsum[:, j % 2, 0:heads, None]
                                  .broadcast_to([128, heads, width]), ALU.mult).then_inc(s["o_done"], 1)

            dve.wait_ge(ld_x, 16)
            dve.wait_ge(ld_ctx, 16)
            dve.wait_ge(ld_a, 16 * 8)
            dve.wait_ge(preset, 1)

            def a_stats(u, b, j):
                if j % 4 == 0:
                    dve.wait_ge(a["x_turned"], upto(0, b - 1))
                    dve.tensor_scalar(nx[:, j // 4], one(CTX, b), 1.0, None, ALU.mult)
                    dve.bn_stats(ln_st[:, 0], one(X, b)).then_inc(a["stats"], 1)
                    dve.wait_ge(a["stats"], upto(0, b + 1))
                    apart(dve)
                    dve.bn_aggr(ln_mv[:, 0], ln_st[:, 0]).then_inc(a["ln_stat"], 1)

            def a_norm(u, b, j):
                if j % 4 == 0:
                    dve.wait_ge(a["ln_rstd"], upto(0, b + 1))
                    normalise(n1[:, j // 4], one(X, b), 0, a["n_done"])

            def a_values(u, b, j):
                if j % 4 == 0:
                    dve.wait_ge(a["proj"], upto(0, b + 1))
                    dve.wait_ge(a["pv_done"], upto(0, u - 4))
                    dve.tensor_tensor(a_v[:, j // 4, :, 0:A_DIM],
                                      bank[:, 1, 0:128].rearrange("p (h n) -> p h n", n=A_DIM),
                                      a_bv[:].rearrange("p (h n) -> p h n", n=A_DIM), ALU.add).then_inc(a["v_done"], 1)

            def a_peaks(u, b, j):
                find_peaks(a, 0, u, j, bank[:, 3 + j % 2, :].rearrange("p (a b n) -> p a b n", a=1, b=4), 4)

            def a_invert(u, b, j):
                invert_sums(a, 0, u, j, 4, A_DIM)

            def a_shift(u, b, j):
                subtract_peaks(a, 0, u, j, bank[:, 3 + j % 2, :].rearrange("p (a b n) -> p a b n", a=1, b=4))

            def a_divide(u, b, j):
                g = j % 4
                if g == 0:
                    dve.wait_ge(a["o_turned"], upto(0, b - 1))
                divide(a, 0, u, j, 4, A_DIM,
                       a_o[:, j // 4, 32 * g:32 * g + 32].rearrange("p (h n) -> p h n", n=A_DIM))

            def a_residual(u, b, j):
                if j % 4 == 3:
                    k = j // 4
                    dve.wait_ge(a["out_done"], upto(0, b + 1))
                    dve.tensor_tensor(a_y[:, k], bank[:, 7, 128:256], a_bo[:], ALU.add).then_inc(a["biased"], 1)
                    dve.wait_ge(a["biased"], upto(0, b + 1))
                    dve.tensor_tensor(one(X, b), one(X, b), a_y[:, k], ALU.add).then_inc(a["res_done"], 1)

            opening = Pipeline(dve, [(0, a_stats), (1, a_norm), (4, a_peaks), (7, a_invert), (4, a_shift), (7, a_divide),
                                     (3, a_values), (8, a_residual)], UNITS, UNROLL, 4)
            opening.start(*range(UNROLL))
            opening.steady()

            dve.wait_ge(ld_m, 48)

            def m_stats(g):
                dve.wait_ge(a["res_done"], upto(0, 4 * g + 4))
                for b in range(4 * g, 4 * g + 4):
                    ins = dve.bn_stats(m_st[:, b], X[:, b])
                ins.then_inc(m["stats"], 1)
                dve.wait_ge(m["stats"], upto(0, g + 1))
                for b in range(4 * g, 4 * g + 4):
                    ins = dve.bn_aggr(m_mv[:, b], m_st[:, b])
                ins.then_inc(m["ln_stat"], 1)

            def m_norm(g):
                dve.wait_ge(m["ln_rstd"], upto(0, g + 1))
                dve.wait_ge(m["turned"], upto(0, g - 1))
                for b in range(4 * g, 4 * g + 4):
                    ins = dve.tensor_scalar(m_n[:, g % 2, b % 4], X[:, b], m_mv[:, b, 0:1], m_rs[:, b:b + 1],
                                            ALU.subtract, ALU.mult)
                ins.then_inc(m["n_done"], 1)

            opening.finish(0, 1)
            m_stats(0)
            opening.finish(2, 3)
            m_stats(1)
            opening.finish(4)
            m_norm(0)
            opening.finish(5)
            m_stats(2)
            opening.finish(6)
            m_norm(1)
            opening.finish(7)
            m_stats(3)
            m_norm(2)
            m_norm(3)

            linked = [0]

            def link(ins):
                ins.then_inc(m["g_chain"], 1)
                linked[0] = linked[0] + 1
                dve.wait_ge(m["g_chain"], upto(0, linked[0]))

            def each(row):
                return m_row[:, row, :, None].broadcast_to([128, B, EXPERTS])

            peaks, total, inverse, gate_sum, floor = range(5)
            p = m_p[:, :, 0:EXPERTS]
            gates = m_gate[:, :, 0:EXPERTS]
            dve.wait_ge(m["logits"], upto(0, 4))
            link(dve.tensor_tensor(m_lg[:], bank[:, 0, 0:B * EXPERTS].rearrange("p (b e) -> p b e", e=EXPERTS),
                                   rb[:, None, :].broadcast_to([128, B, EXPERTS]), ALU.add))
            link(dve.tensor_reduce(m_row[:, peaks], m_lg[:], AX.X, ALU.max))
            dve.tensor_tensor(m_lg[:], m_lg[:], each(peaks), ALU.subtract).then_inc(m["shifted"], 1)
            dve.wait_ge(m["exp_done"], upto(0, 1))
            link(dve.tensor_reduce(m_row[:, total], m_e[:], AX.X, ALU.add))
            link(dve.reciprocal(m_row[:, inverse], m_row[:, total]))
            link(dve.tensor_tensor(p, m_e[:], each(inverse), ALU.mult))
            for b in range(B):
                ins = dve.max(m_top[:, b], m_p[:, b, 0:EXPERTS])
            link(ins)
            link(dve.memset(m_top[:, :, TOP_K:], -1.0))
            for b in range(B):
                ins = dve.match_replace(m_rep[:, b], m_top[:, b], m_p[:, b], 0.0)
            link(ins)
            link(dve.tensor_tensor(m_sel[:], p, m_rep[:, :, 0:EXPERTS], ALU.subtract))
            link(dve.tensor_reduce(m_row[:, total], m_sel[:], AX.X, ALU.add))
            link(dve.tensor_scalar(m_row[:, total], m_row[:, total], MOE_EPS, None, ALU.add))
            link(dve.reciprocal(m_row[:, inverse], m_row[:, total]))
            link(dve.tensor_tensor(m_sel[:], m_sel[:], each(inverse), ALU.mult))
            link(dve.tensor_reduce(m_row[:, gate_sum], m_sel[:], AX.X, ALU.add))
            dve.tensor_scalar(m_gate[:, :, EXPERTS], m_row[:, gate_sum], MOE_EPS, None, ALU.mult)
            link(dve.tensor_scalar(m_row[:, floor], m_row[:, gate_sum], MOE_EPS, None, ALU.max))
            link(dve.reciprocal(m_row[:, inverse], m_row[:, floor]))
            dve.tensor_tensor(gates, m_sel[:], each(inverse), ALU.mult).then_inc(m["gate_done"], 1)
            dve.wait_ge(m["gate_done"], upto(0, 1))

            def m_copy_gates(u, b, j):
                dve.wait_ge(m["scaled"], upto(0, b - 1))
                dve.wait_ge(m["mixed"], upto(0, b - 1))
                dve.tensor_scalar(m_g[:, j], one(m_gate, b), 1.0, None, ALU.mult).then_inc(m["g_copied"], 1)

            def m_mix_in(u, b, j):
                dve.wait_ge(m["g_copied"], upto(0, b + 1))
                dve.wait_ge(m["scaled"], upto(0, b + 1))
                dve.wait_ge(m["high_done"], upto(0, b + 1))
                half = EXPERTS // 2
                for e in range(half):
                    ins = dve.scalar_tensor_tensor(m_mix[:, j, e], bank[:, 4 * j + 2 + e // 4, e % 4 * D:(e % 4 + 1) * D],
                                                   m_g[:, j, half + e:half + e + 1], m_mix[:, j, e], ALU.mult, ALU.add)
                ins.then_inc(m["mixed"], 1)

            def m_residual(u, b, j):
                dve.wait_ge(m["summed"], upto(0, b + 1))
                dve.tensor_tensor(one(X, b), one(X, b), m_acc[:, j], ALU.add).then_inc(m["res_done"], 1)

            drive(dve, [(0, m_copy_gates), (1, m_mix_in), (2, m_residual)], B, 2, 1)

            dve.wait_ge(m["res_done"], upto(0, B))
            dve.wait_ge(ld_const, 16)

            def c_stats(u, b, j):
                if j % 4 == 0:
                    dve.bn_stats(ln_st[:, 0], one(X, b))
                    dve.bn_stats(ln_st[:, 1], one(CTX, b)).then_inc(c["stats"], 1)
                    dve.wait_ge(c["stats"], upto(0, b + 1))
                    apart(dve)
                    dve.bn_aggr(ln_mv[:, 0], ln_st[:, 0])
                    dve.bn_aggr(ln_mv[:, 1], ln_st[:, 1]).then_inc(c["ln_stat"], 1)

            def c_norm(u, b, j):
                if j % 4 == 0:
                    k = j // 4
                    dve.wait_ge(c["x_turned"], upto(0, b - 1))
                    dve.wait_ge(c["ln_rstd"], upto(0, b + 1))
                    dve.tensor_scalar(nx[:, k], one(CTX, b), ln_mv[:, 1, 0:1], ln_rs[:, 1:2], ALU.subtract,
                                      ALU.mult)
                    normalise(n1[:, k], one(X, b), 0, c["n1_done"])
                    dve.wait_ge(c["n1_done"], upto(0, b + 1))
                    dve.bn_stats(ln_st[:, 2], n1[:, k]).then_inc(c["stats2"], 1)
                    dve.wait_ge(c["stats2"], upto(0, b + 1))
                    apart(dve)
                    dve.bn_aggr(ln_mv[:, 2], ln_st[:, 2]).then_inc(c["ln_stat2"], 1)

            def c_norm2(u, b, j):
                if j % 4 == 0:
                    dve.wait_ge(c["ln_rstd2"], upto(0, b + 1))
                    normalise(n2[:, j // 4], n1[:, j // 4], 2, c["n_done"])

            def c_rotate(u, b, j):
                k = j % 2
                dve.wait_ge(c["qk_proj"], upto(0, u + 1))
                dve.tensor_tensor(c_r[:, k, 0], bank[:, 0, 128:256], cos_t, ALU.mult)
                dve.tensor_tensor(c_r[:, k, 1], bank[:, 0, 384:512], sin_t, ALU.mult).then_inc(c["rot_done"], 1)
                dve.wait_ge(c["rot_done"], upto(0, u + 1))
                dve.wait_ge(c["s_done"], upto(0, u - 1))
                dve.tensor_tensor(c_k[:, k, 0:128], c_r[:, k, 0], c_r[:, k, 1], ALU.add).then_inc(c["rope_done"], 1)

            def c_shift(u, b, j):
                shift_scores(c, 0, u, j, bank[:, 3:5, 0:256].rearrange("p a (b n) -> p a b n", b=1), 2)

            def c_divide(u, b, j):
                dve.wait_ge(c["o_turned"], upto(0, u - 1))
                invert_sums(c, 0, u, j, 2, C_DIM)
                divide(c, 0, u, j, 2, C_DIM, o[:, j % 2, 0:128].rearrange("p (h n) -> p h n", n=C_DIM))

            def c_residual(u, b, j):
                if j % 4 == 3:
                    k = j // 4
                    dve.wait_ge(c["out_done"], upto(0, b + 1))
                    dve.tensor_tensor(one(X, b), one(X, b), bank[:, 7, 128:256], ALU.add).then_inc(c["res_done"], 1)
                    dve.wait_ge(c["res_done"], upto(0, b + 1))
                    dve.tensor_scalar(c_x[:, k], one(X, b), 1.0, None, ALU.mult).then_inc(c["y_copied"], 1)
                    dve.wait_ge(c["y_copied"], upto(0, b + 1))
                    dve.bn_stats(ln_st[:, 3], c_x[:, k]).then_inc(c["y_stats"], 1)
                    dve.wait_ge(c["y_stats"], upto(0, b + 1))
                    apart(dve)
                    dve.bn_aggr(ln_mv[:, 3], ln_st[:, 3]).then_inc(c["y_stat"], 1)

            def y_norm(u, b, j):
                if j % 4 == 3:
                    dve.wait_ge(c["y_rstd"], upto(0, b + 1))
                    normalise(one(Y, b), c_x[:, j // 4], 3, c["y_done"])

            second = Pipeline(dve, [(2, c_norm2), (0, c_stats), (1, c_norm), (5, c_shift), (3, c_rotate),
                                    (6, c_divide), (7, c_residual), (8, y_norm)], UNITS, UNROLL, 4)
            second.start(*range(UNROLL))
            second.steady()

            def attention(ly):
                ub, bb = ly * UNITS, ly * B

                def table(k):
                    return l_tab[:, bass.ds(ly, 1), k].rearrange("p a q n -> p (a q) n")

                def l_copy_in(u, b, j):
                    if j % 4 == 0:
                        dve.wait_ge(l["x_turned"], upto(bb, b - 1))
                        dve.tensor_scalar(xin[:, j // 4], one(Y, b), 1.0, None, ALU.mult).then_inc(l["xin_done"], 1)

                def l_split_x(u, b, j):
                    if j % 4 == 0:
                        k = j // 4
                        dve.wait_ge(l["x_high_done"], upto(bb, b + 1))
                        dve.tensor_tensor(xs_part[:, 1, k], xsT[:, k], xs_part[:, 0, k].bitcast(F32), ALU.subtract)\
                           .then_inc(l["x_split"], 1)

                def l_rotate(u, b, j):
                    k = j % 2
                    dve.wait_ge(l["add_done"], upto(ub, u - 1))
                    dve.wait_ge(l["sq_done"], upto(ub, u + 1))
                    shape = [128, 2, 4, L_DIM]
                    dve.tensor_tensor(l_rot[:, k, 0].rearrange("p (q h n) -> p q h n", q=2, h=4),
                                      bank[:, 0, :].rearrange("p (q h n) -> p q h n", q=2, h=4),
                                      table(0)[:, :, None, :].broadcast_to(shape), ALU.mult)
                    shape = [128, 2, 4, 2, L_DIM // 2]
                    dve.tensor_tensor(
                        l_rot[:, k, 1].rearrange("p (q h s n) -> p q h s n", q=2, h=4, s=2),
                        bank[:, 0, :].rearrange("p (q h s n) -> p q h s n", q=2, h=4, s=2)[:, :, :, ::-1, :],
                        table(1).rearrange("p q (s n) -> p q s n", s=2)[:, :, None].broadcast_to(shape),
                        ALU.mult).then_inc(l["rot_done"], 1)

                def l_sum_squares(u, b, j):
                    k = j % 2
                    dve.wait_ge(l["sq_done"], upto(ub, u + 1))
                    dve.wait_ge(l["rn_done"], upto(ub, u - 1))
                    dve.tensor_reduce(l_ss[:, k], l_sq[:].rearrange("p (h n) -> p h n", n=L_DIM), AX.X, ALU.add)\
                       .then_inc(l["ss_done"], 1)

                def l_peaks(u, b, j):
                    find_peaks(l, ub, u, j, bank[:, 3:5, 0:256].rearrange("p a (b n) -> p a b n", b=2), 4)

                def l_floor(u, b, j):
                    dve.wait_ge(l["ss_done"], upto(ub, u + 1))
                    apart(dve)
                    dve.tensor_scalar(l_ss[:, j % 2], l_ss[:, j % 2], 1e-24, None, ALU.max).then_inc(l["floored"], 1)

                def l_shift(u, b, j):
                    subtract_peaks(l, ub, u, j, bank[:, 3:5, 0:256].rearrange("p a (b n) -> p a b n", b=2))

                def l_divide(u, b, j):
                    dve.wait_ge(l["o_turned"], upto(ub, u - 1))
                    invert_sums(l, ub, u, j, 4, L_DIM)
                    divide(l, ub, u, j, 4, L_DIM, o[:, j % 2].rearrange("p (h n) -> p h n", n=L_DIM))

                def l_residual(u, b, j):
                    if j % 4 == 3:
                        dve.wait_ge(l["out_done"], upto(bb, b + 1))
                        dve.tensor_tensor(one(Y, b), one(Y, b), bank[:, 7, 256:384], ALU.add).then_inc(l["res_done"], 1)

                return Pipeline(dve, [(0, l_copy_in), (1, l_split_x), (4, l_peaks), (2, l_floor), (4, l_shift), (6, l_divide),
                                      (7, l_residual), (1, l_rotate), (1, l_sum_squares)], UNITS, UNROLL, 4)

            def feed_forward(ly):
                fb = ly * 4

                def f_stats(g):
                    dve.wait_ge(f["xs"], upto(0, fb + g + 1))
                    v = bank[:, 1, :].rearrange("p (a n) -> p a n", a=4)
                    apart(dve)
                    for q in range(4):
                        ins = dve.bn_stats(f_st[:, q], v[:, q])
                    ins.then_inc(f["stats"], 1)
                    dve.wait_ge(f["stats"], upto(0, fb + g + 1))
                    apart(dve)
                    for q in range(4):
                        ins = dve.bn_aggr(f_mv[:, q], f_st[:, q])
                    ins.then_inc(f["stat"], 1)

                def f_norm(g):
                    v = bank[:, 1, :].rearrange("p (a n) -> p a n", a=4)
                    dve.wait_ge(f["rstd"], upto(0, fb + g + 1))
                    dve.wait_ge(f["turned"], upto(0, fb + g))
                    for q in range(4):
                        ins = dve.tensor_scalar(f_n[:, q], v[:, q], f_mv[:, q, 0:1], f_rs[:, q:q + 1],
                                                ALU.subtract, ALU.mult)
                    ins.then_inc(f["n_done"], 1)

                def f_gated(g, k):
                    n = CHUNKS[k][1]
                    i = len(CHUNKS) * g + k
                    dve.wait_ge(f["gelu_done"], upto(0, ly * 12 + i + 1))
                    dve.wait_ge(f["out_mm"], upto(fb, g - 1))
                    dve.scalar_tensor_tensor(f_h[0:n, g % 2, k], bank[0:n, 4 + i % 2 * 2, :], f_b1[0:n, 0, k:k + 1],
                                             f_ge[0:n, i % 2], ALU.add, ALU.mult).then_inc(f["h_done"], 1)

                def f_residual(g):
                    yg = Y[:, 4 * g:4 * g + 4, :].rearrange("p a n -> p (a n)")
                    dve.wait_ge(f["out_mm"], upto(0, fb + g + 1))
                    dve.wait_ge(f["yb_done"], upto(0, fb + g + 1))
                    dve.tensor_tensor(yg, yg, bank[:, 7, :], ALU.add).then_inc(f["y_done"], 1)

                return f_stats, f_norm, f_gated, f_residual

            def rest_of_layer(ly, att, nxt):
                stats, norm, gated, residual = feed_forward(ly)
                att.steady()
                att.finish(0, 1)
                stats(0)
                att.finish(2)
                norm(0)
                att.finish(3, 4, 5)
                dve.wait_ge(ld_fw, (ly + 1) * (16 * FW_DMAS))
                gated(0, 0)
                stats(1)
                att.finish(6)
                for g in range(4):
                    if 0 < g < 3:
                        stats(g + 1)
                    if g == 3 and nxt is not None:
                        nxt.start(1)
                    if g > 0:
                        gated(g, 0)
                    if g < 3:
                        norm(g + 1)
                    if g > 0:
                        residual(g - 1)
                        if nxt is None:
                            add_up(g - 1)
                    if g == 2 and nxt is not None:
                        dve.wait_ge(f["y_done"], upto(0, ly * 4 + 1))
                        nxt.start(0)
                    if g == 3 and nxt is not None:
                        nxt.start(2)
                    gated(g, 1)
                    gated(g, 2)
                    if g < 3 and nxt is not None:
                        for piece in PIECES[g]:
                            low_weights(ly + 1, piece)
                if nxt is not None:
                    nxt.start(3)
                residual(3)
                if nxt is None:
                    add_up(3)
                else:
                    dve.wait_ge(f["y_done"], upto(0, ly * 4 + 4))
                    nxt.start(4, 5, 6, 7)

            def add_up(g):
                s = slice(4 * g, 4 * g + 4)
                dve.wait_ge(f["y_done"], upto(0, (LAYERS - 1) * 4 + g + 1))
                dve.tensor_tensor(X[:, s, :], X[:, s, :], Y[:, s, :], ALU.add).then_inc(summed, 1)

            def low_weights(ly, piece):
                at = slice(512 * piece, 512 * piece + 512)
                dve.wait_ge(l["w_high_done"], upto(0, ly * W_CHUNKS + piece + 1))
                dve.tensor_tensor(w_low[:, at], l_raw[:, at], w_high[:, at].bitcast(F32), ALU.subtract)\
                   .then_inc(l["w_split"], 1)

            first = attention(0)
            second.finish(0)
            for k in range(3):
                low_weights(0, 2 * k)
                low_weights(0, 2 * k + 1)
                second.finish(k + 1)
            dve.wait_ge(c["y_done"], upto(0, 1))
            dve.wait_ge(tables, 1)
            first.start(0, 1)
            second.finish(4)
            first.start(2)
            second.finish(5, 6, 7)
            dve.wait_ge(c["y_done"], upto(0, B))
            first.start(*range(3, UNROLL))
            with dve.Fori(0, LAYERS - 1) as ly:
                rest_of_layer(ly, attention(ly), attention(ly + 1))
            rest_of_layer(LAYERS - 1, attention(LAYERS - 1), None)


_INS = ["x", "ctx_1024", "L0_xattn_w_q", "L0_xattn_b_q", "L0_xattn_w_k", "L0_xattn_b_k", "L0_xattn_w_v",
        "L0_xattn_b_v", "L0_xattn_w_out", "L0_xattn_b_out", "L0_ffn_router_w", "L0_ffn_router_b",
        "L0_ffn_expert_w", "L1_xattn_gamma_x", "L1_xattn_beta_x", "L1_xattn_gamma_l", "L1_xattn_beta_l",
        "L1_xattn_Wq", "L1_xattn_Wkv", "L1_xattn_Wo", "L1_ffn_Wqkv", "L1_ffn_q_scale", "L1_ffn_k_scale",
        "L1_ffn_Wo", "L1_ffn_ln_g", "L1_ffn_ln_b", "L1_ffn_W1", "L1_ffn_b1", "L1_ffn_W2", "L1_ffn_b2"]


def constants():
    import numpy as np
    from concourse import mybir as _mybir

    f = np.float32
    const = np.zeros((128, K_ALL), f)
    const[:, K_IDENT:K_IDENT + 128] = np.eye(128)
    const[:, K_SHIFT:K_SHIFT + 128] = np.eye(128, k=1)

    half = np.arange(0, L_DIM, 2, dtype=f)
    inv = f(1.0) / f(10000.0) ** (half / f(L_DIM))
    t = np.arange(S, dtype=f)
    freqs = t[:, None] * inv[None, :]
    freqs = np.concatenate([freqs, freqs], -1)
    base = (half + f(0.4 * L_DIM)) / f(1.4 * L_DIM)
    scale = base[None, :] ** ((t - S // 2) / f(WINDOW // 2))[:, None]
    scale = np.concatenate([scale, scale], -1)
    sign = np.where(np.arange(L_DIM) < L_DIM // 2, f(-1.0), f(1.0))[None, :]
    for q, s in enumerate((scale, f(1.0) / scale)):
        const[:, K_COS + q * L_DIM:K_COS + (q + 1) * L_DIM] = np.cos(freqs) * s
        const[:, K_SIN + q * L_DIM:K_SIN + (q + 1) * L_DIM] = np.sin(freqs) * s * sign
    const[:, K_COST:K_COST + 128] = np.tile(np.cos(freqs).T, (2, 1))
    const[:, K_SINT:K_SINT + 128] = np.tile((np.sin(freqs) * sign).T, (2, 1))
    const[np.arange(128), K_HEAD + np.arange(128) // A_DIM] = 1.0

    i, j = np.arange(128)[:, None], np.arange(128)[None, :]
    mask = np.where((i < j) | (i > j + WINDOW), f(MASKED), f(0.0))
    bf = np.concatenate([np.eye(128, dtype=f), mask, mask], 1).astype(_mybir.dt.np(_mybir.dt.bfloat16))
    return {"const": const, "const_bf": bf}


def kernel(**inputs):
    import numpy as _np
    import concourse.bacc as _bacc
    from concourse import mybir as _mybir
    from concourse.bass_utils import run_bass_kernel_spmd as _run

    nc = _bacc.Bacc("TRN2", target_bir_lowering=False, num_devices=1)
    given = {n: _np.ascontiguousarray(inputs[n]) for n in _INS} | constants()
    arrays, args = {}, {}
    for name, a in given.items():
        arrays[f"in_{name}_dram"] = a
        args[name] = nc.dram_tensor(f"in_{name}_dram", a.shape, _mybir.dt.from_np(a.dtype),
                                    kind="ExternalInput").ap()
    out = nc.dram_tensor("out_0_dram", (B, S, D), F32, kind="ExternalOutput").ap()
    build(nc, args, out)
    r = _run(nc, [arrays], core_ids=[0])
    return r.results[0]["out_0_dram"]
```
